# Optimizing a Trainium2 kernel written in Bass

```python
import numpy as np
import jax
import jax.numpy as jnp

def _softmax(x, axis=-1):
    return jax.nn.softmax(x, axis=axis)

def _gelu(x):
    return jax.nn.gelu(x, approximate=True)

def _silu(x):
    return jax.nn.silu(x)

def _sigmoid(x):
    return jax.nn.sigmoid(x)

def _layernorm(x, axis=-1, eps=1e-05):
    m = jnp.mean(x, axis=axis, keepdims=True)
    v = jnp.var(x, axis=axis, keepdims=True)
    return (x - m) / jnp.sqrt(v + eps)

def _scatter_add(tgt, idx, src, axis=0):
    return tgt.at[idx].add(src)

def _segment_sum(src, seg, n):
    return jax.ops.segment_sum(src, seg, n)
kernel_name = 'mk_gnn_preln_d2_gnn_r32_f23904'

def setup_inputs(seed: int=0):
    np.random.seed(seed)
    _w = jnp.asarray

    def _rec_inputs():
        import jax
        import jax.numpy as jnp
        _gk = jax.random.key(seed)
        x = -0.000202 + 1 * jax.random.normal(jax.random.fold_in(_gk, 1), (50000, 128), jnp.float32)
        src = jax.random.randint(jax.random.fold_in(_gk, 2), (50000,), 0, 50000, jnp.int32)
        dst = jax.random.randint(jax.random.fold_in(_gk, 3), (50000,), 0, 50000, jnp.int32)
        _o = jnp.argsort(dst, stable=True)
        src = src[_o]
        dst = dst[_o]
        return (x, src, dst)
    x, src, dst = _rec_inputs()

    def _L0_gnn_setup():
        import jax, jax.numpy as jnp
        import numpy as np
        N = 50000
        E = 18750
        IN = 128
        H = 4
        C = 32
        B = 3
        NEG_SLOPE = 0.2
        key = jax.random.key(seed)
        ks = jax.random.split(key, 6)
        x = jax.random.normal(ks[0], (N, IN), dtype=jnp.float32)
        edge_index = jax.random.randint(ks[1], (2, E), 0, N)
        coeffs_t = jnp.array([0.25, 0.5, 0.25], dtype=jnp.float32)
        glorot_w = float(np.sqrt(2.0) * np.sqrt(6.0 / (H * C + IN)))
        glorot_a = float(np.sqrt(2.0) * np.sqrt(6.0 / (1 + C)))
        lin_weight = jax.random.uniform(ks[2], (B, H * C, IN), jnp.float32, -glorot_w, glorot_w)
        lin_bias = jnp.zeros((B, H * C), dtype=jnp.float32)
        att_src = jax.random.uniform(ks[3], (B, 1, H, C), jnp.float32, -glorot_a, glorot_a)
        att_dst = jax.random.uniform(ks[4], (B, 1, H, C), jnp.float32, -glorot_a, glorot_a)
        return {'x': x, 'edge_index': edge_index, 'coeffs_t': coeffs_t, 'lin_weight': lin_weight, 'lin_bias': lin_bias, 'att_src': att_src, 'att_dst': att_dst}
    _L0_gnn_all = _L0_gnn_setup()
    _L0_gnn_in = {k: v for k, v in _L0_gnn_all.items() if k in ('coeffs_t', 'lin_weight', 'lin_bias', 'att_src', 'att_dst')}
    del _L0_gnn_all

    def _L1_gnn_setup():
        import jax, jax.numpy as jnp
        import numpy as np
        N_NODES = 50000
        N_EDGES = 25000
        D_IN = 128
        D_OUT = 128
        key = jax.random.key(seed)
        ks = jax.random.split(key, 6)
        x = jax.random.normal(ks[0], (N_NODES, D_IN), dtype=jnp.float32)
        edge_index = jax.random.randint(ks[1], (2, N_EDGES), 0, N_NODES, dtype=jnp.int32)
        s1 = 1.0 / np.sqrt(2 * D_IN)
        s2 = 1.0 / np.sqrt(D_IN)
        W1 = jax.random.normal(ks[2], (2 * D_IN, D_IN), dtype=jnp.float32) * s1
        b1 = jnp.zeros((D_IN,), dtype=jnp.float32)
        W2 = jax.random.normal(ks[3], (D_IN, 1), dtype=jnp.float32) * s2
        b2 = jnp.zeros((1,), dtype=jnp.float32)
        Wl = jax.random.normal(ks[4], (D_IN, D_OUT), dtype=jnp.float32) * s2
        bl = jnp.zeros((D_OUT,), dtype=jnp.float32)
        return {'x': x, 'edge_index': edge_index, 'W1': W1, 'b1': b1, 'W2': W2, 'b2': b2, 'Wl': Wl, 'bl': bl}
    _L1_gnn_all = _L1_gnn_setup()
    _L1_gnn_in = {k: v for k, v in _L1_gnn_all.items() if k in ('W1', 'b1', 'W2', 'b2', 'Wl', 'bl')}
    del _L1_gnn_all
    return {'x': x, 'src': src, 'dst': dst, 'L0_gnn_coeffs_t': _L0_gnn_in['coeffs_t'], 'L0_gnn_lin_weight': _L0_gnn_in['lin_weight'], 'L0_gnn_lin_bias': _L0_gnn_in['lin_bias'], 'L0_gnn_att_src': _L0_gnn_in['att_src'], 'L0_gnn_att_dst': _L0_gnn_in['att_dst'], 'L1_gnn_W1': _L1_gnn_in['W1'], 'L1_gnn_b1': _L1_gnn_in['b1'], 'L1_gnn_W2': _L1_gnn_in['W2'], 'L1_gnn_b2': _L1_gnn_in['b2'], 'L1_gnn_Wl': _L1_gnn_in['Wl'], 'L1_gnn_bl': _L1_gnn_in['bl']}

def reference(x, src, dst, L0_gnn_coeffs_t, L0_gnn_lin_weight, L0_gnn_lin_bias, L0_gnn_att_src, L0_gnn_att_dst, L1_gnn_W1, L1_gnn_b1, L1_gnn_W2, L1_gnn_b2, L1_gnn_Wl, L1_gnn_bl):
    import jax
    import jax.numpy as jnp

    def _L0_gnn_ref(x, edge_index, coeffs_t, lin_weight, lin_bias, att_src, att_dst):
        import jax, jax.numpy as jnp
        import numpy as np
        N = 50000
        E = 18750
        IN = 128
        H = 4
        C = 32
        B = 3
        NEG_SLOPE = 0.2
        W = jnp.einsum('b,boi->oi', coeffs_t, lin_weight)
        bias = jnp.einsum('b,bo->o', coeffs_t, lin_bias)
        a_src = jnp.einsum('b,bqhc->qhc', coeffs_t, att_src)
        a_dst = jnp.einsum('b,bqhc->qhc', coeffs_t, att_dst)
        n = x.shape[0]
        xt = (x @ W.T + bias).reshape(n, H, C)
        alpha_src = jnp.sum(xt * a_src, axis=-1)
        alpha_dst = jnp.sum(xt * a_dst, axis=-1)
        row, col = (edge_index[0], edge_index[1])
        alpha = alpha_src[row] + alpha_dst[col]
        alpha = jax.nn.leaky_relu(alpha, NEG_SLOPE)
        amax = jax.ops.segment_max(alpha, col, num_segments=n)
        ex = jnp.exp(alpha - amax[col])
        denom = jax.ops.segment_sum(ex, col, num_segments=n)
        alpha = ex / (denom[col] + 1e-16)
        msg = xt[row] * alpha[..., None]
        out = jax.ops.segment_sum(msg, col, num_segments=n)
        return out.reshape(n, H * C)

    def _L1_gnn_ref(x, edge_index, W1, b1, W2, b2, Wl, bl):
        import jax, jax.numpy as jnp
        import numpy as np
        N_NODES = 50000
        N_EDGES = 25000
        D_IN = 128
        D_OUT = 128
        row, col = (edge_index[0], edge_index[1])
        n, d = x.shape
        xc = x[row]
        xn = x[col]
        h = jax.nn.relu(xc @ W1[:d] + xn @ W1[d:] + b1)
        mask = jax.nn.sigmoid(h @ W2 + b2)[:, 0]
        seg_sum = jax.ops.segment_sum(mask, row, num_segments=n)
        w = mask / (seg_sum[row] + 1e-09)
        agg = jax.ops.segment_sum(w[:, None] * xn, row, num_segments=n)
        deg = jax.ops.segment_sum(jnp.ones_like(mask), row, num_segments=n)
        out_emb = jnp.where((deg > 0)[:, None], 0.5 * x + 0.5 * agg, x)
        return jax.nn.relu(out_emb @ Wl + bl)
    edge_index = jnp.stack([src, dst])
    h = jnp.maximum(_layernorm(x, axis=-1), 0.0)
    x = x + _L0_gnn_ref(h, edge_index, L0_gnn_coeffs_t, L0_gnn_lin_weight, L0_gnn_lin_bias, L0_gnn_att_src, L0_gnn_att_dst)
    h = jnp.maximum(_layernorm(x, axis=-1), 0.0)
    x = x + _L1_gnn_ref(h, edge_index, L1_gnn_W1, L1_gnn_b1, L1_gnn_W2, L1_gnn_b2, L1_gnn_Wl, L1_gnn_bl)
    return x

_drawn_inputs = setup_inputs


def setup_inputs(seed=0):
    import zlib

    import numpy as np

    out = dict(_drawn_inputs(seed))
    spreads = {'L0_gnn_lin_bias': (0.0, 0.1), 'L1_gnn_b1': (0.0, 2.0), 'L1_gnn_bl': (0.0, 0.1)}
    factors = {'L0_gnn_att_dst': 11.114, 'L1_gnn_W1': 8.0, 'L1_gnn_W2': 8.0}
    for name, (base, spread) in spreads.items():
        noise = np.random.default_rng([zlib.crc32(name.encode()), seed]).standard_normal(out[name].shape)
        drawn = base * np.exp(spread * noise) if base else spread * noise
        out[name] = jnp.asarray(drawn.astype(out[name].dtype))
    for name, factor in factors.items():
        out[name] = (out[name] * factor).astype(out[name].dtype)
    return out
```

```python
import concourse.bass as bass
from concourse import mybir
from contextlib import ExitStack

F32 = mybir.dt.float32
I32 = mybir.dt.int32
ALU = mybir.AluOpType
ACT = mybir.ActivationFunctionType
AX = mybir.AxisListType

P = 128
N = 50000
E = 50000
D = 128
HEADS = 4
CH = D // HEADS
SLICES = 3
EPS = 1e-5
SLOPE = 0.2
BIG = 1e38

EC = 14
T = 2 * EC * -(-E // (P * 2 * EC))
ECHUNKS = T // EC
SLOTS = EC + 1
PAD_DST = P * T - 1
SKIP = 1 << 17
LAST_FULL = (P - 1) * T
REST = E - LAST_FULL

NC = 10
NB = 3
NCHUNKS = N // (P * NC)
TAIL = N - NCHUNKS * P * NC
TURNS = NCHUNKS // NB
assert TURNS * NB == NCHUNKS and ECHUNKS % 2 == 0

XT = D + HEADS
XD = D + HEADS
PAIR = 2 * D
AGG = D + 2
RADIX = max(P, T)


def wait_past(eng, sem, value):
    if isinstance(value, int) and value <= 0:
        return
    eng.wait_ge(sem, value)


def wait_apart(eng, past, sem, value):
    wait_past(eng, sem, value)
    if not isinstance(value, int):
        eng.sem_inc(past, 1)


class Chunk:

    def __init__(self, c, buf, turn, parts=P, tiles=NC, group=3):
        self.c, self.buf, self.turn, self.parts, self.tiles = c, buf, turn, parts, tiles
        self.groups = [(j, min(group, tiles - j)) for j in range(0, tiles, group)]
        self.per = -(-NC // group)

    def rows(self, table, cols):
        if self.parts == P:
            part = table[bass.ds(self.c * (P * NC), P * NC), cols]
        else:
            part = table[NCHUNKS * P * NC:N, cols]
        return part.rearrange("(p j) f -> p j f", p=self.parts)


def node_chunks(eng, ahead, behind, group=3):
    def full(k, h):
        return Chunk(NB * k + h, h, k, group=group)

    tail = Chunk(NCHUNKS, 0, TURNS, parts=TAIL, tiles=1, group=group)
    ahead(full(0, 0))
    for h in range(NB):
        ahead(full(0, h + 1) if h + 1 < NB else full(1, 0))
        behind(full(0, h))
    with eng.Fori(1, TURNS - 1) as k:
        for h in range(NB):
            ahead(full(k, h + 1) if h + 1 < NB else Chunk(NB * k + NB, 0, k + 1, group=group))
            behind(full(k, h))
    for h in range(NB):
        ahead(full(TURNS - 1, h + 1) if h + 1 < NB else tail)
        behind(full(TURNS - 1, h))
    behind(tail)


def edge_chunks(eng, body):
    body(0, 0, 0)
    body(1, 1, 0)
    with eng.Fori(1, ECHUNKS // 2) as k:
        body(2 * k, 0, k)
        body(2 * k + 1, 1, k)


class Mem:

    def __init__(self, nc, ctx):
        self.nc, self.ctx = nc, ctx

    def sb(self, name, shape, dt=F32):
        return self.ctx.enter_context(self.nc.sbuf_tensor(name, shape, dt))

    def ps(self, name, banks=1):
        return self.ctx.enter_context(self.nc.psum_tensor(name, [P, 512 * banks], F32))

    def sem(self, name):
        return self.ctx.enter_context(self.nc.semaphore(name))

    def sems(self, name, n):
        return [self.sem(f"{name}{i}") for i in range(n)]


class Const:

    def __init__(self, m):
        self.ident = m.sb("ident", [P, P])
        self.ones = m.sb("ones", [P, P])
        self.before = m.sb("before", [P, P])
        self.upto = m.sb("upto", [P, P])
        self.proj = m.sb("proj", [P, D + 2 * HEADS])
        self.proj_bias = m.sb("proj_bias", [P, D + 2 * HEADS])
        self.w1_src = m.sb("w1_src", [P, D])
        self.w1_dst = m.sb("w1_dst", [P, D])
        self.b1 = m.sb("b1", [P, D])
        self.w2 = m.sb("w2", [P, D])
        self.b2 = m.sb("b2", [P, 1])
        self.wl = m.sb("wl", [P, D])
        self.bl = m.sb("bl", [P, D])
        self.eps = m.sb("eps", [P, 1])
        self.pool_past = m.sem("pool_past")
        self.sp_past = m.sem("sp_past")
        self.trash = m.sb("trash", [P, 1])


class Edges:

    def __init__(self, m):
        self.src = m.sb("e_src", [P, T + 2 * EC], I32)
        self.dst = m.sb("e_dst", [P, T], I32)
        self.dst_pick = m.sb("e_dst_pick", [P, T + 2 * EC], I32)
        self.put = m.sb("e_put", [P, T], I32)
        self.dst_f = m.sb("e_dst_f", [P, T])
        self.reset = m.sb("e_reset", [P, T])
        self.last = m.sb("e_last", [P, T])
        self.head_end = m.sb("e_head_end", [P, T])
        self.go_on_rev = m.sb("e_go_on_rev", [P, T])
        self.key_rev = m.sb("e_key_rev", [P, T + 2 * EC])
        self.pick_rev = m.sb("e_pick_rev", [P, T + 2 * EC], I32)



def constants(nc, m, k, coeffs, lin_weight, lin_bias, att_src, att_dst, w1, b1, w2, b2, wl, bl):
    w_all = m.sb("w_all", [P, SLICES, D])
    col_all = m.sb("col_all", [P, 3, SLICES])
    mix = m.sb("mix", [P, SLICES])
    w_mix = m.sb("w_mix", [P, D])
    cols = m.sb("cols", [P, 3])
    eye_att = m.sb("eye_att", [P, D + 2 * HEADS])
    bias_wide = m.sb("bias_wide", [P, P])
    ps_w = m.ps("ps_w")
    ps_b = m.ps("ps_b")
    loaded, filled, drawn, mixed, spread, folded, kept = (
        m.sem("const_loaded"), m.sem("const_filled"), m.sem("const_drawn"), m.sem("const_mixed"),
        m.sem("const_spread"), m.sem("const_folded"), m.sem("const_kept"))

    with nc.Block() as block:
        @block.sync
        def _(sp):
            loads = [
                (w_all[:, :, :], lin_weight.rearrange("b o i -> o b i")),
                (col_all[:, 0, :], lin_bias.rearrange("b o -> o b")),
                (col_all[:, 1, :], att_src.rearrange("b q h c -> (q h c) b")),
                (col_all[:, 2, :], att_dst.rearrange("b q h c -> (q h c) b")),
                (mix[:, :], coeffs.unsqueeze(0).to_broadcast([P, SLICES])),
                (k.w1_src[:, :], w1[0:D, :]),
                (k.w1_dst[:, :], w1[D:2 * D, :]),
                (k.b1[:, :], b1.unsqueeze(0).to_broadcast([P, D])),
                (k.w2[:, :], w2.rearrange("d one -> one d").to_broadcast([P, D])),
                (k.b2[:, :], b2.unsqueeze(0).to_broadcast([P, 1])),
                (k.wl[:, :], wl[:, :]),
                (k.bl[:, :], bl.unsqueeze(0).to_broadcast([P, D])),
            ]
            with nc.allow_non_contiguous_dma(reason="small weights, once"):
                for to, of in loads:
                    sp.dma_start(to, of).then_inc(loaded, 16)
            wait_apart(sp, k.sp_past, loaded, 16 * len(loads))
            sp.sem_inc(kept, 1)

        @block.gpsimd
        def _(pool):
            wait_apart(pool, k.pool_past, filled, 1)
            nc.gpsimd.affine_select(out=k.ident[:, :], in_=k.ones[:, :], pattern=[[-1, P]], compare_op=ALU.is_equal,
                                    fill=0.0, base=0, channel_multiplier=1).then_inc(drawn, 1)
            nc.gpsimd.affine_select(out=k.before[:, :], in_=k.ones[:, :], pattern=[[1, P]], compare_op=ALU.is_gt,
                                    fill=0.0, base=0, channel_multiplier=-1).then_inc(drawn, 1)
            nc.gpsimd.affine_select(out=k.upto[:, :], in_=k.ones[:, :], pattern=[[-1, P]], compare_op=ALU.is_ge,
                                    fill=0.0, base=0, channel_multiplier=1).then_inc(drawn, 1)
            nc.gpsimd.iota(k.trash[:, :], pattern=[[0, 1]], base=N, channel_multiplier=1,
                           allow_small_or_imprecise_dtypes=True).then_inc(drawn, 1)
            wait_apart(pool, k.pool_past, drawn, 4)

        @block.vector
        def _(v):
            v.memset(k.ones[:, :], 1.0).then_inc(filled, 1)
            v.memset(k.eps[:, :], EPS)
            v.memset(eye_att[:, :], 0.0).then_inc(spread, 1)
            v.wait_ge(kept, 1)
            v.tensor_scalar(w_mix[:, :], w_all[:, 0, :], mix[:, 0:1], None, op0=ALU.mult).then_inc(mixed, 1)
            v.tensor_scalar(cols[:, :], col_all[:, :, 0], mix[:, 0:1], None, op0=ALU.mult).then_inc(mixed, 1)
            for b in range(1, SLICES):
                v.wait_ge(mixed, 2 * b)
                v.scalar_tensor_tensor(out=w_mix[:, :], in0=w_all[:, b, :], scalar=mix[:, b:b + 1], in1=w_mix[:, :],
                                       op0=ALU.mult, op1=ALU.add).then_inc(mixed, 1)
                v.scalar_tensor_tensor(out=cols[:, :], in0=col_all[:, :, b], scalar=mix[:, b:b + 1], in1=cols[:, :],
                                       op0=ALU.mult, op1=ALU.add).then_inc(mixed, 1)
            v.wait_ge(mixed, 2 * SLICES)
            v.wait_ge(spread, 1)
            v.wait_ge(drawn, 1)
            for h in range(HEADS):
                rows = slice(CH * h, CH * h + CH)
                v.tensor_copy(eye_att[rows, D + h:D + h + 1], cols[rows, 1:2])
                v.tensor_copy(eye_att[rows, D + HEADS + h:D + HEADS + h + 1], cols[rows, 2:3])
            v.tensor_copy(eye_att[:, 0:D], k.ident[:, :])
            v.tensor_scalar(bias_wide[:, :], k.ones[:, :], cols[:, 0:1], None, op0=ALU.mult).then_inc(spread, 1)
            v.wait_ge(folded, 2)
            v.tensor_copy(k.proj[:, :], ps_w[:, 0:D + 2 * HEADS])
            v.tensor_copy(k.proj_bias[:, :], ps_b[:, 0:D + 2 * HEADS]).then_inc(kept, 1)
            v.wait_ge(kept, 2)

        @block.tensor
        def _(pe):
            pe.wait_ge(spread, 2)
            pe.matmul(ps_w[:, 0:D + 2 * HEADS], w_mix[:, :], eye_att[:, :], start=True, stop=True).then_inc(folded, 1)
            pe.matmul(ps_b[:, 0:D + 2 * HEADS], bias_wide[:, :], eye_att[:, :], start=True, stop=True).then_inc(folded, 1)



def edges_in(nc, m, k, e, src, dst, flag):
    prev = m.sb("prev", [P, T], I32)
    prev_f = m.sb("prev_f", [P, T])
    falls = m.sb("falls", [P, T])
    fall = m.sb("fall", [P, 1])
    ps_f = m.ps("ps_fall")
    blank, loaded, step, counted = m.sem("edges_blank"), m.sem("edges_loaded"), m.sem("falls_step"), m.sem("falls_counted")

    with nc.Block() as block:
        @block.sync
        def _(sp):
            wait_apart(sp, k.sp_past, blank, 1)
            loads = [
                (e.src[0:P - 1, 0:T], src[0:LAST_FULL].rearrange("(p t) -> p t", t=T)),
                (e.src[P - 1:P, 0:REST], src[LAST_FULL:E].unsqueeze(0)),
                (e.dst[0:P - 1, :], dst[0:LAST_FULL].rearrange("(p t) -> p t", t=T)),
                (e.dst[P - 1:P, 0:REST], dst[LAST_FULL:E].unsqueeze(0)),
                (prev[0:1, 1:T], dst[0:T - 1].unsqueeze(0)),
                (prev[1:P - 1, :], dst[T - 1:LAST_FULL - 1].rearrange("(p t) -> p t", t=T)),
                (prev[P - 1:P, 0:REST + 1], dst[LAST_FULL - 1:E].unsqueeze(0)),
            ]
            for to, of in loads:
                sp.dma_start(to, of).then_inc(loaded, 16)
            wait_apart(sp, k.sp_past, loaded, 16 * len(loads))

        @block.vector
        def _(v):
            v.memset(e.src[:, :], 0)
            v.memset(e.dst[:, :], PAD_DST)
            v.memset(prev[:, :], 0).then_inc(blank, 1)
            v.wait_ge(loaded, 16 * 7)
            v.tensor_copy(e.dst_f[:, :], e.dst[:, :])
            v.tensor_copy(prev_f[:, :], prev[:, :]).then_inc(step, 1)
            v.wait_ge(step, 1)
            v.tensor_tensor(falls[:, :], prev_f[:, :], e.dst_f[:, :], op=ALU.is_gt).then_inc(step, 1)
            v.wait_ge(step, 2)
            v.tensor_reduce(fall[:, :], falls[:, :], AX.X, ALU.max).then_inc(step, 1)
            v.wait_ge(counted, 1)
            v.tensor_copy(flag[:, :], ps_f[0:1, 0:1]).then_inc(step, 1)
            v.wait_ge(step, 4)

        @block.tensor
        def _(pe):
            pe.wait_ge(step, 3)
            pe.matmul(ps_f[0:1, 0:1], fall[:, :], k.ones[:, 0:1], start=True, stop=True).then_inc(counted, 1)


def edges_sorted(nc, m, k, e, flag, by_low, by_dst):
    pairs = m.sb("pairs", [P, T, 2], I32)
    bucket_i = m.sb("bucket_i", [P, T], I32)
    bucket = m.sb("bucket", [P, T])
    number_i = m.sb("number_i", [P, RADIX], I32)
    number = m.sb("number", [P, RADIX])
    count = m.sb("count", [P, RADIX])
    ends = m.sb("ends", [P, RADIX])
    place = m.sb("place", [P, RADIX])
    scrap = m.sb("scrap", [P, RADIX])
    at = m.sb("at", [P, 1])
    at_i = m.sb("at_i", [P, 1], I32)
    pair = m.sb("pair", [P, 2], I32)
    ps_c = m.ps("ps_count")
    ps_e = m.ps("ps_before")
    numbered, ready, counted, summed, sent, back = (m.sem("sort_numbered"), m.sem("sort_ready"), m.sem("sort_counted"),
                                                    m.sem("sort_summed"), m.sem("sort_sent"), m.sem("sort_back"))
    step, taken, placed = m.sem("sort_step"), m.sem("sort_taken"), m.sem("sort_placed")
    passes = [(0, P, by_low), (1, T, by_dst)]

    with nc.Block() as block:
        @block.gpsimd
        def _(pool):
            nc.gpsimd.iota(number_i[:, :], pattern=[[1, RADIX]], base=0, channel_multiplier=0).then_inc(numbered, 1)
            with pool.If(pool.value_load(flag[0:1, 0:1], min_val=0, max_val=P) != 0):
                for n, radix, table in passes:
                    with pool.Fori(0, T) as t:
                        wait_apart(pool, k.pool_past, ready, n * T + t + 1)
                        pool.indirect_dma_start(table[:, :], bass.IndirectOffsetOnAxis(at_i[:, 0:1], 0), pair[:, :],
                                                None).then_inc(sent, 16)
                        wait_apart(pool, k.pool_past, sent, 16 * (n * T + t + 1))
                        pool.sem_inc(taken, 1)

        @block.sync
        def _(sp):
            with sp.If(sp.value_load(flag[0:1, 0:1], min_val=0, max_val=P) != 0):
                for n, radix, table in passes:
                    wait_apart(sp, k.sp_past, taken, (n + 1) * T)
                    sp.dma_start(pairs[:, :, :], table.rearrange("(p t) two -> p t two", t=T)).then_inc(back, 16)
                    wait_apart(sp, k.sp_past, back, 16 * (n + 1))

        @block.tensor
        def _(pe):
            with pe.If(pe.value_load(flag[0:1, 0:1], min_val=0, max_val=P) != 0):
                for n, radix, table in passes:
                    pe.wait_ge(counted, n + 1)
                    pe.matmul(ps_c[:, 0:radix], k.ones[:, :], count[:, 0:radix], start=True, stop=True)
                    pe.matmul(ps_e[:, 0:radix], k.before[:, :], count[:, 0:radix], start=True,
                              stop=True).then_inc(summed, 1)

        @block.vector
        def _(v):
            with v.If(v.value_load(flag[0:1, 0:1], min_val=0, max_val=P) != 0):
                done = [0]

                def link(ins):
                    done[0] += 1
                    ins.then_inc(step, 1)
                    v.wait_ge(step, done[0])

                v.tensor_copy(pairs[:, :, 0], e.src[:, 0:T])
                link(v.tensor_copy(pairs[:, :, 1], e.dst[:, :]))
                v.wait_ge(numbered, 1)
                link(v.tensor_copy(number[:, :], number_i[:, :]))
                for n, radix, table in passes:
                    if n:
                        v.wait_ge(back, 16 * n)
                        link(v.tensor_single_scalar(bucket_i[:, :], pairs[:, :, 1], 7, op=ALU.logical_shift_right))
                    else:
                        link(v.tensor_single_scalar(bucket_i[:, :], pairs[:, :, 1], P - 1, op=ALU.bitwise_and))
                    link(v.tensor_copy(bucket[:, :], bucket_i[:, :]))
                    link(v.memset(count[:, 0:radix], 0.0))
                    base = done[0]
                    with v.Fori(0, T) as t:
                        v.scalar_tensor_tensor(out=count[:, 0:radix], in0=number[:, 0:radix],
                                               scalar=bucket[:, bass.ds(t, 1)], in1=count[:, 0:radix],
                                               op0=ALU.is_equal, op1=ALU.add).then_inc(step, 1)
                        v.wait_ge(step, t + (base + 1))
                    done[0] += T
                    v.sem_inc(counted, 1)
                    v.wait_ge(summed, n + 1)
                    link(v.tensor_copy(scrap[:, 0:radix], ps_c[:, 0:radix]))
                    link(v.tensor_tensor_scan(ends[:, 0:radix], k_ones(k, radix), scrap[:, 0:radix], 0.0,
                                              op0=ALU.mult, op1=ALU.add))
                    link(v.tensor_tensor(ends[:, 0:radix], ends[:, 0:radix], scrap[:, 0:radix], op=ALU.subtract))
                    link(v.tensor_tensor(place[:, 0:radix], ends[:, 0:radix], ps_e[:, 0:radix], op=ALU.add))
                    base = done[0]
                    with v.Fori(0, T) as t:
                        v.scalar_tensor_tensor(out=scrap[:, 0:radix], in0=number[:, 0:radix],
                                               scalar=bucket[:, bass.ds(t, 1)], in1=place[:, 0:radix],
                                               op0=ALU.is_equal, op1=ALU.mult, accum_out=at[:, :]).then_inc(step, 1)
                        v.scalar_tensor_tensor(out=place[:, 0:radix], in0=number[:, 0:radix],
                                               scalar=bucket[:, bass.ds(t, 1)], in1=place[:, 0:radix],
                                               op0=ALU.is_equal, op1=ALU.add).then_inc(step, 1)
                        v.wait_ge(step, 2 * t + (base + 2))
                        v.tensor_copy(at_i[:, :], at[:, :])
                        v.tensor_copy(pair[:, :], pairs[:, bass.ds(t, 1), :].rearrange("p one two -> p (one two)")).then_inc(ready, 1)
                        v.wait_ge(taken, n * T + t + 1)
                    done[0] += 2 * T
                v.wait_ge(back, 16 * len(passes))
                v.tensor_copy(e.src[:, 0:T], pairs[:, :, 0])
                v.tensor_copy(e.dst[:, :], pairs[:, :, 1]).then_inc(placed, 1)
                v.wait_ge(placed, 1)


def k_ones(k, n):
    return k.ones[:, 0:1].to_broadcast([P, n])


def edge_marks(nc, m, k, e, joint):
    src_f = m.sb("src_f", [P, T])
    first = m.sb("first", [P, T])
    in_head = m.sb("in_head", [P, T])
    in_tail = m.sb("in_tail", [P, T])
    work = m.sb("work", [P, T])
    step = m.sem("marks_step")

    with nc.Block() as block:
        @block.vector
        def _(v):
            done = [0]

            def link(ins):
                done[0] += 1
                ins.then_inc(step, 1)
                v.wait_ge(step, done[0])

            v.memset(first[:, 0:1], 1.0)
            v.memset(e.last[:, T - 1:T], 1.0)
            v.memset(e.dst_pick[:, T:], 0)
            v.memset(e.pick_rev[:, T:], 0)
            v.memset(e.key_rev[:, T:], 0.0)
            v.tensor_copy(src_f[:, :], e.src[:, 0:T])
            link(v.tensor_copy(e.dst_f[:, :], e.dst[:, :]))
            v.tensor_tensor(first[:, 1:T], e.dst_f[:, 1:T], e.dst_f[:, 0:T - 1], op=ALU.not_equal)
            v.tensor_tensor(e.last[:, 0:T - 1], e.dst_f[:, 1:T], e.dst_f[:, 0:T - 1], op=ALU.not_equal)
            v.tensor_scalar(in_head[:, :], e.dst_f[:, :], e.dst_f[:, 0:1], None, op0=ALU.is_equal)
            v.tensor_scalar(in_tail[:, :], e.dst_f[:, :], e.dst_f[:, T - 1:T], None, op0=ALU.is_equal)
            link(v.tensor_scalar(e.dst_pick[:, 0:T], e.dst_f[:, :], float(N - 1), None, op0=ALU.min))
            v.tensor_scalar(e.reset[:, :], first[:, :], -BIG, None, op0=ALU.mult)
            v.tensor_scalar(e.go_on_rev[:, ::-1], e.last[:, :], -1.0, 1.0, op0=ALU.mult, op1=ALU.add)
            v.tensor_reduce(joint["head_len"][:, :], in_head[:, :], AX.X, ALU.add)
            v.tensor_scalar(work[:, :], in_tail[:, :], -1.0, 1.0, op0=ALU.mult, op1=ALU.add).then_inc(step, 1)
            done[0] += 1
            v.wait_ge(step, done[0])
            link(v.tensor_tensor(work[:, :], work[:, :], e.last[:, :], op=ALU.mult))
            link(v.tensor_tensor(e.head_end[:, :], work[:, :], in_head[:, :], op=ALU.mult))
            link(v.tensor_tensor(work[:, :], work[:, :], e.head_end[:, :], op=ALU.subtract))
            link(v.scalar_tensor_tensor(out=work[:, :], in0=e.dst_f[:, :], scalar=-float(SKIP), in1=work[:, :],
                                        op0=ALU.add, op1=ALU.mult))
            v.tensor_scalar(e.put[:, :], work[:, :], float(SKIP), None, op0=ALU.add)
            link(v.tensor_scalar(first[:, :], e.dst_f[:, :], float(N), float(N + P - 1), op0=ALU.is_ge, op1=ALU.mult))
            v.tensor_tensor(e.key_rev[:, 0:T][:, ::-1], first[:, :], src_f[:, :], op=ALU.max)
            link(v.tensor_scalar(e.pick_rev[:, 0:T][:, ::-1], src_f[:, :], 2.0, 1.0, op0=ALU.mult, op1=ALU.add))



def norm_moments(v, x, stats, small, step, at, parts, tiles):
    for j in range(tiles):
        ins = v.bn_stats(stats[0:parts, j, :], x(j))
    ins.then_inc(step, 1)
    v.wait_ge(step, at + 1)
    st = stats[0:parts, 0:tiles, :]
    v.tensor_tensor(small[0:parts, 0, 0:tiles], st[:, :, 1], st[:, :, 4], op=ALU.add)
    v.tensor_tensor(small[0:parts, 1, 0:tiles], st[:, :, 1], st[:, :, 4], op=ALU.subtract)
    v.tensor_tensor(small[0:parts, 2, 0:tiles], st[:, :, 2], st[:, :, 5], op=ALU.add).then_inc(step, 1)
    v.wait_ge(step, at + 2)
    v.tensor_tensor(small[0:parts, 3, 0:tiles], small[0:parts, 1, 0:tiles], small[0:parts, 1, 0:tiles], op=ALU.mult)
    v.tensor_scalar(small[0:parts, 2, 0:tiles], small[0:parts, 2, 0:tiles], 1.0 / D, None, op0=ALU.mult).then_inc(step, 1)
    v.wait_ge(step, at + 3)


NORM_STEPS = 3



def nodes_in(nc, m, k, x, by_src, by_dst, pairs):
    src_rows = [m.sb(f"src_rows{i}", [P, NC, XT]) for i in range(NB)]
    dst_rows = [m.sb(f"dst_rows{i}", [P, NC, XD]) for i in range(NB)]
    pair_rows = [m.sb(f"pair_rows{i}", [P, NC, PAIR]) for i in range(NB)]
    normed = [m.sb(f"normed{i}", [P, NC, D]) for i in range(NB)]
    turned = [m.sb(f"turned{i}", [P, 3, D]) for i in range(2)]
    stats = [m.sb(f"stats{i}", [P, NC, 6]) for i in range(NB)]
    small = [m.sb(f"small{i}", [P, 8, NC]) for i in range(NB)]
    ps_t = [m.ps(f"ps_t{i}") for i in range(2)]
    ps_a = [m.ps(f"ps_a{i}") for i in range(2)]
    ps_b = [m.ps(f"ps_b{i}") for i in range(2)]
    x_in = m.sems("in_x_landed", NB)
    stored = m.sems("in_stored", NB)
    moments, varied, rooted, scaled, biased = (m.sem("in_moments"), m.sem("in_varied"), m.sem("in_rooted"),
                                               m.sem("in_scaled"), m.sem("in_biased"))
    x_copied, norm_done, turn_done, turn_kept, mul_done, mul_kept = (
        m.sem("in_x_copied"), m.sem("in_norm_done"), m.sem("in_turn_done"), m.sem("in_turn_kept"),
        m.sem("in_mul_done"), m.sem("in_mul_kept"))

    def groups(ch):
        for g, (j, n) in enumerate(ch.groups):
            yield ch.c * ch.per + g, g % 2, j, n

    with nc.Block() as block:
        @block.sync
        def _(sp):
            def load(ch):
                wait_apart(sp, k.sp_past, stored[ch.buf], 48 * ch.turn)
                sp.dma_start(pair_rows[ch.buf][0:ch.parts, 0:ch.tiles, 0:D], ch.rows(x, slice(0, D))).then_inc(x_in[ch.buf], 16)

            def store(ch):
                part = (slice(0, ch.parts), slice(0, ch.tiles))
                wait_apart(sp, k.sp_past, x_copied, ch.c + 1)
                wait_apart(sp, k.sp_past, mul_kept, ch.c * ch.per + len(ch.groups))
                for table, rows, width in ((by_src, src_rows, XT), (by_dst, dst_rows, XD), (pairs, pair_rows, PAIR)):
                    sp.dma_start(ch.rows(table, slice(0, width)), rows[ch.buf][part]).then_inc(stored[ch.buf], 16)

            node_chunks(sp, load, store)
            for h in range(NB):
                wait_apart(sp, k.sp_past, stored[h], 48 * (TURNS + (h == 0)))

        @block.vector
        def _(v):
            def norm(ch):
                p, n, s = ch.parts, ch.tiles, small[ch.buf]
                v.wait_ge(x_in[ch.buf], 16 * (ch.turn + 1))
                norm_moments(v, lambda j: pair_rows[ch.buf][0:p, j, 0:D], stats[ch.buf], s, moments, NORM_STEPS * ch.c, p, n)
                v.scalar_tensor_tensor(out=s[0:p, 4, 0:n], in0=s[0:p, 3, 0:n], scalar=0.25, in1=s[0:p, 2, 0:n],
                                       op0=ALU.mult, op1=ALU.add).then_inc(varied, 1)
                v.wait_ge(rooted, ch.c + 1)
                wait_past(v, norm_done, ch.c - (NB - 1))
                v.reciprocal(s[0:p, 6, 0:n], s[0:p, 5, 0:n]).then_inc(scaled, 1)
                v.wait_ge(scaled, ch.c + 1)
                v.scalar_tensor_tensor(out=s[0:p, 7, 0:n], in0=s[0:p, 0, 0:n], scalar=-0.5, in1=s[0:p, 6, 0:n],
                                       op0=ALU.mult, op1=ALU.mult).then_inc(biased, 1)

            def keep(ch):
                p = ch.parts
                wait_past(v, stored[ch.buf], 48 * ch.turn)
                for q, b, j, n in groups(ch):
                    a = ps_a[b][0:p, 0:n * (D + 2 * HEADS)].rearrange("p (j f) -> p j f", j=n)
                    bias = k.proj_bias[0:p, :].unsqueeze(1)
                    v.wait_ge(mul_done, q + 1)
                    v.tensor_tensor(src_rows[ch.buf][0:p, j:j + n, :], a[:, :, 0:XT],
                                    bias[:, :, 0:XT].to_broadcast([p, n, XT]), op=ALU.add)
                    v.tensor_tensor(dst_rows[ch.buf][0:p, j:j + n, D:XD], a[:, :, XT:XT + HEADS],
                                    bias[:, :, XT:XT + HEADS].to_broadcast([p, n, HEADS]), op=ALU.add)
                    v.tensor_tensor(pair_rows[ch.buf][0:p, j:j + n, D:PAIR],
                                    ps_b[b][0:p, 0:n * D].rearrange("p (j f) -> p j f", j=n),
                                    k.b1[0:p, :].unsqueeze(1).to_broadcast([p, n, D]), op=ALU.add).then_inc(mul_kept, 1)

            node_chunks(v, norm, keep)

        @block.scalar
        def _(act):
            def norm(ch):
                p, n, s = ch.parts, ch.tiles, small[ch.buf]
                act.wait_ge(varied, ch.c + 1)
                act.activation(s[0:p, 5, 0:n], s[0:p, 4, 0:n], ACT.Sqrt, bias=k.eps[0:p, :]).then_inc(rooted, 1)
                wait_past(act, stored[ch.buf], 48 * ch.turn)
                act.activation(dst_rows[ch.buf][0:p, 0:n, 0:D], pair_rows[ch.buf][0:p, 0:n, 0:D], ACT.Copy).then_inc(x_copied, 1)
                act.wait_ge(biased, ch.c + 1)
                wait_past(act, turn_done, (ch.c - (NB - 1)) * ch.per)
                for j in range(n):
                    ins = act.activation(normed[ch.buf][0:p, j, :], pair_rows[ch.buf][0:p, j, 0:D], ACT.Relu,
                                         bias=s[0:p, 7, j:j + 1], scale=s[0:p, 6, j:j + 1])
                ins.then_inc(norm_done, 1)

            def turn(ch):
                p = ch.parts
                for q, b, j, n in groups(ch):
                    act.wait_ge(turn_done, q + 1)
                    wait_past(act, mul_done, q - 1)
                    act.activation(turned[b][:, 0:n, 0:p], ps_t[b][:, 0:n * D].rearrange("p (j f) -> p j f", j=n)[:, :, 0:p],
                                   ACT.Copy).then_inc(turn_kept, 1)

            node_chunks(act, norm, turn)

        @block.tensor
        def _(pe):
            def nothing(ch):
                pass

            def multiply(ch, q, b, j, n):
                p = ch.parts
                pe.wait_ge(turn_kept, q + 1)
                wait_past(pe, mul_kept, q - 1)
                for i in range(n):
                    w = D + 2 * HEADS
                    pe.matmul(ps_a[b][0:p, i * w:(i + 1) * w], turned[b][:, i, 0:p], k.proj[:, :], start=True, stop=True)
                    ins = pe.matmul(ps_b[b][0:p, i * D:(i + 1) * D], turned[b][:, i, 0:p], k.w1_src[:, :], start=True, stop=True)
                ins.then_inc(mul_done, 1)

            def chunk(ch):
                p, late = ch.parts, None
                pe.wait_ge(norm_done, ch.c + 1)
                for q, b, j, n in groups(ch):
                    wait_past(pe, turn_kept, q - 1)
                    for i in range(n):
                        ins = pe.transpose(ps_t[b][:, i * D:i * D + p], normed[ch.buf][0:p, j + i, :], k.ident[0:p, 0:p])
                    ins.then_inc(turn_done, 1)
                    if late:
                        multiply(*late)
                    late = (ch, q, b, j, n)
                multiply(*late)

            node_chunks(pe, nothing, chunk)



def attention(nc, m, k, e, by_src, by_dst, pairs, h_rev, sums, joint):
    HALF = EC // 2
    src_rows = [m.sb(f"at_src{i}", [P, EC, XT]) for i in range(2)]
    dst_rows = [m.sb(f"at_dst{i}", [P, EC, XD]) for i in range(2)]
    out_rows = [m.sb(f"at_out{i}", [P, EC, PAIR]) for i in range(2)]
    h_rows = [m.sb(f"at_h{i}", [P, EC, D]) for i in range(2)]
    src_at = [m.sb(f"src_at{i}", [P, EC], I32) for i in range(2)]
    dst_at = [m.sb(f"dst_at{i}", [P, EC], I32) for i in range(2)]
    put_at = [m.sb(f"put_at{i}", [P, EC], I32) for i in range(2)]
    score = m.sb("score", [P, HEADS, EC])
    score_in = m.sb("score_in", [P, HEADS, SLOTS])
    reset_in = m.sb("reset_in", [P, HEADS, SLOTS])
    peak = m.sb("peak", [P, HEADS, SLOTS])
    gap = m.sb("gap", [P, 2, HEADS, EC])
    fade = m.sb("fade", [P, HEADS, SLOTS])
    weight = m.sb("weight", [P, HEADS, SLOTS])
    total = m.sb("total", [P, HEADS, SLOTS])
    over = m.sb("over", [P, HEADS, EC])
    fades = m.sb("fades", [P, D, SLOTS])
    part = m.sb("part", [P, D, SLOTS])
    acc = m.sb("acc", [P, D, SLOTS])
    mixed = m.sb("mixed_rows", [P, EC, D])
    caught = m.sb("caught", [P, D, EC])
    caught_sum = m.sb("caught_sum", [P, D])
    few = m.sb("few", [P, 2, HEADS, EC])
    few_sum = m.sb("few_sum", [P, 2, HEADS])
    stats = m.sb("at_stats", [P, EC, 6])
    small = m.sb("at_small", [P, 8, EC])
    turned = [m.sb(f"at_turned{i}", [P, HALF, P]) for i in range(2)]
    zeros = m.sb("zeros", [P, EC * AGG])
    ps_t = [m.ps(f"at_ps_t{i}", 2) for i in range(2)]
    ps_p = [m.ps(f"at_ps_p{i}", 2) for i in range(2)]
    picked = m.sems("at_picked", 2)
    put = m.sems("at_put", 2)
    h_out = m.sems("at_h_out", 2)
    zeroed, ready, set_up = m.sem("at_zeroed"), m.sem("at_indices"), m.sem("at_set_up")
    step, gaps, fade_done, weight_done, spread = (m.sem("at_step"), m.sem("at_gaps"), m.sem("at_fade"),
                                                  m.sem("at_weight"), m.sem("at_spread"))
    moments, varied, rooted, scaled = m.sem("at_moments"), m.sem("at_varied"), m.sem("at_rooted"), m.sem("at_scaled")
    norm_done, turn_done, turn_kept, mul_done, rows_done, scanned = (
        m.sem("at_norm_done"), m.sem("at_turn_done"), m.sem("at_turn_kept"), m.sem("at_mul_done"),
        m.sem("at_rows_done"), m.sem("at_scanned"))
    PICKS = 16 * 2 * EC
    PUTS = 16 * EC
    STEPS = 13

    with nc.Block() as block:
        @block.gpsimd
        def _(pool):
            def pick(c, b, turn):
                wait_apart(pool, k.pool_past, ready, c + 1)
                for j in range(EC):
                    pool.indirect_dma_start(src_rows[b][:, j, :], None, by_src[:, :],
                                            bass.IndirectOffsetOnAxis(src_at[b][:, j:j + 1], 0)).then_inc(picked[b], 16)
                    pool.indirect_dma_start(dst_rows[b][:, j, :], None, by_dst[:, :],
                                            bass.IndirectOffsetOnAxis(dst_at[b][:, j:j + 1], 0)).then_inc(picked[b], 16)

            def put_rows(c, b):
                wait_apart(pool, k.pool_past, rows_done, 2 * c + 2)
                for j in range(EC):
                    pool.indirect_dma_start(pairs[:, :], bass.IndirectOffsetOnAxis(put_at[b][:, j:j + 1], 0),
                                            out_rows[b][:, j, :], None, bounds_check=N - 1,
                                            oob_is_err=False).then_inc(put[b], 16)

            pick(0, 0, 0)
            with pool.Fori(0, ECHUNKS // 2 - 1) as t:
                pick(2 * t + 1, 1, t)
                put_rows(2 * t, 0)
                pick(2 * t + 2, 0, t + 1)
                put_rows(2 * t + 1, 1)
            pick(ECHUNKS - 1, 1, ECHUNKS // 2 - 1)
            put_rows(ECHUNKS - 2, 0)
            put_rows(ECHUNKS - 1, 1)
            for b in range(2):
                wait_apart(pool, k.pool_past, put[b], PUTS * (ECHUNKS // 2))

        @block.sync
        def _(sp):
            wait_apart(sp, k.sp_past, set_up, 1)

            def chunk(c, b, turn):
                for table in sums:
                    sp.dma_start(table[bass.ds(c * (P * EC), P * EC), :].rearrange("(p j) f -> p (j f)", p=P),
                                 zeros[:, :]).then_inc(zeroed, 16)
                wait_apart(sp, k.sp_past, norm_done, c + 1)
                sp.dma_start(h_rev[:, bass.ds((ECHUNKS - 1 - c) * EC, EC), :], h_rows[b][:, :, :]).then_inc(h_out[b], 16)

            edge_chunks(sp, chunk)
            wait_apart(sp, k.sp_past, zeroed, 16 * 2 * ECHUNKS)
            for b in range(2):
                wait_apart(sp, k.sp_past, h_out[b], 16 * (ECHUNKS // 2))

        @block.vector
        def _(v):
            def indices(c, b):
                v.tensor_copy(src_at[b][:, :], e.src[:, bass.ds(c * EC, EC)])
                v.tensor_copy(dst_at[b][:, :], e.dst_pick[:, bass.ds(c * EC, EC)]).then_inc(ready, 1)

            for b in range(2):
                indices(b, b)
            v.memset(reset_in[:, :, 0:1], -BIG)
            v.memset(fade[:, :, :], 0.0)
            v.memset(peak[:, :, :], 0.0)
            v.memset(total[:, :, :], 0.0)
            v.memset(acc[:, :, :], 0.0)
            v.memset(joint["head"][:, :], 0.0)
            v.memset(zeros[:, :], 0.0).then_inc(set_up, 1)
            v.wait_ge(set_up, 1)

            def chunk(c, b, turn):
                cols = bass.ds(c * EC, EC)
                base = c * STEPS
                xs, xd, out, s = src_rows[b], dst_rows[b], out_rows[b], small

                def at(n):
                    v.wait_ge(step, base + n)

                if not (isinstance(c, int) and c == 0):
                    v.wait_ge(scanned, 3 * c)
                v.tensor_copy(score_in[:, :, 0:1], peak[:, :, EC:SLOTS])
                v.tensor_copy(weight[:, :, 0:1], total[:, :, EC:SLOTS])
                v.tensor_copy(part[:, :, 0:1], acc[:, :, EC:SLOTS])
                v.tensor_copy(reset_in[:, :, 1:SLOTS], e.reset[:, cols].unsqueeze(1).to_broadcast([P, HEADS, EC])).then_inc(step, 1)
                v.wait_ge(picked[b], PICKS * (turn + 1))
                v.tensor_tensor(score[:, :, :], xs[:, :, D:XT].rearrange("p j h -> p h j"),
                                xd[:, :, D:XD].rearrange("p j h -> p h j"), op=ALU.add).then_inc(step, 1)
                at(2)
                v.scalar_tensor_tensor(out=score_in[:, :, 1:SLOTS], in0=score[:, :, :], scalar=SLOPE, in1=score[:, :, :],
                                       op0=ALU.mult, op1=ALU.max).then_inc(step, 1)
                at(3)
                v.tensor_tensor_scan(peak[:, :, :].rearrange("p h j -> p (h j)"), reset_in[:, :, :].rearrange("p h j -> p (h j)"),
                                     score_in[:, :, :].rearrange("p h j -> p (h j)"), 0.0, op0=ALU.add,
                                     op1=ALU.max).then_inc(scanned, 1)
                v.wait_ge(scanned, 3 * c + 1)
                v.tensor_tensor(score[:, :, :], peak[:, :, 0:EC], reset_in[:, :, 1:SLOTS], op=ALU.add).then_inc(step, 1)
                v.tensor_tensor(gap[:, 1, :, :], score_in[:, :, 1:SLOTS], peak[:, :, 1:SLOTS], op=ALU.subtract)
                at(4)
                v.tensor_tensor(gap[:, 0, :, :], score[:, :, :], peak[:, :, 1:SLOTS], op=ALU.subtract).then_inc(gaps, 1)
                v.wait_ge(weight_done, c + 1)
                v.tensor_tensor_scan(total[:, :, :].rearrange("p h j -> p (h j)"), fade[:, :, :].rearrange("p h j -> p (h j)"),
                                     weight[:, :, :].rearrange("p h j -> p (h j)"), 0.0, op0=ALU.mult,
                                     op1=ALU.add).then_inc(scanned, 1)
                v.tensor_tensor(part[:, :, 1:SLOTS].rearrange("p (h f) j -> p h f j", h=HEADS),
                                xs[:, :, 0:D].rearrange("p j (h f) -> p h f j", h=HEADS),
                                weight[:, :, 1:SLOTS].unsqueeze(2).to_broadcast([P, HEADS, CH, EC]),
                                op=ALU.mult).then_inc(step, 1)
                v.wait_ge(scanned, 3 * c + 2)
                v.tensor_scalar(over[:, :, :], total[:, :, 1:SLOTS], 1e-16, None, op0=ALU.add).then_inc(step, 1)
                at(6)
                v.reciprocal(score[:, :, :], over[:, :, :])
                v.wait_ge(spread, c + 1)
                v.tensor_tensor_scan(acc[:, :, :].rearrange("p f j -> p (f j)"), fades[:, :, :].rearrange("p f j -> p (f j)"),
                                     part[:, :, :].rearrange("p f j -> p (f j)"), 0.0, op0=ALU.mult,
                                     op1=ALU.add).then_inc(scanned, 1)
                v.wait_ge(scanned, 3 * c + 3)
                v.tensor_tensor(mixed[:, :, :].rearrange("p j (h f) -> p h f j", h=HEADS),
                                acc[:, :, 1:SLOTS].rearrange("p (h f) j -> p h f j", h=HEADS),
                                score[:, :, :].unsqueeze(2).to_broadcast([P, HEADS, CH, EC]),
                                op=ALU.mult).then_inc(step, 1)
                at(7)
                if not (isinstance(turn, int) and turn == 0):
                    v.wait_ge(put[b], PUTS * turn)
                v.tensor_tensor(out[:, :, 0:D], mixed[:, :, :], xd[:, :, 0:D], op=ALU.add).then_inc(step, 1)
                indices(c + 2, b)
                v.tensor_copy(put_at[b][:, :], e.put[:, cols])
                mark = e.head_end[:, cols]
                v.tensor_tensor(caught[:, :, :], acc[:, :, 1:SLOTS], mark.unsqueeze(1).to_broadcast([P, D, EC]), op=ALU.mult)
                v.tensor_tensor(few[:, 0, :, :], peak[:, :, 1:SLOTS], mark.unsqueeze(1).to_broadcast([P, HEADS, EC]), op=ALU.mult)
                v.tensor_tensor(few[:, 1, :, :], total[:, :, 1:SLOTS], mark.unsqueeze(1).to_broadcast([P, HEADS, EC]),
                                op=ALU.mult).then_inc(step, 1)
                at(9)
                v.tensor_reduce(caught_sum[:, :], caught[:, :, :], AX.X, ALU.add)
                v.tensor_reduce(few_sum[:, :, :], few[:, :, :, :], AX.X, ALU.add).then_inc(step, 1)
                at(10)
                head = joint["head"]
                v.tensor_tensor(head[:, 0:D], head[:, 0:D], caught_sum[:, :], op=ALU.add)
                v.tensor_tensor(head[:, D:D + 2 * HEADS], head[:, D:D + 2 * HEADS],
                                few_sum[:, :, :].rearrange("p two h -> p (two h)"), op=ALU.add).then_inc(step, 1)
                norm_moments(v, lambda j: out[:, j, 0:D], stats, s, moments, NORM_STEPS * c, P, EC)
                v.scalar_tensor_tensor(out=s[:, 4, :], in0=s[:, 3, :], scalar=0.25, in1=s[:, 2, :],
                                       op0=ALU.mult, op1=ALU.add).then_inc(varied, 1)
                v.wait_ge(rooted, c + 1)
                wait_past(v, norm_done, c)
                v.reciprocal(s[:, 3, :], s[:, 5, :]).then_inc(step, 1)
                at(12)
                v.tensor_tensor(s[:, 6, :], s[:, 3, :], e.last[:, cols], op=ALU.mult).then_inc(step, 1)
                at(13)
                v.scalar_tensor_tensor(out=s[:, 7, :], in0=s[:, 0, :], scalar=-0.5, in1=s[:, 6, :],
                                       op0=ALU.mult, op1=ALU.mult).then_inc(scaled, 1)
                for half in range(2):
                    js = slice(half * HALF, half * HALF + HALF)
                    v.wait_ge(mul_done, 2 * c + half + 1)
                    v.tensor_tensor(out[:, js, D:PAIR], ps_p[half][:, 0:HALF * D].rearrange("p (j f) -> p j f", j=HALF),
                                    k.b1[:, :].unsqueeze(1).to_broadcast([P, HALF, D]), op=ALU.add).then_inc(rows_done, 1)

            edge_chunks(v, chunk)
            v.tensor_copy(joint["tail"][:, 0:D], acc[:, :, EC])
            v.tensor_copy(joint["tail"][:, D:D + HEADS], peak[:, :, EC])
            v.tensor_copy(joint["tail"][:, D + HEADS:D + 2 * HEADS], total[:, :, EC]).then_inc(set_up, 1)
            v.wait_ge(set_up, 2)

        @block.scalar
        def _(act):
            def chunk(c, b, turn):
                act.wait_ge(gaps, c + 1)
                act.activation(fade[:, :, 1:SLOTS], gap[:, 0, :, :], ACT.Exp).then_inc(fade_done, 1)
                act.activation(weight[:, :, 1:SLOTS], gap[:, 1, :, :], ACT.Exp).then_inc(weight_done, 1)
                act.wait_ge(fade_done, c + 1)
                act.activation(fades[:, :, :].rearrange("p (h f) j -> p h f j", h=HEADS),
                               fade[:, :, :].unsqueeze(2).to_broadcast([P, HEADS, CH, SLOTS]), ACT.Copy).then_inc(spread, 1)
                act.wait_ge(varied, c + 1)
                act.activation(small[:, 5, :], small[:, 4, :], ACT.Sqrt, bias=k.eps[:, :]).then_inc(rooted, 1)
                act.wait_ge(scaled, c + 1)
                if not (isinstance(turn, int) and turn == 0):
                    act.wait_ge(h_out[b], 16 * turn)
                wait_past(act, turn_done, 2 * c - 2)
                for j in range(EC):
                    ins = act.activation(h_rows[b][:, EC - 1 - j, :], out_rows[b][:, j, 0:D], ACT.Relu,
                                         bias=small[:, 7, j:j + 1], scale=small[:, 6, j:j + 1])
                ins.then_inc(norm_done, 1)
                for half in range(2):
                    act.wait_ge(turn_done, 2 * c + half + 1)
                    wait_past(act, mul_done, 2 * c + half - 1)
                    act.activation(turned[half][:, :, :], ps_t[half][:, 0:HALF * P].rearrange("p (j f) -> p j f", j=HALF),
                                   ACT.Copy).then_inc(turn_kept, 1)

            edge_chunks(act, chunk)

        @block.tensor
        def _(pe):
            def chunk(c, b, turn):
                pe.wait_ge(norm_done, c + 1)
                for half in range(2):
                    wait_past(pe, turn_kept, 2 * c + half - 1)
                    for i in range(HALF):
                        ins = pe.transpose(ps_t[half][:, i * P:(i + 1) * P], h_rows[b][:, EC - 1 - (half * HALF + i), :], k.ident[:, :])
                    ins.then_inc(turn_done, 1)
                for half in range(2):
                    pe.wait_ge(turn_kept, 2 * c + half + 1)
                    wait_past(pe, rows_done, 2 * c + half - 1)
                    for i in range(HALF):
                        ins = pe.matmul(ps_p[half][:, i * D:(i + 1) * D], turned[half][:, i, :], k.w1_src[:, :], start=True, stop=True)
                    ins.then_inc(mul_done, 1)

            edge_chunks(pe, chunk)



def joints(nc, m, k, e, by_dst, pairs, h_rev, joint):
    W = D + HEADS
    part = [joint["tail"], joint["head"]]
    key = m.sb("j_key", [P, 2])
    key_at = [m.sb(f"j_at{i}", [P, 1], I32) for i in range(2)]
    same = [m.sb(f"j_same{i}", [P, 2, P]) for i in range(2)]
    pen = m.sb("j_pen", [P, 2, P])
    top = [m.sb(f"j_top{i}", [P, HEADS]) for i in range(2)]
    cand = m.sb("j_cand", [P, HEADS, 2 * P])
    fac = m.sb("j_fac", [P, 2, HEADS])
    scaled = m.sb("j_scaled", [P, 2, W])
    xrow = [m.sb(f"j_x{i}", [P, XD]) for i in range(2)]
    den = m.sb("j_den", [P, 2, HEADS])
    rows = [m.sb(f"j_rows{i}", [P, PAIR]) for i in range(2)]
    h = [m.sb(f"j_h{i}", [P, D]) for i in range(2)]
    hT = [m.sb(f"j_ht{i}", [P, P]) for i in range(2)]
    stats = m.sb("j_stats", [P, 2, 6])
    small = m.sb("j_small", [P, 8, 2])
    scrap = m.sb("j_scrap", [P, P])
    cnt = m.sb("j_cnt", [P, 2])
    flat = m.sb("j_flat", [P, 4])
    put = [m.sb(f"j_put{i}", [P, 1], I32) for i in range(2)]
    h_put = m.sb("j_h_put", [P, 1], I32)
    ps_k = m.ps("j_ps_k")
    ps_m = m.ps("j_ps_m", 2)
    ps_s = m.ps("j_ps_s", 1)
    ps_h = m.ps("j_ps_h")
    step, turned, peaks, weighed, gathered, out, stage, muls, acts = (
        m.sem("j_step"), m.sem("j_turned"), m.sem("j_peaks"), m.sem("j_weighed"), m.sem("j_gathered"), m.sem("j_out"),
        m.sem("j_stage"), m.sem("j_muls"), m.sem("j_acts"))
    tails_out = m.sem("j_tails_out")
    keyed, indexed, masked, summed, normed_, h_kept, ready = (
        m.sem("j_keyed"), m.sem("j_indexed"), m.sem("j_masked"), m.sem("j_summed"), m.sem("j_normed"), m.sem("j_h_kept"),
        m.sem("j_ready"))
    edge0 = m.sb("j_edge0", [P, 1])

    with nc.Block() as block:
        @block.vector
        def _(v):
            done = [0]

            def link(ins):
                done[0] += 1
                ins.then_inc(step, 1)
                v.wait_ge(step, done[0])

            first, last = e.dst_f[:, 0:1], e.dst_f[:, T - 1:T]
            v.tensor_copy(key[:, 0:1], last)
            v.tensor_copy(key_at[0][:, :], e.dst_pick[:, T - 1:T])
            v.tensor_copy(key_at[1][:, :], e.dst_pick[:, 0:1]).then_inc(indexed, 1)
            link(v.tensor_tensor(flat[:, 0:1], first, last, op=ALU.is_equal))
            v.tensor_tensor(flat[:, 1:2], flat[:, 0:1], k.trash[:, :], op=ALU.mult)
            link(v.tensor_scalar(flat[:, 2:3], flat[:, 0:1], -1.0, 1.0, op0=ALU.mult, op1=ALU.add))
            link(v.tensor_tensor(flat[:, 3:4], flat[:, 2:3], first, op=ALU.mult))
            link(v.scalar_tensor_tensor(out=key[:, 1:2], in0=flat[:, 1:2], scalar=-1.0, in1=flat[:, 3:4],
                                        op0=ALU.mult, op1=ALU.add))
            v.sem_inc(keyed, 1)
            v.wait_ge(turned, 1)
            keys = ps_k[:, 0:2 * P].rearrange("p (a f) -> p a f", a=2)
            for i in range(2):
                link(v.tensor_scalar(same[i][:, :, :], keys, key[:, i:i + 1], None, op0=ALU.is_equal))
            v.sem_inc(masked, 1)
            for i in range(2):
                link(v.tensor_scalar(pen[:, :, :], same[i][:, :, :], -1.0, BIG, op0=ALU.add, op1=ALU.mult))
                v.wait_ge(peaks, 1)
                link(v.tensor_tensor(cand[:, :, :], ps_m[:, :].rearrange("p (h a) -> p h a", h=HEADS),
                                     pen[:, :, :].rearrange("p a f -> p (a f)").unsqueeze(1).to_broadcast([P, HEADS, 2 * P]), op=ALU.add))
                link(v.tensor_reduce(top[i][:, :], cand[:, :, :], AX.X, ALU.max))
                link(v.tensor_tensor(fac[:, i, :], part[i][:, D:D + HEADS], top[i][:, :], op=ALU.subtract))
            v.sem_inc(stage, 1)
            v.wait_ge(weighed, 1)
            for i in range(2):
                v.tensor_tensor(scaled[:, i, 0:D].rearrange("p (h f) -> p h f", h=HEADS),
                                part[i][:, 0:D].rearrange("p (h f) -> p h f", h=HEADS),
                                fac[:, i, :].unsqueeze(2).to_broadcast([P, HEADS, CH]), op=ALU.mult)
                link(v.tensor_tensor(scaled[:, i, D:W], part[i][:, D + HEADS:D + 2 * HEADS], fac[:, i, :], op=ALU.mult))
            v.sem_inc(stage, 1)
            v.tensor_tensor(scrap[:, :], same[0][:, 0, :], k.upto[:, :], op=ALU.mult)
            link(v.tensor_reduce(cnt[:, 1:2], same[1][:, 0, :], AX.X, ALU.max))
            link(v.tensor_reduce(cnt[:, 0:1], scrap[:, :], AX.X, ALU.add))
            link(v.tensor_scalar(flat[:, 0:1], cnt[:, 0:1], 1.0, None, op0=ALU.is_equal))
            link(v.tensor_scalar(flat[:, 3:4], cnt[:, 1:2], -1.0, 1.0, op0=ALU.mult, op1=ALU.add))
            link(v.tensor_tensor(flat[:, 1:2], flat[:, 3:4], flat[:, 2:3], op=ALU.mult))
            for i in range(2):
                link(v.scalar_tensor_tensor(out=den[:, i, 0:1], in0=key[:, i:i + 1], scalar=-float(SKIP), in1=flat[:, i:i + 1],
                                            op0=ALU.add, op1=ALU.mult))
                link(v.tensor_scalar(put[i][:, :], den[:, i, 0:1], float(SKIP), None, op0=ALU.add))
            link(v.tensor_scalar(edge0[:, :], k.trash[:, :], float(1 - N), float(T), op0=ALU.add, op1=ALU.mult))
            link(v.tensor_tensor(edge0[:, :], edge0[:, :], joint["head_len"][:, :], op=ALU.subtract))
            link(v.scalar_tensor_tensor(out=edge0[:, :], in0=edge0[:, :], scalar=-float(SKIP), in1=flat[:, 2:3],
                                        op0=ALU.add, op1=ALU.mult))
            link(v.tensor_scalar(h_put[:, :], edge0[:, :], float(SKIP), None, op0=ALU.add))
            v.wait_ge(summed, 1)
            v.wait_ge(gathered, 32)
            for i in range(2):
                got = ps_s[:, i * W:(i + 1) * W]
                link(v.tensor_scalar(den[:, i, :], got[:, D:W], 1e-16, None, op0=ALU.add))
                link(v.reciprocal(fac[:, i, :], den[:, i, :]))
                link(v.tensor_tensor(rows[i][:, 0:D].rearrange("p (h f) -> p h f", h=HEADS),
                                     got[:, 0:D].rearrange("p (h f) -> p h f", h=HEADS),
                                     fac[:, i, :].unsqueeze(2).to_broadcast([P, HEADS, CH]), op=ALU.mult))
                link(v.tensor_tensor(rows[i][:, 0:D], rows[i][:, 0:D], xrow[i][:, 0:D], op=ALU.add))
            norm_moments(v, lambda j: rows[j][:, 0:D], stats, small, normed_, 0, P, 2)
            link(v.scalar_tensor_tensor(out=small[:, 4, :], in0=small[:, 3, :], scalar=0.25, in1=small[:, 2, :],
                                        op0=ALU.mult, op1=ALU.add))
            v.sem_inc(stage, 1)
            v.wait_ge(acts, 1)
            link(v.reciprocal(small[:, 6, :], small[:, 5, :]))
            link(v.scalar_tensor_tensor(out=small[:, 7, :], in0=small[:, 0, :], scalar=-0.5, in1=small[:, 6, :],
                                        op0=ALU.mult, op1=ALU.mult))
            v.sem_inc(stage, 1)
            v.wait_ge(muls, 2)
            for i in range(2):
                link(v.tensor_copy(hT[i][:, :], ps_h[:, i * P:(i + 1) * P]))
            v.sem_inc(stage, 1)
            v.wait_ge(muls, 4)
            for i in range(2):
                link(v.tensor_tensor(rows[i][:, D:PAIR], ps_h[:, 256 + i * D:256 + (i + 1) * D], k.b1[:, :], op=ALU.add))
            v.sem_inc(ready, 1)

        @block.scalar
        def _(act):
            act.wait_ge(stage, 1)
            act.activation(fac[:, :, :], fac[:, :, :], ACT.Exp).then_inc(weighed, 1)
            act.wait_ge(stage, 3)
            act.activation(small[:, 5, :], small[:, 4, :], ACT.Sqrt, bias=k.eps[:, :]).then_inc(acts, 1)
            act.wait_ge(stage, 4)
            for i in range(2):
                act.activation(h[i][:, :], rows[i][:, 0:D], ACT.Relu, bias=small[:, 7, i:i + 1],
                               scale=small[:, 6, i:i + 1]).then_inc(h_kept, 1)

        @block.tensor
        def _(pe):
            pe.wait_ge(keyed, 1)
            for i in range(2):
                ins = pe.transpose(ps_k[:, i * P:(i + 1) * P], key[:, i:i + 1].to_broadcast([P, P]), k.ident[:, :])
            ins.then_inc(turned, 1)
            for hd in range(HEADS):
                for i in range(2):
                    ins = pe.transpose(ps_m[:, (2 * hd + i) * P:(2 * hd + i + 1) * P],
                                       part[i][:, D + hd:D + hd + 1].to_broadcast([P, P]), k.ident[:, :])
            ins.then_inc(peaks, 1)
            pe.wait_ge(masked, 1)
            pe.wait_ge(stage, 2)
            for i in range(2):
                for j in range(2):
                    ins = pe.matmul(ps_s[:, i * W:(i + 1) * W], same[j][:, i, :], scaled[:, j, :], start=(j == 0), stop=(j == 1))
            ins.then_inc(summed, 1)
            for i in range(2):
                pe.wait_ge(h_kept, 2)
                pe.transpose(ps_h[:, i * P:(i + 1) * P], h[i][:, :], k.ident[:, :]).then_inc(muls, 1)
            pe.wait_ge(stage, 5)
            for i in range(2):
                pe.matmul(ps_h[:, 256 + i * D:256 + (i + 1) * D], hT[i][:, :], k.w1_src[:, :], start=True, stop=True).then_inc(muls, 1)

        @block.gpsimd
        def _(pool):
            wait_apart(pool, k.pool_past, indexed, 1)
            for i in range(2):
                pool.indirect_dma_start(xrow[i][:, :], None, by_dst[:, :],
                                        bass.IndirectOffsetOnAxis(key_at[i][:, 0:1], 0)).then_inc(gathered, 16)
            wait_apart(pool, k.pool_past, ready, 1)
            for i in range(2):
                pool.indirect_dma_start(pairs[:, :], bass.IndirectOffsetOnAxis(put[i][:, 0:1], 0), rows[i][:, :], None,
                                        bounds_check=N - 1, oob_is_err=False).then_inc(out, 16)
            pool.indirect_dma_start(h_rev.rearrange("p t f -> (p t) f"), bass.IndirectOffsetOnAxis(h_put[:, 0:1], 0),
                                    h[1][:, :], None, bounds_check=P * T - 1, oob_is_err=False).then_inc(out, 16)
            wait_apart(pool, k.pool_past, out, 48)

        @block.sync
        def _(sp):
            wait_apart(sp, k.sp_past, h_kept, 2)
            sp.dma_start(h_rev[:, 0:1, :].rearrange("p one f -> p (one f)"), h[0][:, :]).then_inc(tails_out, 16)
            wait_apart(sp, k.sp_past, tails_out, 16)



def messages(nc, m, k, e, halves, h_rev, sums):
    HALF = EC // 2
    VG = 3
    vgroups = [(j, min(VG, EC - j)) for j in range(0, EC, VG)]
    NV = len(vgroups)
    h_in = [m.sb(f"me_h{i}", [P, EC, D]) for i in range(2)]
    prod = [m.sb(f"me_prod{i}", [P, EC, D]) for i in range(2)]
    out = [m.sb(f"me_out{i}", [P, EC, AGG]) for i in range(2)]
    at_in = [m.sb(f"me_at{i}", [P, EC], I32) for i in range(2)]
    at_out = [m.sb(f"me_to{i}", [P, EC], I32) for i in range(2)]
    keys = [m.sb(f"me_keys{i}", [P, EC]) for i in range(2)]
    ends = m.sb("me_ends", [P, D, SLOTS])
    keep = m.sb("me_keep", [P, D, SLOTS])
    xn = [m.sb(f"me_xn{i}", [P, D, SLOTS]) for i in range(2)]
    turned = [m.sb(f"me_turned{i}", [P, HALF, P]) for i in range(2)]
    same = m.sb("me_same", [P, EC, P])
    cnt = m.sb("me_cnt", [P, EC])
    once = m.sb("me_once", [P, EC])
    less = m.sb("me_less", [P, EC])
    to_f = m.sb("me_to_f", [P, EC])
    logit = m.sb("me_logit", [P, EC])
    msg = m.sb("me_msg", [P, EC, AGG])
    mask = m.sb("me_mask", [P, EC])
    ps_t = m.ps("me_ps_t", 2)
    ps_q = m.ps("me_ps_q", 2)
    ps_r = m.ps("me_ps_r", 2)
    ps_v = [m.ps(f"me_ps_v{i}") for i in range(2)]
    landed = m.sems("me_landed", 2)
    picked = m.sems("me_picked", 2)
    added = m.sems("me_added", 2)
    ready, set_up, ends_in, keep_in, scanned = (m.sem("me_indices"), m.sem("me_set_up"), m.sem("me_ends_in"),
                                                m.sem("me_keep_in"), m.sem("me_scanned"))
    turn_done, turn_kept, q_done, q_kept, r_done, r_kept = (m.sem("me_turn_done"), m.sem("me_turn_kept"), m.sem("me_q_done"),
                                                            m.sem("me_q_kept"), m.sem("me_r_done"), m.sem("me_r_kept"))
    step, dotted, masked, msg_done, to_done, v_done, v_kept, free = (
        m.sem("me_step"), m.sem("me_dotted"), m.sem("me_masked"), m.sem("me_msg_done"), m.sem("me_to_done"),
        m.sem("me_v_done"), m.sem("me_v_kept"), m.sem("me_out_free"))
    STEPS = 5
    PER = EC // 2

    with nc.Block() as block:
        @block.gpsimd
        def _(pool):
            def pick(c, b):
                wait_apart(pool, k.pool_past, ready, c + 1)
                for j in range(EC):
                    pool.indirect_dma_start(prod[b][:, j, :], None, halves[:, :],
                                            bass.IndirectOffsetOnAxis(at_in[b][:, j:j + 1], 0)).then_inc(picked[b], 16)

            def add(c, b):
                wait_apart(pool, k.pool_past, v_kept, NV * c + NV)
                wait_apart(pool, k.pool_past, to_done, c + 1)
                for j in range(EC):
                    wait_apart(pool, k.pool_past, added[j % 2], 16 * (PER * c + j // 2))
                    pool.indirect_dma_start(sums[j % 2][:, :], bass.IndirectOffsetOnAxis(at_out[b][:, j:j + 1], 0),
                                            out[b][:, j, :], None, compute_op=ALU.add).then_inc(added[j % 2], 16)

            pick(0, 0)
            pick(1, 1)
            add(0, 0)
            with pool.Fori(1, ECHUNKS // 2) as t:
                pick(2 * t, 0)
                add(2 * t - 1, 1)
                pick(2 * t + 1, 1)
                add(2 * t, 0)
            add(ECHUNKS - 1, 1)
            for b in range(2):
                wait_apart(pool, k.pool_past, added[b], 16 * PER * ECHUNKS)

        @block.sync
        def _(sp):
            def chunk(c, b, turn):
                wait_apart(sp, k.sp_past, ends_in, c - 1)
                sp.dma_start(h_in[b][:, :, :], h_rev[:, bass.ds(c * EC, EC), :]).then_inc(landed[b], 16)

            edge_chunks(sp, chunk)

        @block.vector
        def _(v):
            def indices(c, b):
                v.tensor_copy(keys[b][:, :], e.key_rev[:, bass.ds(c * EC, EC)])
                v.tensor_copy(at_in[b][:, :], e.pick_rev[:, bass.ds(c * EC, EC)]).then_inc(ready, 1)

            for b in range(2):
                indices(b, b)
            v.memset(keep[:, :, 0:1], 0.0)
            v.memset(xn[1][:, :, :], 0.0)
            v.memset(msg[:, :, D + 1:AGG], 1.0).then_inc(set_up, 1)
            v.wait_ge(set_up, 1)

            def chunk(c, b, turn):
                base = c * STEPS

                def at(n):
                    v.wait_ge(step, base + n)

                for half in range(2):
                    v.wait_ge(r_done, 2 * c + half + 1)
                    wait_past(v, v_done, NV * c)
                    for i in range(HALF):
                        j = half * HALF + i
                        ins = v.scalar_tensor_tensor(out=same[:, j, :], in0=ps_r[:, i * P:(i + 1) * P],
                                                     scalar=keys[b][:, j:j + 1], in1=k.upto[:, :],
                                                     op0=ALU.is_equal, op1=ALU.mult, accum_out=cnt[:, j:j + 1])
                    ins.then_inc(r_kept, 1)
                wait_past(v, scanned, c)
                v.wait_ge(ends_in, c + 1)
                v.tensor_copy(ends[:, :, 0:1], xn[1 - b][:, :, EC:SLOTS]).then_inc(step, 1)
                v.wait_ge(keep_in, c + 1)
                at(1)
                v.tensor_tensor_scan(xn[b][:, :, :].rearrange("p f j -> p (f j)"), keep[:, :, :].rearrange("p f j -> p (f j)"),
                                     ends[:, :, :].rearrange("p f j -> p (f j)"), 0.0, op0=ALU.mult,
                                     op1=ALU.add).then_inc(scanned, 1)
                v.tensor_scalar(once[:, :], cnt[:, :], 1.0, None, op0=ALU.is_equal)
                v.tensor_scalar(less[:, :], keys[b][:, :], k.trash[:, :], None, op0=ALU.subtract).then_inc(step, 1)
                at(2)
                v.tensor_tensor(to_f[:, :], once[:, :], less[:, :], op=ALU.mult).then_inc(step, 1)
                at(3)
                if not (isinstance(c, int) and c < 2):
                    for table in range(2):
                        v.wait_ge(added[table], 16 * PER * (c - 1))
                v.tensor_scalar(at_out[b][:, :], to_f[:, :], k.trash[:, :], None, op0=ALU.add).then_inc(to_done, 1)
                v.wait_ge(picked[b], 16 * EC * (turn + 1))
                z = prod[b]
                for half in range(2):
                    js = slice(half * HALF, half * HALF + HALF)
                    v.wait_ge(q_done, 2 * c + half + 1)
                    v.tensor_tensor(z[:, js, :], z[:, js, :], ps_q[:, 0:HALF * D].rearrange("p (j f) -> p j f", j=HALF),
                                    op=ALU.add).then_inc(q_kept, 1)
                    v.wait_ge(q_kept, 2 * c + half + 1)
                    v.scalar_tensor_tensor(out=z[:, js, :], in0=z[:, js, :], scalar=0.0,
                                           in1=k.w2[:, :].unsqueeze(1).to_broadcast([P, HALF, D]), op0=ALU.max,
                                           op1=ALU.mult).then_inc(step, 1)
                    at(4 + half)
                v.tensor_reduce(logit[:, :], z[:, :, :], AX.X, ALU.add).then_inc(dotted, 1)
                v.wait_ge(dotted, c + 1)
                indices(c + 2, b)
                v.wait_ge(masked, c + 1)
                wait_past(v, v_done, NV * c)
                v.tensor_copy(msg[:, :, D:D + 1], mask[:, :].unsqueeze(2))
                v.tensor_tensor(msg[:, :, 0:D], xn[b][:, :, 1:SLOTS].rearrange("p f j -> p j f"),
                                mask[:, :].unsqueeze(2).to_broadcast([P, EC, D]), op=ALU.mult).then_inc(msg_done, 1)

            edge_chunks(v, chunk)

        @block.scalar
        def _(act):
            def chunk(c, b, turn):
                act.wait_ge(landed[b], 16 * (turn + 1))
                wait_past(act, scanned, c)
                act.activation(ends[:, :, 1:SLOTS].rearrange("p f j -> p j f"), h_in[b][:, :, :], ACT.Copy).then_inc(ends_in, 1)
                act.activation(keep[:, :, 1:SLOTS], e.go_on_rev[:, bass.ds(c * EC, EC)].unsqueeze(1).to_broadcast([P, D, EC]),
                               ACT.Copy).then_inc(keep_in, 1)
                for half in range(2):
                    act.wait_ge(turn_done, 2 * c + half + 1)
                    wait_past(act, q_done, 2 * c + half - 1)
                    act.activation(turned[half][:, :, :], ps_t[:, 0:HALF * P].rearrange("p (j f) -> p j f", j=HALF),
                                   ACT.Copy).then_inc(turn_kept, 1)
                act.wait_ge(dotted, c + 1)
                wait_past(act, msg_done, c)
                act.activation(mask[:, :], logit[:, :], ACT.Sigmoid, bias=k.b2[:, :]).then_inc(masked, 1)
                if not (isinstance(c, int) and c < 2):
                    for table in range(2):
                        act.wait_ge(added[table], 16 * PER * (c - 1))
                for g, (j, n) in enumerate(vgroups):
                    q = NV * c + g
                    act.wait_ge(v_done, q + 1)
                    act.activation(out[b][:, j:j + n, :], ps_v[(NV * b + g) % 2][:, 0:n * AGG].rearrange("p (j f) -> p j f", j=n),
                                   ACT.Copy).then_inc(v_kept, 1)

            edge_chunks(act, chunk)

        @block.tensor
        def _(pe):
            def chunk(c, b, turn):
                pe.wait_ge(ready, c + 1)
                for half in range(2):
                    wait_past(pe, r_kept, 2 * c + half)
                    for i in range(HALF):
                        j = half * HALF + i
                        ins = pe.transpose(ps_r[:, i * P:(i + 1) * P], keys[b][:, j:j + 1].to_broadcast([P, P]), k.ident[:, :])
                    ins.then_inc(r_done, 1)
                pe.wait_ge(scanned, c + 1)
                for half in range(2):
                    wait_past(pe, turn_kept, 2 * c + half)
                    for i in range(HALF):
                        ins = pe.transpose(ps_t[:, i * P:(i + 1) * P], xn[b][:, :, 1 + half * HALF + i], k.ident[:, :])
                    ins.then_inc(turn_done, 1)
                    pe.wait_ge(turn_kept, 2 * c + half + 1)
                    wait_past(pe, q_kept, 2 * c + half)
                    for i in range(HALF):
                        ins = pe.matmul(ps_q[:, i * D:(i + 1) * D], turned[half][:, i, :], k.w1_dst[:, :], start=True, stop=True)
                    ins.then_inc(q_done, 1)
                pe.wait_ge(msg_done, c + 1)
                for g, (j, n) in enumerate(vgroups):
                    q = NV * c + g
                    wait_past(pe, v_kept, q - 1)
                    for i in range(n):
                        ins = pe.matmul(ps_v[(NV * b + g) % 2][:, i * AGG:(i + 1) * AGG], same[:, j + i, :], msg[:, j + i, :], start=True, stop=True)
                    ins.then_inc(v_done, 1)

            edge_chunks(pe, chunk)



def nodes_out(nc, m, k, pairs, sums, out):
    x1 = [m.sb(f"no_x{i}", [P, NC, D]) for i in range(NB)]
    sum_a = [m.sb(f"no_a{i}", [P, NC, AGG]) for i in range(NB)]
    sum_b = [m.sb(f"no_b{i}", [P, NC, AGG]) for i in range(NB)]
    normed = [m.sb(f"no_h{i}", [P, NC, D]) for i in range(NB)]
    emb = [m.sb(f"no_emb{i}", [P, NC, D]) for i in range(NB)]
    res = [m.sb(f"no_res{i}", [P, NC, D]) for i in range(NB)]
    turned = [m.sb(f"no_turned{i}", [P, 3, P]) for i in range(2)]
    stats = [m.sb(f"no_stats{i}", [P, NC, 6]) for i in range(NB)]
    small = [m.sb(f"no_small{i}", [P, 12, NC]) for i in range(NB)]
    ps_t = [m.ps(f"no_ps_t{i}") for i in range(2)]
    ps_y = [m.ps(f"no_ps_y{i}") for i in range(2)]
    landed = m.sems("no_landed", NB)
    stored = m.sems("no_stored", NB)
    moments, varied, rooted, scaled, biased, norm_done = (m.sem("no_moments"), m.sem("no_varied"), m.sem("no_rooted"),
                                                          m.sem("no_scaled"), m.sem("no_biased"), m.sem("no_norm_done"))
    step, emb_done, turn_done, turn_kept, mul_done, positive, res_done = (
        m.sem("no_step"), m.sem("no_emb_done"), m.sem("no_turn_done"), m.sem("no_turn_kept"), m.sem("no_mul_done"),
        m.sem("no_positive"), m.sem("no_res_done"))
    STEPS = 6

    def groups(ch):
        for g, (j, n) in enumerate(ch.groups):
            yield ch.c * ch.per + g, g % 2, j, n

    with nc.Block() as block:
        @block.sync
        def _(sp):
            def load(ch):
                wait_apart(sp, k.sp_past, res_done, (ch.c - (NB - 1)) * ch.per)
                for to, table, width in ((x1, pairs, D), (sum_a, sums[0], AGG), (sum_b, sums[1], AGG)):
                    sp.dma_start(to[ch.buf][0:ch.parts, 0:ch.tiles, :], ch.rows(table, slice(0, width))).then_inc(landed[ch.buf], 16)

            def store(ch):
                wait_apart(sp, k.sp_past, res_done, ch.c * ch.per + len(ch.groups))
                sp.dma_start(ch.rows(out, slice(0, D)), res[ch.buf][0:ch.parts, 0:ch.tiles, :]).then_inc(stored[ch.buf], 16)

            node_chunks(sp, load, store)
            for h in range(NB):
                wait_apart(sp, k.sp_past, stored[h], 16 * (TURNS + (h == 0)))

        @block.vector
        def _(v):
            def norm(ch):
                p, n, s, a = ch.parts, ch.tiles, small[ch.buf], sum_a[ch.buf]
                base = ch.c * STEPS
                v.wait_ge(landed[ch.buf], 48 * (ch.turn + 1))
                norm_moments(v, lambda j: x1[ch.buf][0:p, j, :], stats[ch.buf], s, moments, NORM_STEPS * ch.c, p, n)
                v.scalar_tensor_tensor(out=s[0:p, 4, 0:n], in0=s[0:p, 3, 0:n], scalar=0.25, in1=s[0:p, 2, 0:n],
                                       op0=ALU.mult, op1=ALU.add).then_inc(varied, 1)
                v.tensor_tensor(a[0:p, 0:n, :], a[0:p, 0:n, :], sum_b[ch.buf][0:p, 0:n, :], op=ALU.add).then_inc(step, 1)
                v.wait_ge(step, base + 1)
                v.tensor_scalar(s[0:p, 10, 0:n], a[0:p, 0:n, D], 1e-9, None, op0=ALU.add)
                v.tensor_scalar(s[0:p, 11, 0:n], a[0:p, 0:n, D + 1], 1.0, -0.5, op0=ALU.min, op1=ALU.mult).then_inc(step, 1)
                v.wait_ge(step, base + 2)
                v.reciprocal(s[0:p, 8, 0:n], s[0:p, 10, 0:n])
                v.tensor_scalar(s[0:p, 9, 0:n], s[0:p, 11, 0:n], 1.0, None, op0=ALU.add).then_inc(step, 1)
                v.wait_ge(step, base + 3)
                v.tensor_scalar(s[0:p, 10, 0:n], s[0:p, 8, 0:n], 0.5, None, op0=ALU.mult)
                v.wait_ge(rooted, ch.c + 1)
                wait_past(v, norm_done, ch.c - (NB - 1))
                v.reciprocal(s[0:p, 3, 0:n], s[0:p, 5, 0:n]).then_inc(step, 1)
                v.wait_ge(step, base + 4)
                v.tensor_tensor(s[0:p, 6, 0:n], s[0:p, 3, 0:n], s[0:p, 9, 0:n], op=ALU.mult).then_inc(scaled, 1)
                v.wait_ge(scaled, ch.c + 1)
                v.scalar_tensor_tensor(out=s[0:p, 7, 0:n], in0=s[0:p, 0, 0:n], scalar=-0.5, in1=s[0:p, 6, 0:n],
                                       op0=ALU.mult, op1=ALU.mult).then_inc(biased, 1)
                wait_past(v, turn_done, (ch.c - (NB - 1)) * ch.per)
                v.tensor_tensor(emb[ch.buf][0:p, 0:n, :], a[0:p, 0:n, 0:D],
                                s[0:p, 10, 0:n].unsqueeze(2).to_broadcast([p, n, D]), op=ALU.mult).then_inc(step, 1)
                v.wait_ge(norm_done, ch.c + 1)
                v.wait_ge(step, base + 5)
                v.tensor_tensor(emb[ch.buf][0:p, 0:n, :], emb[ch.buf][0:p, 0:n, :], normed[ch.buf][0:p, 0:n, :],
                                op=ALU.add).then_inc(emb_done, 1)
                v.sem_inc(step, 1)

            def finish(ch):
                p = ch.parts
                wait_past(v, stored[ch.buf], 16 * ch.turn)
                for q, b, j, n in groups(ch):
                    r = res[ch.buf][0:p, j:j + n, :]
                    v.wait_ge(mul_done, q + 1)
                    v.scalar_tensor_tensor(out=r, in0=ps_y[b][0:p, 0:n * D].rearrange("p (j f) -> p j f", j=n), scalar=0.0,
                                           in1=x1[ch.buf][0:p, j:j + n, :], op0=ALU.max, op1=ALU.add).then_inc(res_done, 1)

            node_chunks(v, norm, finish)

        @block.scalar
        def _(act):
            def norm(ch):
                p, n, s = ch.parts, ch.tiles, small[ch.buf]
                act.wait_ge(varied, ch.c + 1)
                act.activation(s[0:p, 5, 0:n], s[0:p, 4, 0:n], ACT.Sqrt, bias=k.eps[0:p, :]).then_inc(rooted, 1)
                act.wait_ge(biased, ch.c + 1)
                wait_past(act, emb_done, ch.c - (NB - 1))
                for j in range(n):
                    ins = act.activation(normed[ch.buf][0:p, j, :], x1[ch.buf][0:p, j, :], ACT.Relu,
                                         bias=s[0:p, 7, j:j + 1], scale=s[0:p, 6, j:j + 1])
                ins.then_inc(norm_done, 1)

            def turn(ch):
                p = ch.parts
                for q, b, j, n in groups(ch):
                    act.wait_ge(turn_done, q + 1)
                    wait_past(act, mul_done, q - 1)
                    act.activation(turned[b][:, 0:n, 0:p], ps_t[b][:, 0:n * P].rearrange("p (j f) -> p j f", j=n)[:, :, 0:p],
                                   ACT.Copy).then_inc(turn_kept, 1)

            node_chunks(act, norm, turn)

        @block.tensor
        def _(pe):
            def nothing(ch):
                pass

            def multiply(ch, q, b, j, n):
                p = ch.parts
                pe.wait_ge(turn_kept, q + 1)
                wait_past(pe, res_done, q - 1)
                for i in range(n):
                    y = ps_y[b][0:p, i * D:(i + 1) * D]
                    pe.matmul(y, turned[b][:, i, 0:p], k.wl[:, :], start=True, stop=False)
                    ins = pe.matmul(y, k.ones[0:1, 0:p], k.bl[0:1, :], start=False, stop=True)
                ins.then_inc(mul_done, 1)

            def chunk(ch):
                p, late = ch.parts, None
                pe.wait_ge(emb_done, ch.c + 1)
                for q, b, j, n in groups(ch):
                    wait_past(pe, turn_kept, q - 1)
                    for i in range(n):
                        ins = pe.transpose(ps_t[b][:, i * P:i * P + p], emb[ch.buf][0:p, j + i, :], k.ident[0:p, 0:p])
                    ins.then_inc(turn_done, 1)
                    if late:
                        multiply(*late)
                    late = (ch, q, b, j, n)
                multiply(*late)

            node_chunks(pe, nothing, chunk)


def program(nc, x, src, dst, coeffs, lin_weight, lin_bias, att_src, att_dst, w1, b1, w2, b2, wl, bl, out):
    def scratch(name, shape, dt=F32):
        return nc.dram_tensor(name, shape, dt, kind="Internal").ap()

    by_src = scratch("by_src", [N, XT])
    by_dst = scratch("by_dst", [N, XD])
    pairs = scratch("node_pairs", [N, PAIR])
    h_rev = scratch("h_rev", [P, T, D])
    sums = [scratch(f"sums{i}", [P * T, AGG]) for i in range(2)]
    by_low, by_key = (scratch(name, [P * T, 2], I32) for name in ("edges_by_low", "edges_by_dst"))

    with ExitStack() as outer:
        shared = Mem(nc, outer)
        k = Const(shared)
        e = Edges(shared)
        flag = shared.sb("unsorted", [1, 1], I32)
        joint = {"head": shared.sb("head_state", [P, D + 2 * HEADS]), "tail": shared.sb("tail_state", [P, D + 2 * HEADS]),
                 "head_len": shared.sb("head_len", [P, 1])}

        def run(part, *args):
            with ExitStack() as ctx:
                part(nc, Mem(nc, ctx), k, *args)

        run(constants, coeffs, lin_weight, lin_bias, att_src, att_dst, w1, b1, w2, b2, wl, bl)
        run(edges_in, e, src, dst, flag)
        run(edges_sorted, e, flag, by_low, by_key)
        run(edge_marks, e, joint)
        run(nodes_in, x, by_src, by_dst, pairs)
        run(attention, e, by_src, by_dst, pairs, h_rev, sums, joint)
        run(joints, e, by_dst, pairs, h_rev, joint)
        run(messages, e, pairs.rearrange("n (two f) -> (n two) f", two=2), h_rev, sums)
        run(nodes_out, pairs, sums, out)


_INS = ['x', 'src', 'dst', 'L0_gnn_coeffs_t', 'L0_gnn_lin_weight', 'L0_gnn_lin_bias', 'L0_gnn_att_src', 'L0_gnn_att_dst',
        'L1_gnn_W1', 'L1_gnn_b1', 'L1_gnn_W2', 'L1_gnn_b2', 'L1_gnn_Wl', 'L1_gnn_bl']


def kernel(**inputs):
    import numpy as _np
    import concourse.bacc as _bacc
    from concourse import mybir as _mybir
    from concourse.bass_utils import run_bass_kernel_spmd as _run

    nc = _bacc.Bacc("TRN2", target_bir_lowering=False, num_devices=1)
    arrays, args = {}, []
    for name in _INS:
        a = _np.ascontiguousarray(inputs[name])
        arrays[f"in_{name}_dram"] = a
        args.append(nc.dram_tensor(f"in_{name}_dram", a.shape, _mybir.dt.from_np(a.dtype), kind="ExternalInput").ap())
    out = nc.dram_tensor("out_0_dram", (N, D), _mybir.dt.float32, kind="ExternalOutput").ap()
    program(nc, *args, out)
    r = _run(nc, [arrays], core_ids=[0])
    return r.results[0]["out_0_dram"]
```

```python
import concourse.bass as bass
from concourse import mybir
from contextlib import ExitStack

F32 = mybir.dt.float32
I32 = mybir.dt.int32
ALU = mybir.AluOpType
ACT = mybir.ActivationFunctionType
AX = mybir.AxisListType

P = 128
N = 50000
E = 50000
D = 128
HEADS = 4
CH = D // HEADS
SLICES = 3
EPS = 1e-5
SLOPE = 0.2
BIG = 1e38

EC = 14
T = 2 * EC * -(-E // (P * 2 * EC))
ECHUNKS = T // EC
SLOTS = EC + 1
PAD_DST = P * T - 1
SKIP = 1 << 17
LAST_FULL = (P - 1) * T
REST = E - LAST_FULL

NC = 10
NB = 5
NCHUNKS = N // (P * NC)
TAIL = N - NCHUNKS * P * NC
NGROUP = 3
NGROUPS = -(-NC // NGROUP)
assert ECHUNKS % 2 == 0 and NGROUPS % 2 == 0

XT = D + HEADS
XD = D + HEADS
PAIR = 2 * D
AGG = D + 2
RADIX = max(P, T)


def wait_past(eng, sem, value):
    if isinstance(value, int) and value <= 0:
        return
    eng.wait_ge(sem, value)


def wait_apart(eng, past, sem, value):
    wait_past(eng, sem, value)
    if not isinstance(value, int):
        eng.sem_inc(past, 1)


class Chunk:

    def __init__(self, c, buf, turn, parts=P, tiles=NC):
        self.c, self.buf, self.turn, self.parts, self.tiles = c, buf, turn, parts, tiles

    def rows(self, table, cols):
        if self.parts == P:
            part = table[bass.ds(self.c * (P * NC), P * NC), cols]
        else:
            part = table[NCHUNKS * P * NC:N, cols]
        return part.rearrange("(p j) f -> p j f", p=self.parts)

    def group(self, g):
        return self.c * NGROUPS + g, g % 2, g * NGROUP, min(NGROUP, self.tiles - g * NGROUP)

    def groups(self):
        return -(-self.tiles // NGROUP)


def groups_of(*chunks):
    return range(max(ch.groups() if ch else 0 for ch in chunks))


def uses(buf):
    return len(range(buf, NCHUNKS + 1, NB))


def node_chunks(eng, body, lead):
    def at(c):
        if 0 <= c < NCHUNKS:
            return Chunk(c, c % NB, c // NB)
        return Chunk(c, c % NB, c // NB, parts=TAIL, tiles=1) if c == NCHUNKS else None

    turns = (NCHUNKS - lead) // NB
    for c in range(-lead, NB):
        body(*(at(c + i) for i in range(lead + 1)))
    with eng.Fori(1, turns) as k:
        for h in range(NB):
            body(*(Chunk(NB * k + (h + i), (h + i) % NB, k + (h + i) // NB) for i in range(lead + 1)))
    for c in range(NB * turns, NCHUNKS + 1):
        body(*(at(c + i) for i in range(lead + 1)))


def edge_chunks(eng, body):
    body(0, 0, 0)
    body(1, 1, 0)
    with eng.Fori(1, ECHUNKS // 2) as k:
        body(2 * k, 0, k)
        body(2 * k + 1, 1, k)


class Mem:

    def __init__(self, nc, ctx):
        self.nc, self.ctx = nc, ctx

    def sb(self, name, shape, dt=F32):
        return self.ctx.enter_context(self.nc.sbuf_tensor(name, shape, dt))

    def ps(self, name, banks=1):
        return self.ctx.enter_context(self.nc.psum_tensor(name, [P, 512 * banks], F32))

    def sem(self, name):
        return self.ctx.enter_context(self.nc.semaphore(name))

    def sems(self, name, n):
        return [self.sem(f"{name}{i}") for i in range(n)]


class Const:

    def __init__(self, m):
        self.ident = m.sb("ident", [P, P])
        self.ones = m.sb("ones", [P, P])
        self.before = m.sb("before", [P, P])
        self.upto = m.sb("upto", [P, P])
        self.proj = m.sb("proj", [P, D + 2 * HEADS])
        self.proj_bias = m.sb("proj_bias", [P, D + 2 * HEADS])
        self.w1_src = m.sb("w1_src", [P, D])
        self.w1_dst = m.sb("w1_dst", [P, D])
        self.b1 = m.sb("b1", [P, D])
        self.w2 = m.sb("w2", [P, D])
        self.b2 = m.sb("b2", [P, 1])
        self.wl = m.sb("wl", [P, D])
        self.bl = m.sb("bl", [P, D])
        self.eps = m.sb("eps", [P, 1])
        self.pool_past = m.sem("pool_past")
        self.sp_past = m.sem("sp_past")
        self.trash = m.sb("trash", [P, 1])


class Edges:

    def __init__(self, m):
        self.src = m.sb("e_src", [P, T + 2 * EC], I32)
        self.dst = m.sb("e_dst", [P, T], I32)
        self.dst_pick = m.sb("e_dst_pick", [P, T + 2 * EC], I32)
        self.put = m.sb("e_put", [P, T], I32)
        self.dst_f = m.sb("e_dst_f", [P, T])
        self.reset = m.sb("e_reset", [P, T])
        self.last = m.sb("e_last", [P, T])
        self.head_end = m.sb("e_head_end", [P, T])
        self.go_on_rev = m.sb("e_go_on_rev", [P, T])
        self.key_rev = m.sb("e_key_rev", [P, T + 2 * EC])
        self.pick_rev = m.sb("e_pick_rev", [P, T + 2 * EC], I32)



def constants(nc, m, k, coeffs, lin_weight, lin_bias, att_src, att_dst, w1, b1, w2, b2, wl, bl):
    w_all = m.sb("w_all", [P, SLICES, D])
    col_all = m.sb("col_all", [P, 3, SLICES])
    mix = m.sb("mix", [P, SLICES])
    w_mix = m.sb("w_mix", [P, D])
    cols = m.sb("cols", [P, 3])
    eye_att = m.sb("eye_att", [P, D + 2 * HEADS])
    bias_wide = m.sb("bias_wide", [P, P])
    ps_w = m.ps("ps_w")
    ps_b = m.ps("ps_b")
    loaded, filled, drawn, mixed, spread, folded, kept = (
        m.sem("const_loaded"), m.sem("const_filled"), m.sem("const_drawn"), m.sem("const_mixed"),
        m.sem("const_spread"), m.sem("const_folded"), m.sem("const_kept"))

    with nc.Block() as block:
        @block.sync
        def _(sp):
            loads = [
                (w_all[:, :, :], lin_weight.rearrange("b o i -> o b i")),
                (col_all[:, 0, :], lin_bias.rearrange("b o -> o b")),
                (col_all[:, 1, :], att_src.rearrange("b q h c -> (q h c) b")),
                (col_all[:, 2, :], att_dst.rearrange("b q h c -> (q h c) b")),
                (mix[:, :], coeffs.unsqueeze(0).to_broadcast([P, SLICES])),
                (k.w1_src[:, :], w1[0:D, :]),
                (k.w1_dst[:, :], w1[D:2 * D, :]),
                (k.b1[:, :], b1.unsqueeze(0).to_broadcast([P, D])),
                (k.w2[:, :], w2.rearrange("d one -> one d").to_broadcast([P, D])),
                (k.b2[:, :], b2.unsqueeze(0).to_broadcast([P, 1])),
                (k.wl[:, :], wl[:, :]),
                (k.bl[:, :], bl.unsqueeze(0).to_broadcast([P, D])),
            ]
            with nc.allow_non_contiguous_dma(reason="small weights, once"):
                for to, of in loads:
                    sp.dma_start(to, of).then_inc(loaded, 16)
            wait_apart(sp, k.sp_past, loaded, 16 * len(loads))
            sp.sem_inc(kept, 1)

        @block.gpsimd
        def _(pool):
            wait_apart(pool, k.pool_past, filled, 1)
            nc.gpsimd.affine_select(out=k.ident[:, :], in_=k.ones[:, :], pattern=[[-1, P]], compare_op=ALU.is_equal,
                                    fill=0.0, base=0, channel_multiplier=1).then_inc(drawn, 1)
            nc.gpsimd.affine_select(out=k.before[:, :], in_=k.ones[:, :], pattern=[[1, P]], compare_op=ALU.is_gt,
                                    fill=0.0, base=0, channel_multiplier=-1).then_inc(drawn, 1)
            nc.gpsimd.affine_select(out=k.upto[:, :], in_=k.ones[:, :], pattern=[[-1, P]], compare_op=ALU.is_ge,
                                    fill=0.0, base=0, channel_multiplier=1).then_inc(drawn, 1)
            nc.gpsimd.iota(k.trash[:, :], pattern=[[0, 1]], base=N, channel_multiplier=1,
                           allow_small_or_imprecise_dtypes=True).then_inc(drawn, 1)
            wait_apart(pool, k.pool_past, drawn, 4)

        @block.vector
        def _(v):
            v.memset(k.ones[:, :], 1.0).then_inc(filled, 1)
            v.memset(k.eps[:, :], EPS)
            v.memset(eye_att[:, :], 0.0).then_inc(spread, 1)
            v.wait_ge(kept, 1)
            v.tensor_scalar(w_mix[:, :], w_all[:, 0, :], mix[:, 0:1], None, op0=ALU.mult).then_inc(mixed, 1)
            v.tensor_scalar(cols[:, :], col_all[:, :, 0], mix[:, 0:1], None, op0=ALU.mult).then_inc(mixed, 1)
            for b in range(1, SLICES):
                v.wait_ge(mixed, 2 * b)
                v.scalar_tensor_tensor(out=w_mix[:, :], in0=w_all[:, b, :], scalar=mix[:, b:b + 1], in1=w_mix[:, :],
                                       op0=ALU.mult, op1=ALU.add).then_inc(mixed, 1)
                v.scalar_tensor_tensor(out=cols[:, :], in0=col_all[:, :, b], scalar=mix[:, b:b + 1], in1=cols[:, :],
                                       op0=ALU.mult, op1=ALU.add).then_inc(mixed, 1)
            v.wait_ge(mixed, 2 * SLICES)
            v.wait_ge(spread, 1)
            v.wait_ge(drawn, 1)
            for h in range(HEADS):
                rows = slice(CH * h, CH * h + CH)
                v.tensor_copy(eye_att[rows, D + h:D + h + 1], cols[rows, 1:2])
                v.tensor_copy(eye_att[rows, D + HEADS + h:D + HEADS + h + 1], cols[rows, 2:3])
            v.tensor_copy(eye_att[:, 0:D], k.ident[:, :])
            v.tensor_scalar(bias_wide[:, :], k.ones[:, :], cols[:, 0:1], None, op0=ALU.mult).then_inc(spread, 1)
            v.wait_ge(folded, 2)
            v.tensor_copy(k.proj[:, :], ps_w[:, 0:D + 2 * HEADS])
            v.tensor_copy(k.proj_bias[:, :], ps_b[:, 0:D + 2 * HEADS]).then_inc(kept, 1)
            v.wait_ge(kept, 2)

        @block.tensor
        def _(pe):
            pe.wait_ge(spread, 2)
            pe.matmul(ps_w[:, 0:D + 2 * HEADS], w_mix[:, :], eye_att[:, :], start=True, stop=True).then_inc(folded, 1)
            pe.matmul(ps_b[:, 0:D + 2 * HEADS], bias_wide[:, :], eye_att[:, :], start=True, stop=True).then_inc(folded, 1)



def edges_in(nc, m, k, e, src, dst, flag):
    prev = m.sb("prev", [P, T], I32)
    prev_f = m.sb("prev_f", [P, T])
    falls = m.sb("falls", [P, T])
    fall = m.sb("fall", [P, 1])
    ps_f = m.ps("ps_fall")
    blank, loaded, step, counted = m.sem("edges_blank"), m.sem("edges_loaded"), m.sem("falls_step"), m.sem("falls_counted")

    with nc.Block() as block:
        @block.sync
        def _(sp):
            wait_apart(sp, k.sp_past, blank, 1)
            loads = [
                (e.src[0:P - 1, 0:T], src[0:LAST_FULL].rearrange("(p t) -> p t", t=T)),
                (e.src[P - 1:P, 0:REST], src[LAST_FULL:E].unsqueeze(0)),
                (e.dst[0:P - 1, :], dst[0:LAST_FULL].rearrange("(p t) -> p t", t=T)),
                (e.dst[P - 1:P, 0:REST], dst[LAST_FULL:E].unsqueeze(0)),
                (prev[0:1, 1:T], dst[0:T - 1].unsqueeze(0)),
                (prev[1:P - 1, :], dst[T - 1:LAST_FULL - 1].rearrange("(p t) -> p t", t=T)),
                (prev[P - 1:P, 0:REST + 1], dst[LAST_FULL - 1:E].unsqueeze(0)),
            ]
            for to, of in loads:
                sp.dma_start(to, of).then_inc(loaded, 16)
            wait_apart(sp, k.sp_past, loaded, 16 * len(loads))

        @block.vector
        def _(v):
            v.memset(e.src[:, :], 0)
            v.memset(e.dst[:, :], PAD_DST)
            v.memset(prev[:, :], 0).then_inc(blank, 1)
            v.wait_ge(loaded, 16 * 7)
            v.tensor_copy(e.dst_f[:, :], e.dst[:, :])
            v.tensor_copy(prev_f[:, :], prev[:, :]).then_inc(step, 1)
            v.wait_ge(step, 1)
            v.tensor_tensor(falls[:, :], prev_f[:, :], e.dst_f[:, :], op=ALU.is_gt).then_inc(step, 1)
            v.wait_ge(step, 2)
            v.tensor_reduce(fall[:, :], falls[:, :], AX.X, ALU.max).then_inc(step, 1)
            v.wait_ge(counted, 1)
            v.tensor_copy(flag[:, :], ps_f[0:1, 0:1]).then_inc(step, 1)
            v.wait_ge(step, 4)

        @block.tensor
        def _(pe):
            pe.wait_ge(step, 3)
            pe.matmul(ps_f[0:1, 0:1], fall[:, :], k.ones[:, 0:1], start=True, stop=True).then_inc(counted, 1)


def edges_sorted(nc, m, k, e, flag, by_low, by_dst):
    pairs = m.sb("pairs", [P, T, 2], I32)
    bucket_i = m.sb("bucket_i", [P, T], I32)
    bucket = m.sb("bucket", [P, T])
    number_i = m.sb("number_i", [P, RADIX], I32)
    number = m.sb("number", [P, RADIX])
    count = m.sb("count", [P, RADIX])
    ends = m.sb("ends", [P, RADIX])
    place = m.sb("place", [P, RADIX])
    scrap = m.sb("scrap", [P, RADIX])
    at = m.sb("at", [P, 1])
    at_i = m.sb("at_i", [P, 1], I32)
    pair = m.sb("pair", [P, 2], I32)
    ps_c = m.ps("ps_count")
    ps_e = m.ps("ps_before")
    numbered, ready, counted, summed, sent, back = (m.sem("sort_numbered"), m.sem("sort_ready"), m.sem("sort_counted"),
                                                    m.sem("sort_summed"), m.sem("sort_sent"), m.sem("sort_back"))
    step, taken, placed = m.sem("sort_step"), m.sem("sort_taken"), m.sem("sort_placed")
    passes = [(0, P, by_low), (1, T, by_dst)]

    with nc.Block() as block:
        @block.gpsimd
        def _(pool):
            nc.gpsimd.iota(number_i[:, :], pattern=[[1, RADIX]], base=0, channel_multiplier=0).then_inc(numbered, 1)
            with pool.If(pool.value_load(flag[0:1, 0:1], min_val=0, max_val=P) != 0):
                for n, radix, table in passes:
                    with pool.Fori(0, T) as t:
                        wait_apart(pool, k.pool_past, ready, n * T + t + 1)
                        pool.indirect_dma_start(table[:, :], bass.IndirectOffsetOnAxis(at_i[:, 0:1], 0), pair[:, :],
                                                None).then_inc(sent, 16)
                        wait_apart(pool, k.pool_past, sent, 16 * (n * T + t + 1))
                        pool.sem_inc(taken, 1)

        @block.sync
        def _(sp):
            with sp.If(sp.value_load(flag[0:1, 0:1], min_val=0, max_val=P) != 0):
                for n, radix, table in passes:
                    wait_apart(sp, k.sp_past, taken, (n + 1) * T)
                    sp.dma_start(pairs[:, :, :], table.rearrange("(p t) two -> p t two", t=T)).then_inc(back, 16)
                    wait_apart(sp, k.sp_past, back, 16 * (n + 1))

        @block.tensor
        def _(pe):
            with pe.If(pe.value_load(flag[0:1, 0:1], min_val=0, max_val=P) != 0):
                for n, radix, table in passes:
                    pe.wait_ge(counted, n + 1)
                    pe.matmul(ps_c[:, 0:radix], k.ones[:, :], count[:, 0:radix], start=True, stop=True)
                    pe.matmul(ps_e[:, 0:radix], k.before[:, :], count[:, 0:radix], start=True,
                              stop=True).then_inc(summed, 1)

        @block.vector
        def _(v):
            with v.If(v.value_load(flag[0:1, 0:1], min_val=0, max_val=P) != 0):
                done = [0]

                def link(ins):
                    done[0] += 1
                    ins.then_inc(step, 1)
                    v.wait_ge(step, done[0])

                v.tensor_copy(pairs[:, :, 0], e.src[:, 0:T])
                link(v.tensor_copy(pairs[:, :, 1], e.dst[:, :]))
                v.wait_ge(numbered, 1)
                link(v.tensor_copy(number[:, :], number_i[:, :]))
                for n, radix, table in passes:
                    if n:
                        v.wait_ge(back, 16 * n)
                        link(v.tensor_single_scalar(bucket_i[:, :], pairs[:, :, 1], 7, op=ALU.logical_shift_right))
                    else:
                        link(v.tensor_single_scalar(bucket_i[:, :], pairs[:, :, 1], P - 1, op=ALU.bitwise_and))
                    link(v.tensor_copy(bucket[:, :], bucket_i[:, :]))
                    link(v.memset(count[:, 0:radix], 0.0))
                    base = done[0]
                    with v.Fori(0, T) as t:
                        v.scalar_tensor_tensor(out=count[:, 0:radix], in0=number[:, 0:radix],
                                               scalar=bucket[:, bass.ds(t, 1)], in1=count[:, 0:radix],
                                               op0=ALU.is_equal, op1=ALU.add).then_inc(step, 1)
                        v.wait_ge(step, t + (base + 1))
                    done[0] += T
                    v.sem_inc(counted, 1)
                    v.wait_ge(summed, n + 1)
                    link(v.tensor_copy(scrap[:, 0:radix], ps_c[:, 0:radix]))
                    link(v.tensor_tensor_scan(ends[:, 0:radix], k_ones(k, radix), scrap[:, 0:radix], 0.0,
                                              op0=ALU.mult, op1=ALU.add))
                    link(v.tensor_tensor(ends[:, 0:radix], ends[:, 0:radix], scrap[:, 0:radix], op=ALU.subtract))
                    link(v.tensor_tensor(place[:, 0:radix], ends[:, 0:radix], ps_e[:, 0:radix], op=ALU.add))
                    base = done[0]
                    with v.Fori(0, T) as t:
                        v.scalar_tensor_tensor(out=scrap[:, 0:radix], in0=number[:, 0:radix],
                                               scalar=bucket[:, bass.ds(t, 1)], in1=place[:, 0:radix],
                                               op0=ALU.is_equal, op1=ALU.mult, accum_out=at[:, :]).then_inc(step, 1)
                        v.scalar_tensor_tensor(out=place[:, 0:radix], in0=number[:, 0:radix],
                                               scalar=bucket[:, bass.ds(t, 1)], in1=place[:, 0:radix],
                                               op0=ALU.is_equal, op1=ALU.add).then_inc(step, 1)
                        v.wait_ge(step, 2 * t + (base + 2))
                        v.tensor_copy(at_i[:, :], at[:, :])
                        v.tensor_copy(pair[:, :], pairs[:, bass.ds(t, 1), :].rearrange("p one two -> p (one two)")).then_inc(ready, 1)
                        v.wait_ge(taken, n * T + t + 1)
                    done[0] += 2 * T
                v.wait_ge(back, 16 * len(passes))
                v.tensor_copy(e.src[:, 0:T], pairs[:, :, 0])
                v.tensor_copy(e.dst[:, :], pairs[:, :, 1]).then_inc(placed, 1)
                v.wait_ge(placed, 1)


def k_ones(k, n):
    return k.ones[:, 0:1].to_broadcast([P, n])


def edge_marks(nc, m, k, e, joint):
    src_f = m.sb("src_f", [P, T])
    first = m.sb("first", [P, T])
    in_head = m.sb("in_head", [P, T])
    in_tail = m.sb("in_tail", [P, T])
    work = m.sb("work", [P, T])
    step = m.sem("marks_step")

    with nc.Block() as block:
        @block.vector
        def _(v):
            done = [0]

            def link(ins):
                done[0] += 1
                ins.then_inc(step, 1)
                v.wait_ge(step, done[0])

            v.memset(first[:, 0:1], 1.0)
            v.memset(e.last[:, T - 1:T], 1.0)
            v.memset(e.dst_pick[:, T:], 0)
            v.memset(e.pick_rev[:, T:], 0)
            v.memset(e.key_rev[:, T:], 0.0)
            v.tensor_copy(src_f[:, :], e.src[:, 0:T])
            link(v.tensor_copy(e.dst_f[:, :], e.dst[:, :]))
            v.tensor_tensor(first[:, 1:T], e.dst_f[:, 1:T], e.dst_f[:, 0:T - 1], op=ALU.not_equal)
            v.tensor_tensor(e.last[:, 0:T - 1], e.dst_f[:, 1:T], e.dst_f[:, 0:T - 1], op=ALU.not_equal)
            v.tensor_scalar(in_head[:, :], e.dst_f[:, :], e.dst_f[:, 0:1], None, op0=ALU.is_equal)
            v.tensor_scalar(in_tail[:, :], e.dst_f[:, :], e.dst_f[:, T - 1:T], None, op0=ALU.is_equal)
            link(v.tensor_scalar(e.dst_pick[:, 0:T], e.dst_f[:, :], float(N - 1), None, op0=ALU.min))
            v.tensor_scalar(e.reset[:, :], first[:, :], -BIG, None, op0=ALU.mult)
            v.tensor_scalar(e.go_on_rev[:, ::-1], e.last[:, :], -1.0, 1.0, op0=ALU.mult, op1=ALU.add)
            v.tensor_reduce(joint["head_len"][:, :], in_head[:, :], AX.X, ALU.add)
            v.tensor_scalar(work[:, :], in_tail[:, :], -1.0, 1.0, op0=ALU.mult, op1=ALU.add).then_inc(step, 1)
            done[0] += 1
            v.wait_ge(step, done[0])
            link(v.tensor_tensor(work[:, :], work[:, :], e.last[:, :], op=ALU.mult))
            link(v.tensor_tensor(e.head_end[:, :], work[:, :], in_head[:, :], op=ALU.mult))
            link(v.tensor_tensor(work[:, :], work[:, :], e.head_end[:, :], op=ALU.subtract))
            link(v.scalar_tensor_tensor(out=work[:, :], in0=e.dst_f[:, :], scalar=-float(SKIP), in1=work[:, :],
                                        op0=ALU.add, op1=ALU.mult))
            v.tensor_scalar(e.put[:, :], work[:, :], float(SKIP), None, op0=ALU.add)
            link(v.tensor_scalar(first[:, :], e.dst_f[:, :], float(N), float(N + P - 1), op0=ALU.is_ge, op1=ALU.mult))
            v.tensor_tensor(e.key_rev[:, 0:T][:, ::-1], first[:, :], src_f[:, :], op=ALU.max)
            link(v.tensor_scalar(e.pick_rev[:, 0:T][:, ::-1], src_f[:, :], 2.0, 1.0, op0=ALU.mult, op1=ALU.add))



def norm_stats(v, x, stats, parts, tiles):
    for j in tiles:
        ins = v.bn_stats(stats[0:parts, j, :], x(j))
    return ins


def norm_moments(v, stats, small, step, at, parts, tiles):
    st = stats[0:parts, 0:tiles, :]
    v.wait_ge(step, at + 1)
    v.tensor_tensor(small[0:parts, 0, 0:tiles], st[:, :, 1], st[:, :, 4], op=ALU.add)
    v.tensor_tensor(small[0:parts, 1, 0:tiles], st[:, :, 1], st[:, :, 4], op=ALU.subtract)
    v.tensor_tensor(small[0:parts, 2, 0:tiles], st[:, :, 2], st[:, :, 5], op=ALU.add).then_inc(step, 1)
    v.wait_ge(step, at + 2)
    v.tensor_tensor(small[0:parts, 3, 0:tiles], small[0:parts, 1, 0:tiles], small[0:parts, 1, 0:tiles], op=ALU.mult)
    v.tensor_scalar(small[0:parts, 2, 0:tiles], small[0:parts, 2, 0:tiles], 1.0 / D, None, op0=ALU.mult).then_inc(step, 1)
    v.wait_ge(step, at + 3)


NORM_STEPS = 3



def nodes_in(nc, m, k, x, by_src, by_dst, pairs):
    src_rows = [m.sb(f"src_rows{i}", [P, NC, XT]) for i in range(NB)]
    dst_rows = [m.sb(f"dst_rows{i}", [P, NC, XD]) for i in range(NB)]
    pair_rows = [m.sb(f"pair_rows{i}", [P, NC, PAIR]) for i in range(NB)]
    normed = [m.sb(f"normed{i}", [P, NC, D]) for i in range(NB)]
    turned = [m.sb(f"turned{i}", [P, NGROUP, P]) for i in range(2)]
    stats = [m.sb(f"stats{i}", [P, NC, 6]) for i in range(NB)]
    small = [m.sb(f"small{i}", [P, 8, NC]) for i in range(NB)]
    ps_t = [m.ps(f"ps_t{i}") for i in range(2)]
    ps_a = [m.ps(f"ps_a{i}") for i in range(2)]
    ps_b = [m.ps(f"ps_b{i}") for i in range(2)]
    x_in = m.sems("in_x_landed", NB)
    stored = m.sems("in_stored", NB)
    moments, varied, rooted, scaled, biased = (m.sem("in_moments"), m.sem("in_varied"), m.sem("in_rooted"),
                                               m.sem("in_scaled"), m.sem("in_biased"))
    x_copied, norm_done, turn_done, turn_kept, mul_done, mul_kept = (
        m.sem("in_x_copied"), m.sem("in_norm_done"), m.sem("in_turn_done"), m.sem("in_turn_kept"),
        m.sem("in_mul_done"), m.sem("in_mul_kept"))

    with nc.Block() as block:
        @block.sync
        def _(sp):
            def body(now, _1, _2, coming):
                if coming:
                    wait_apart(sp, k.sp_past, stored[coming.buf], 48 * coming.turn)
                    sp.dma_start(pair_rows[coming.buf][0:coming.parts, 0:coming.tiles, 0:D],
                                 coming.rows(x, slice(0, D))).then_inc(x_in[coming.buf], 16)
                if now:
                    part = (slice(0, now.parts), slice(0, now.tiles))
                    wait_apart(sp, k.sp_past, x_copied, now.c + 1)
                    wait_apart(sp, k.sp_past, mul_kept, now.c * NGROUPS + now.groups())
                    for table, rows, width in ((by_src, src_rows, XT), (by_dst, dst_rows, XD), (pairs, pair_rows, PAIR)):
                        sp.dma_start(now.rows(table, slice(0, width)), rows[now.buf][part]).then_inc(stored[now.buf], 16)

            node_chunks(sp, body, lead=3)
            for h in range(NB):
                wait_apart(sp, k.sp_past, stored[h], 48 * uses(h))

        @block.gpsimd
        def _(pool):
            def body(_0, _1, soon):
                if soon:
                    p, n = soon.parts, soon.tiles
                    wait_apart(pool, k.pool_past, x_in[soon.buf], 16 * (soon.turn + 1))
                    pool.tensor_copy(dst_rows[soon.buf][0:p, 0:n, 0:D], pair_rows[soon.buf][0:p, 0:n, 0:D]).then_inc(x_copied, 1)

            node_chunks(pool, body, lead=2)

        @block.vector
        def _(v):
            def stats_of(ch, g):
                q, b, j, n = ch.group(g)
                ins = norm_stats(v, lambda j: pair_rows[ch.buf][0:ch.parts, j, 0:D], stats[ch.buf], ch.parts, range(j, j + n))
                if g == ch.groups() - 1:
                    ins.then_inc(moments, 1)

            def keep(ch, g):
                p = ch.parts
                q, b, j, n = ch.group(g)
                a = ps_a[b][0:p, 0:n * (D + 2 * HEADS)].rearrange("p (j f) -> p j f", j=n)
                bias = k.proj_bias[0:p, :].unsqueeze(1)
                v.wait_ge(mul_done, q + 1)
                v.tensor_tensor(src_rows[ch.buf][0:p, j:j + n, :], a[:, :, 0:XT],
                                bias[:, :, 0:XT].to_broadcast([p, n, XT]), op=ALU.add)
                v.tensor_tensor(dst_rows[ch.buf][0:p, j:j + n, D:XD], a[:, :, XT:XT + HEADS],
                                bias[:, :, XT:XT + HEADS].to_broadcast([p, n, HEADS]), op=ALU.add)
                v.tensor_tensor(pair_rows[ch.buf][0:p, j:j + n, D:PAIR],
                                ps_b[b][0:p, 0:n * D].rearrange("p (j f) -> p j f", j=n),
                                k.b1[0:p, :].unsqueeze(1).to_broadcast([p, n, D]), op=ALU.add).then_inc(mul_kept, 1)

            def scales(ch):
                p, n, s = ch.parts, ch.tiles, small[ch.buf]
                norm_moments(v, stats[ch.buf], s, moments, NORM_STEPS * ch.c, p, n)
                v.scalar_tensor_tensor(out=s[0:p, 4, 0:n], in0=s[0:p, 3, 0:n], scalar=0.25, in1=s[0:p, 2, 0:n],
                                       op0=ALU.mult, op1=ALU.add).then_inc(varied, 1)
                v.wait_ge(rooted, ch.c + 1)
                wait_past(v, norm_done, ch.c - (NB - 1))
                v.reciprocal(s[0:p, 6, 0:n], s[0:p, 5, 0:n]).then_inc(scaled, 1)
                v.wait_ge(scaled, ch.c + 1)
                v.scalar_tensor_tensor(out=s[0:p, 7, 0:n], in0=s[0:p, 0, 0:n], scalar=-0.5, in1=s[0:p, 6, 0:n],
                                       op0=ALU.mult, op1=ALU.mult).then_inc(biased, 1)

            def body(now, _1, soon):
                if soon:
                    v.wait_ge(x_in[soon.buf], 16 * (soon.turn + 1))
                for g in groups_of(now, soon):
                    if soon and g < soon.groups():
                        stats_of(soon, g)
                    if now and g < now.groups():
                        keep(now, g)
                if soon:
                    scales(soon)

            node_chunks(v, body, lead=2)

        @block.scalar
        def _(act):
            def turn(ch, g):
                p = ch.parts
                q, b, j, n = ch.group(g)
                act.wait_ge(turn_done, q + 1)
                wait_past(act, mul_done, q - 1)
                act.activation(turned[b][:, 0:n, 0:p], ps_t[b][:, 0:n * D].rearrange("p (j f) -> p j f", j=n)[:, :, 0:p],
                               ACT.Copy).then_inc(turn_kept, 1)

            def norm(ch, g):
                p, s = ch.parts, small[ch.buf]
                q, b, j0, n = ch.group(g)
                for j in range(j0, j0 + n):
                    ins = act.activation(normed[ch.buf][0:p, j, :], pair_rows[ch.buf][0:p, j, 0:D], ACT.Relu,
                                         bias=s[0:p, 7, j:j + 1], scale=s[0:p, 6, j:j + 1])
                if g == ch.groups() - 1:
                    ins.then_inc(norm_done, 1)

            def body(now, next_, soon):
                if next_:
                    act.wait_ge(biased, next_.c + 1)
                    wait_past(act, turn_done, (next_.c - (NB - 1)) * NGROUPS)
                for g in groups_of(now, next_):
                    if now and g < now.groups():
                        turn(now, g)
                    if next_ and g < next_.groups():
                        norm(next_, g)
                if soon:
                    p, n, s = soon.parts, soon.tiles, small[soon.buf]
                    act.wait_ge(varied, soon.c + 1)
                    act.activation(s[0:p, 5, 0:n], s[0:p, 4, 0:n], ACT.Sqrt, bias=k.eps[0:p, :]).then_inc(rooted, 1)

            node_chunks(act, body, lead=2)

        @block.tensor
        def _(pe):
            def multiply(ch, g):
                p = ch.parts
                q, b, j, n = ch.group(g)
                pe.wait_ge(turn_kept, q + 1)
                wait_past(pe, mul_kept, q - 1)
                for i in range(n):
                    w = D + 2 * HEADS
                    pe.matmul(ps_a[b][0:p, i * w:(i + 1) * w], turned[b][:, i, 0:p], k.proj[:, :], start=True, stop=True)
                    ins = pe.matmul(ps_b[b][0:p, i * D:(i + 1) * D], turned[b][:, i, 0:p], k.w1_src[:, :], start=True, stop=True)
                ins.then_inc(mul_done, 1)

            def body(now):
                if not now:
                    return
                p = now.parts
                pe.wait_ge(norm_done, now.c + 1)
                for g in range(now.groups()):
                    q, b, j, n = now.group(g)
                    wait_past(pe, turn_kept, q - 1)
                    for i in range(n):
                        ins = pe.transpose(ps_t[b][:, i * D:i * D + p], normed[now.buf][0:p, j + i, :], k.ident[0:p, 0:p])
                    ins.then_inc(turn_done, 1)
                    if g:
                        multiply(now, g - 1)
                multiply(now, now.groups() - 1)

            node_chunks(pe, body, lead=0)



def attention(nc, m, k, e, by_src, by_dst, pairs, h_rev, sums, joint):
    HALF = EC // 2
    src_rows = [m.sb(f"at_src{i}", [P, EC, XT]) for i in range(2)]
    dst_rows = [m.sb(f"at_dst{i}", [P, EC, XD]) for i in range(2)]
    out_rows = [m.sb(f"at_out{i}", [P, EC, PAIR]) for i in range(2)]
    h_rows = [m.sb(f"at_h{i}", [P, EC, D]) for i in range(2)]
    src_at = [m.sb(f"src_at{i}", [P, EC], I32) for i in range(2)]
    dst_at = [m.sb(f"dst_at{i}", [P, EC], I32) for i in range(2)]
    put_at = [m.sb(f"put_at{i}", [P, EC], I32) for i in range(2)]
    score = m.sb("score", [P, HEADS, EC])
    score_in = m.sb("score_in", [P, HEADS, SLOTS])
    reset_in = m.sb("reset_in", [P, HEADS, SLOTS])
    peak = m.sb("peak", [P, HEADS, SLOTS])
    gap = m.sb("gap", [P, 2, HEADS, EC])
    fade = m.sb("fade", [P, HEADS, SLOTS])
    weight = m.sb("weight", [P, HEADS, SLOTS])
    total = m.sb("total", [P, HEADS, SLOTS])
    over = m.sb("over", [P, HEADS, EC])
    fades = m.sb("fades", [P, D, SLOTS])
    part = m.sb("part", [P, D, SLOTS])
    acc = m.sb("acc", [P, D, SLOTS])
    mixed = m.sb("mixed_rows", [P, EC, D])
    caught = m.sb("caught", [P, D, EC])
    caught_sum = m.sb("caught_sum", [P, D])
    few = m.sb("few", [P, 2, HEADS, EC])
    few_sum = m.sb("few_sum", [P, 2, HEADS])
    stats = m.sb("at_stats", [P, EC, 6])
    small = m.sb("at_small", [P, 8, EC])
    turned = [m.sb(f"at_turned{i}", [P, HALF, P]) for i in range(2)]
    zeros = m.sb("zeros", [P, EC * AGG])
    ps_t = [m.ps(f"at_ps_t{i}", 2) for i in range(2)]
    ps_p = [m.ps(f"at_ps_p{i}", 2) for i in range(2)]
    picked = m.sems("at_picked", 2)
    put = m.sems("at_put", 2)
    h_out = m.sems("at_h_out", 2)
    zeroed, ready, set_up = m.sem("at_zeroed"), m.sem("at_indices"), m.sem("at_set_up")
    step, gaps, fade_done, weight_done, spread = (m.sem("at_step"), m.sem("at_gaps"), m.sem("at_fade"),
                                                  m.sem("at_weight"), m.sem("at_spread"))
    moments, varied, rooted, scaled = m.sem("at_moments"), m.sem("at_varied"), m.sem("at_rooted"), m.sem("at_scaled")
    norm_done, turn_done, turn_kept, mul_done, rows_done, scanned = (
        m.sem("at_norm_done"), m.sem("at_turn_done"), m.sem("at_turn_kept"), m.sem("at_mul_done"),
        m.sem("at_rows_done"), m.sem("at_scanned"))
    PICKS = 16 * 2 * EC
    PUTS = 16 * EC
    STEPS = 13

    with nc.Block() as block:
        @block.gpsimd
        def _(pool):
            def pick(c, b, turn):
                wait_apart(pool, k.pool_past, ready, c + 1)
                for j in range(EC):
                    pool.indirect_dma_start(src_rows[b][:, j, :], None, by_src[:, :],
                                            bass.IndirectOffsetOnAxis(src_at[b][:, j:j + 1], 0)).then_inc(picked[b], 16)
                    pool.indirect_dma_start(dst_rows[b][:, j, :], None, by_dst[:, :],
                                            bass.IndirectOffsetOnAxis(dst_at[b][:, j:j + 1], 0)).then_inc(picked[b], 16)

            def put_rows(c, b):
                wait_apart(pool, k.pool_past, rows_done, 2 * c + 2)
                for j in range(EC):
                    pool.indirect_dma_start(pairs[:, :], bass.IndirectOffsetOnAxis(put_at[b][:, j:j + 1], 0),
                                            out_rows[b][:, j, :], None, bounds_check=N - 1,
                                            oob_is_err=False).then_inc(put[b], 16)

            pick(0, 0, 0)
            with pool.Fori(0, ECHUNKS // 2 - 1) as t:
                pick(2 * t + 1, 1, t)
                put_rows(2 * t, 0)
                pick(2 * t + 2, 0, t + 1)
                put_rows(2 * t + 1, 1)
            pick(ECHUNKS - 1, 1, ECHUNKS // 2 - 1)
            put_rows(ECHUNKS - 2, 0)
            put_rows(ECHUNKS - 1, 1)
            for b in range(2):
                wait_apart(pool, k.pool_past, put[b], PUTS * (ECHUNKS // 2))

        @block.sync
        def _(sp):
            wait_apart(sp, k.sp_past, set_up, 1)

            def chunk(c, b, turn):
                for table in sums:
                    sp.dma_start(table[bass.ds(c * (P * EC), P * EC), :].rearrange("(p j) f -> p (j f)", p=P),
                                 zeros[:, :]).then_inc(zeroed, 16)
                wait_apart(sp, k.sp_past, norm_done, c + 1)
                sp.dma_start(h_rev[:, bass.ds((ECHUNKS - 1 - c) * EC, EC), :], h_rows[b][:, :, :]).then_inc(h_out[b], 16)

            edge_chunks(sp, chunk)
            wait_apart(sp, k.sp_past, zeroed, 16 * 2 * ECHUNKS)
            for b in range(2):
                wait_apart(sp, k.sp_past, h_out[b], 16 * (ECHUNKS // 2))

        @block.vector
        def _(v):
            def indices(c, b):
                v.tensor_copy(src_at[b][:, :], e.src[:, bass.ds(c * EC, EC)])
                v.tensor_copy(dst_at[b][:, :], e.dst_pick[:, bass.ds(c * EC, EC)]).then_inc(ready, 1)

            for b in range(2):
                indices(b, b)
            v.memset(reset_in[:, :, 0:1], -BIG)
            v.memset(fade[:, :, :], 0.0)
            v.memset(peak[:, :, :], 0.0)
            v.memset(total[:, :, :], 0.0)
            v.memset(acc[:, :, :], 0.0)
            v.memset(joint["head"][:, :], 0.0)
            v.memset(zeros[:, :], 0.0).then_inc(set_up, 1)
            v.wait_ge(set_up, 1)

            def chunk(c, b, turn):
                cols = bass.ds(c * EC, EC)
                base = c * STEPS
                xs, xd, out, s = src_rows[b], dst_rows[b], out_rows[b], small

                def at(n):
                    v.wait_ge(step, base + n)

                if not (isinstance(c, int) and c == 0):
                    v.wait_ge(scanned, 3 * c)
                v.tensor_copy(score_in[:, :, 0:1], peak[:, :, EC:SLOTS])
                v.tensor_copy(weight[:, :, 0:1], total[:, :, EC:SLOTS])
                v.tensor_copy(part[:, :, 0:1], acc[:, :, EC:SLOTS])
                v.tensor_copy(reset_in[:, :, 1:SLOTS], e.reset[:, cols].unsqueeze(1).to_broadcast([P, HEADS, EC])).then_inc(step, 1)
                v.wait_ge(picked[b], PICKS * (turn + 1))
                v.tensor_tensor(score[:, :, :], xs[:, :, D:XT].rearrange("p j h -> p h j"),
                                xd[:, :, D:XD].rearrange("p j h -> p h j"), op=ALU.add).then_inc(step, 1)
                at(2)
                v.scalar_tensor_tensor(out=score_in[:, :, 1:SLOTS], in0=score[:, :, :], scalar=SLOPE, in1=score[:, :, :],
                                       op0=ALU.mult, op1=ALU.max).then_inc(step, 1)
                at(3)
                v.tensor_tensor_scan(peak[:, :, :].rearrange("p h j -> p (h j)"), reset_in[:, :, :].rearrange("p h j -> p (h j)"),
                                     score_in[:, :, :].rearrange("p h j -> p (h j)"), 0.0, op0=ALU.add,
                                     op1=ALU.max).then_inc(scanned, 1)
                v.wait_ge(scanned, 3 * c + 1)
                v.tensor_tensor(score[:, :, :], peak[:, :, 0:EC], reset_in[:, :, 1:SLOTS], op=ALU.add).then_inc(step, 1)
                v.tensor_tensor(gap[:, 1, :, :], score_in[:, :, 1:SLOTS], peak[:, :, 1:SLOTS], op=ALU.subtract)
                at(4)
                v.tensor_tensor(gap[:, 0, :, :], score[:, :, :], peak[:, :, 1:SLOTS], op=ALU.subtract).then_inc(gaps, 1)
                v.wait_ge(weight_done, c + 1)
                v.tensor_tensor_scan(total[:, :, :].rearrange("p h j -> p (h j)"), fade[:, :, :].rearrange("p h j -> p (h j)"),
                                     weight[:, :, :].rearrange("p h j -> p (h j)"), 0.0, op0=ALU.mult,
                                     op1=ALU.add).then_inc(scanned, 1)
                v.tensor_tensor(part[:, :, 1:SLOTS].rearrange("p (h f) j -> p h f j", h=HEADS),
                                xs[:, :, 0:D].rearrange("p j (h f) -> p h f j", h=HEADS),
                                weight[:, :, 1:SLOTS].unsqueeze(2).to_broadcast([P, HEADS, CH, EC]),
                                op=ALU.mult).then_inc(step, 1)
                v.wait_ge(scanned, 3 * c + 2)
                v.tensor_scalar(over[:, :, :], total[:, :, 1:SLOTS], 1e-16, None, op0=ALU.add).then_inc(step, 1)
                at(6)
                v.reciprocal(score[:, :, :], over[:, :, :])
                v.wait_ge(spread, c + 1)
                v.tensor_tensor_scan(acc[:, :, :].rearrange("p f j -> p (f j)"), fades[:, :, :].rearrange("p f j -> p (f j)"),
                                     part[:, :, :].rearrange("p f j -> p (f j)"), 0.0, op0=ALU.mult,
                                     op1=ALU.add).then_inc(scanned, 1)
                v.wait_ge(scanned, 3 * c + 3)
                v.tensor_tensor(mixed[:, :, :].rearrange("p j (h f) -> p h f j", h=HEADS),
                                acc[:, :, 1:SLOTS].rearrange("p (h f) j -> p h f j", h=HEADS),
                                score[:, :, :].unsqueeze(2).to_broadcast([P, HEADS, CH, EC]),
                                op=ALU.mult).then_inc(step, 1)
                at(7)
                if not (isinstance(turn, int) and turn == 0):
                    v.wait_ge(put[b], PUTS * turn)
                v.tensor_tensor(out[:, :, 0:D], mixed[:, :, :], xd[:, :, 0:D], op=ALU.add).then_inc(step, 1)
                indices(c + 2, b)
                v.tensor_copy(put_at[b][:, :], e.put[:, cols])
                mark = e.head_end[:, cols]
                v.tensor_tensor(caught[:, :, :], acc[:, :, 1:SLOTS], mark.unsqueeze(1).to_broadcast([P, D, EC]), op=ALU.mult)
                v.tensor_tensor(few[:, 0, :, :], peak[:, :, 1:SLOTS], mark.unsqueeze(1).to_broadcast([P, HEADS, EC]), op=ALU.mult)
                v.tensor_tensor(few[:, 1, :, :], total[:, :, 1:SLOTS], mark.unsqueeze(1).to_broadcast([P, HEADS, EC]),
                                op=ALU.mult).then_inc(step, 1)
                at(9)
                v.tensor_reduce(caught_sum[:, :], caught[:, :, :], AX.X, ALU.add)
                v.tensor_reduce(few_sum[:, :, :], few[:, :, :, :], AX.X, ALU.add).then_inc(step, 1)
                at(10)
                head = joint["head"]
                v.tensor_tensor(head[:, 0:D], head[:, 0:D], caught_sum[:, :], op=ALU.add)
                v.tensor_tensor(head[:, D:D + 2 * HEADS], head[:, D:D + 2 * HEADS],
                                few_sum[:, :, :].rearrange("p two h -> p (two h)"), op=ALU.add).then_inc(step, 1)
                norm_stats(v, lambda j: out[:, j, 0:D], stats, P, range(EC)).then_inc(moments, 1)
                norm_moments(v, stats, s, moments, NORM_STEPS * c, P, EC)
                v.scalar_tensor_tensor(out=s[:, 4, :], in0=s[:, 3, :], scalar=0.25, in1=s[:, 2, :],
                                       op0=ALU.mult, op1=ALU.add).then_inc(varied, 1)
                v.wait_ge(rooted, c + 1)
                wait_past(v, norm_done, c)
                v.reciprocal(s[:, 3, :], s[:, 5, :]).then_inc(step, 1)
                at(12)
                v.tensor_tensor(s[:, 6, :], s[:, 3, :], e.last[:, cols], op=ALU.mult).then_inc(step, 1)
                at(13)
                v.scalar_tensor_tensor(out=s[:, 7, :], in0=s[:, 0, :], scalar=-0.5, in1=s[:, 6, :],
                                       op0=ALU.mult, op1=ALU.mult).then_inc(scaled, 1)
                for half in range(2):
                    js = slice(half * HALF, half * HALF + HALF)
                    v.wait_ge(mul_done, 2 * c + half + 1)
                    v.tensor_tensor(out[:, js, D:PAIR], ps_p[half][:, 0:HALF * D].rearrange("p (j f) -> p j f", j=HALF),
                                    k.b1[:, :].unsqueeze(1).to_broadcast([P, HALF, D]), op=ALU.add).then_inc(rows_done, 1)

            edge_chunks(v, chunk)
            v.tensor_copy(joint["tail"][:, 0:D], acc[:, :, EC])
            v.tensor_copy(joint["tail"][:, D:D + HEADS], peak[:, :, EC])
            v.tensor_copy(joint["tail"][:, D + HEADS:D + 2 * HEADS], total[:, :, EC]).then_inc(set_up, 1)
            v.wait_ge(set_up, 2)

        @block.scalar
        def _(act):
            def chunk(c, b, turn):
                act.wait_ge(gaps, c + 1)
                act.activation(fade[:, :, 1:SLOTS], gap[:, 0, :, :], ACT.Exp).then_inc(fade_done, 1)
                act.activation(weight[:, :, 1:SLOTS], gap[:, 1, :, :], ACT.Exp).then_inc(weight_done, 1)
                act.wait_ge(fade_done, c + 1)
                act.activation(fades[:, :, :].rearrange("p (h f) j -> p h f j", h=HEADS),
                               fade[:, :, :].unsqueeze(2).to_broadcast([P, HEADS, CH, SLOTS]), ACT.Copy).then_inc(spread, 1)
                act.wait_ge(varied, c + 1)
                act.activation(small[:, 5, :], small[:, 4, :], ACT.Sqrt, bias=k.eps[:, :]).then_inc(rooted, 1)
                act.wait_ge(scaled, c + 1)
                if not (isinstance(turn, int) and turn == 0):
                    act.wait_ge(h_out[b], 16 * turn)
                wait_past(act, turn_done, 2 * c - 2)
                for j in range(EC):
                    ins = act.activation(h_rows[b][:, EC - 1 - j, :], out_rows[b][:, j, 0:D], ACT.Relu,
                                         bias=small[:, 7, j:j + 1], scale=small[:, 6, j:j + 1])
                ins.then_inc(norm_done, 1)
                for half in range(2):
                    act.wait_ge(turn_done, 2 * c + half + 1)
                    wait_past(act, mul_done, 2 * c + half - 1)
                    act.activation(turned[half][:, :, :], ps_t[half][:, 0:HALF * P].rearrange("p (j f) -> p j f", j=HALF),
                                   ACT.Copy).then_inc(turn_kept, 1)

            edge_chunks(act, chunk)

        @block.tensor
        def _(pe):
            def chunk(c, b, turn):
                pe.wait_ge(norm_done, c + 1)
                for half in range(2):
                    wait_past(pe, turn_kept, 2 * c + half - 1)
                    for i in range(HALF):
                        ins = pe.transpose(ps_t[half][:, i * P:(i + 1) * P], h_rows[b][:, EC - 1 - (half * HALF + i), :], k.ident[:, :])
                    ins.then_inc(turn_done, 1)
                for half in range(2):
                    pe.wait_ge(turn_kept, 2 * c + half + 1)
                    wait_past(pe, rows_done, 2 * c + half - 1)
                    for i in range(HALF):
                        ins = pe.matmul(ps_p[half][:, i * D:(i + 1) * D], turned[half][:, i, :], k.w1_src[:, :], start=True, stop=True)
                    ins.then_inc(mul_done, 1)

            edge_chunks(pe, chunk)



def joints(nc, m, k, e, by_dst, pairs, h_rev, joint):
    W = D + HEADS
    part = [joint["tail"], joint["head"]]
    key = m.sb("j_key", [P, 2])
    key_at = [m.sb(f"j_at{i}", [P, 1], I32) for i in range(2)]
    same = [m.sb(f"j_same{i}", [P, 2, P]) for i in range(2)]
    pen = m.sb("j_pen", [P, 2, P])
    top = [m.sb(f"j_top{i}", [P, HEADS]) for i in range(2)]
    cand = m.sb("j_cand", [P, HEADS, 2 * P])
    fac = m.sb("j_fac", [P, 2, HEADS])
    scaled = m.sb("j_scaled", [P, 2, W])
    xrow = [m.sb(f"j_x{i}", [P, XD]) for i in range(2)]
    den = m.sb("j_den", [P, 2, HEADS])
    rows = [m.sb(f"j_rows{i}", [P, PAIR]) for i in range(2)]
    h = [m.sb(f"j_h{i}", [P, D]) for i in range(2)]
    hT = [m.sb(f"j_ht{i}", [P, P]) for i in range(2)]
    stats = m.sb("j_stats", [P, 2, 6])
    small = m.sb("j_small", [P, 8, 2])
    scrap = m.sb("j_scrap", [P, P])
    cnt = m.sb("j_cnt", [P, 2])
    flat = m.sb("j_flat", [P, 4])
    put = [m.sb(f"j_put{i}", [P, 1], I32) for i in range(2)]
    h_put = m.sb("j_h_put", [P, 1], I32)
    ps_k = m.ps("j_ps_k")
    ps_m = m.ps("j_ps_m", 2)
    ps_s = m.ps("j_ps_s", 1)
    ps_h = m.ps("j_ps_h")
    step, turned, peaks, weighed, gathered, out, stage, muls, acts = (
        m.sem("j_step"), m.sem("j_turned"), m.sem("j_peaks"), m.sem("j_weighed"), m.sem("j_gathered"), m.sem("j_out"),
        m.sem("j_stage"), m.sem("j_muls"), m.sem("j_acts"))
    tails_out = m.sem("j_tails_out")
    keyed, indexed, masked, summed, normed_, h_kept, ready = (
        m.sem("j_keyed"), m.sem("j_indexed"), m.sem("j_masked"), m.sem("j_summed"), m.sem("j_normed"), m.sem("j_h_kept"),
        m.sem("j_ready"))
    edge0 = m.sb("j_edge0", [P, 1])

    with nc.Block() as block:
        @block.vector
        def _(v):
            done = [0]

            def link(ins):
                done[0] += 1
                ins.then_inc(step, 1)
                v.wait_ge(step, done[0])

            first, last = e.dst_f[:, 0:1], e.dst_f[:, T - 1:T]
            v.tensor_copy(key[:, 0:1], last)
            v.tensor_copy(key_at[0][:, :], e.dst_pick[:, T - 1:T])
            v.tensor_copy(key_at[1][:, :], e.dst_pick[:, 0:1]).then_inc(indexed, 1)
            link(v.tensor_tensor(flat[:, 0:1], first, last, op=ALU.is_equal))
            v.tensor_tensor(flat[:, 1:2], flat[:, 0:1], k.trash[:, :], op=ALU.mult)
            link(v.tensor_scalar(flat[:, 2:3], flat[:, 0:1], -1.0, 1.0, op0=ALU.mult, op1=ALU.add))
            link(v.tensor_tensor(flat[:, 3:4], flat[:, 2:3], first, op=ALU.mult))
            link(v.scalar_tensor_tensor(out=key[:, 1:2], in0=flat[:, 1:2], scalar=-1.0, in1=flat[:, 3:4],
                                        op0=ALU.mult, op1=ALU.add))
            v.sem_inc(keyed, 1)
            v.wait_ge(turned, 1)
            keys = ps_k[:, 0:2 * P].rearrange("p (a f) -> p a f", a=2)
            for i in range(2):
                link(v.tensor_scalar(same[i][:, :, :], keys, key[:, i:i + 1], None, op0=ALU.is_equal))
            v.sem_inc(masked, 1)
            for i in range(2):
                link(v.tensor_scalar(pen[:, :, :], same[i][:, :, :], -1.0, BIG, op0=ALU.add, op1=ALU.mult))
                v.wait_ge(peaks, 1)
                link(v.tensor_tensor(cand[:, :, :], ps_m[:, :].rearrange("p (h a) -> p h a", h=HEADS),
                                     pen[:, :, :].rearrange("p a f -> p (a f)").unsqueeze(1).to_broadcast([P, HEADS, 2 * P]), op=ALU.add))
                link(v.tensor_reduce(top[i][:, :], cand[:, :, :], AX.X, ALU.max))
                link(v.tensor_tensor(fac[:, i, :], part[i][:, D:D + HEADS], top[i][:, :], op=ALU.subtract))
            v.sem_inc(stage, 1)
            v.wait_ge(weighed, 1)
            for i in range(2):
                v.tensor_tensor(scaled[:, i, 0:D].rearrange("p (h f) -> p h f", h=HEADS),
                                part[i][:, 0:D].rearrange("p (h f) -> p h f", h=HEADS),
                                fac[:, i, :].unsqueeze(2).to_broadcast([P, HEADS, CH]), op=ALU.mult)
                link(v.tensor_tensor(scaled[:, i, D:W], part[i][:, D + HEADS:D + 2 * HEADS], fac[:, i, :], op=ALU.mult))
            v.sem_inc(stage, 1)
            v.tensor_tensor(scrap[:, :], same[0][:, 0, :], k.upto[:, :], op=ALU.mult)
            link(v.tensor_reduce(cnt[:, 1:2], same[1][:, 0, :], AX.X, ALU.max))
            link(v.tensor_reduce(cnt[:, 0:1], scrap[:, :], AX.X, ALU.add))
            link(v.tensor_scalar(flat[:, 0:1], cnt[:, 0:1], 1.0, None, op0=ALU.is_equal))
            link(v.tensor_scalar(flat[:, 3:4], cnt[:, 1:2], -1.0, 1.0, op0=ALU.mult, op1=ALU.add))
            link(v.tensor_tensor(flat[:, 1:2], flat[:, 3:4], flat[:, 2:3], op=ALU.mult))
            for i in range(2):
                link(v.scalar_tensor_tensor(out=den[:, i, 0:1], in0=key[:, i:i + 1], scalar=-float(SKIP), in1=flat[:, i:i + 1],
                                            op0=ALU.add, op1=ALU.mult))
                link(v.tensor_scalar(put[i][:, :], den[:, i, 0:1], float(SKIP), None, op0=ALU.add))
            link(v.tensor_scalar(edge0[:, :], k.trash[:, :], float(1 - N), float(T), op0=ALU.add, op1=ALU.mult))
            link(v.tensor_tensor(edge0[:, :], edge0[:, :], joint["head_len"][:, :], op=ALU.subtract))
            link(v.scalar_tensor_tensor(out=edge0[:, :], in0=edge0[:, :], scalar=-float(SKIP), in1=flat[:, 2:3],
                                        op0=ALU.add, op1=ALU.mult))
            link(v.tensor_scalar(h_put[:, :], edge0[:, :], float(SKIP), None, op0=ALU.add))
            v.wait_ge(summed, 1)
            v.wait_ge(gathered, 32)
            for i in range(2):
                got = ps_s[:, i * W:(i + 1) * W]
                link(v.tensor_scalar(den[:, i, :], got[:, D:W], 1e-16, None, op0=ALU.add))
                link(v.reciprocal(fac[:, i, :], den[:, i, :]))
                link(v.tensor_tensor(rows[i][:, 0:D].rearrange("p (h f) -> p h f", h=HEADS),
                                     got[:, 0:D].rearrange("p (h f) -> p h f", h=HEADS),
                                     fac[:, i, :].unsqueeze(2).to_broadcast([P, HEADS, CH]), op=ALU.mult))
                link(v.tensor_tensor(rows[i][:, 0:D], rows[i][:, 0:D], xrow[i][:, 0:D], op=ALU.add))
            norm_stats(v, lambda j: rows[j][:, 0:D], stats, P, range(2)).then_inc(normed_, 1)
            norm_moments(v, stats, small, normed_, 0, P, 2)
            link(v.scalar_tensor_tensor(out=small[:, 4, :], in0=small[:, 3, :], scalar=0.25, in1=small[:, 2, :],
                                        op0=ALU.mult, op1=ALU.add))
            v.sem_inc(stage, 1)
            v.wait_ge(acts, 1)
            link(v.reciprocal(small[:, 6, :], small[:, 5, :]))
            link(v.scalar_tensor_tensor(out=small[:, 7, :], in0=small[:, 0, :], scalar=-0.5, in1=small[:, 6, :],
                                        op0=ALU.mult, op1=ALU.mult))
            v.sem_inc(stage, 1)
            v.wait_ge(muls, 2)
            for i in range(2):
                link(v.tensor_copy(hT[i][:, :], ps_h[:, i * P:(i + 1) * P]))
            v.sem_inc(stage, 1)
            v.wait_ge(muls, 4)
            for i in range(2):
                link(v.tensor_tensor(rows[i][:, D:PAIR], ps_h[:, 256 + i * D:256 + (i + 1) * D], k.b1[:, :], op=ALU.add))
            v.sem_inc(ready, 1)

        @block.scalar
        def _(act):
            act.wait_ge(stage, 1)
            act.activation(fac[:, :, :], fac[:, :, :], ACT.Exp).then_inc(weighed, 1)
            act.wait_ge(stage, 3)
            act.activation(small[:, 5, :], small[:, 4, :], ACT.Sqrt, bias=k.eps[:, :]).then_inc(acts, 1)
            act.wait_ge(stage, 4)
            for i in range(2):
                act.activation(h[i][:, :], rows[i][:, 0:D], ACT.Relu, bias=small[:, 7, i:i + 1],
                               scale=small[:, 6, i:i + 1]).then_inc(h_kept, 1)

        @block.tensor
        def _(pe):
            pe.wait_ge(keyed, 1)
            for i in range(2):
                ins = pe.transpose(ps_k[:, i * P:(i + 1) * P], key[:, i:i + 1].to_broadcast([P, P]), k.ident[:, :])
            ins.then_inc(turned, 1)
            for hd in range(HEADS):
                for i in range(2):
                    ins = pe.transpose(ps_m[:, (2 * hd + i) * P:(2 * hd + i + 1) * P],
                                       part[i][:, D + hd:D + hd + 1].to_broadcast([P, P]), k.ident[:, :])
            ins.then_inc(peaks, 1)
            pe.wait_ge(masked, 1)
            pe.wait_ge(stage, 2)
            for i in range(2):
                for j in range(2):
                    ins = pe.matmul(ps_s[:, i * W:(i + 1) * W], same[j][:, i, :], scaled[:, j, :], start=(j == 0), stop=(j == 1))
            ins.then_inc(summed, 1)
            for i in range(2):
                pe.wait_ge(h_kept, 2)
                pe.transpose(ps_h[:, i * P:(i + 1) * P], h[i][:, :], k.ident[:, :]).then_inc(muls, 1)
            pe.wait_ge(stage, 5)
            for i in range(2):
                pe.matmul(ps_h[:, 256 + i * D:256 + (i + 1) * D], hT[i][:, :], k.w1_src[:, :], start=True, stop=True).then_inc(muls, 1)

        @block.gpsimd
        def _(pool):
            wait_apart(pool, k.pool_past, indexed, 1)
            for i in range(2):
                pool.indirect_dma_start(xrow[i][:, :], None, by_dst[:, :],
                                        bass.IndirectOffsetOnAxis(key_at[i][:, 0:1], 0)).then_inc(gathered, 16)
            wait_apart(pool, k.pool_past, ready, 1)
            for i in range(2):
                pool.indirect_dma_start(pairs[:, :], bass.IndirectOffsetOnAxis(put[i][:, 0:1], 0), rows[i][:, :], None,
                                        bounds_check=N - 1, oob_is_err=False).then_inc(out, 16)
            pool.indirect_dma_start(h_rev.rearrange("p t f -> (p t) f"), bass.IndirectOffsetOnAxis(h_put[:, 0:1], 0),
                                    h[1][:, :], None, bounds_check=P * T - 1, oob_is_err=False).then_inc(out, 16)
            wait_apart(pool, k.pool_past, out, 48)

        @block.sync
        def _(sp):
            wait_apart(sp, k.sp_past, h_kept, 2)
            sp.dma_start(h_rev[:, 0:1, :].rearrange("p one f -> p (one f)"), h[0][:, :]).then_inc(tails_out, 16)
            wait_apart(sp, k.sp_past, tails_out, 16)



def messages(nc, m, k, e, halves, h_rev, sums):
    HALF = EC // 2
    VG = 3
    vgroups = [(j, min(VG, EC - j)) for j in range(0, EC, VG)]
    NV = len(vgroups)
    h_in = [m.sb(f"me_h{i}", [P, EC, D]) for i in range(2)]
    prod = [m.sb(f"me_prod{i}", [P, EC, D]) for i in range(2)]
    out = [m.sb(f"me_out{i}", [P, EC, AGG]) for i in range(2)]
    at_in = [m.sb(f"me_at{i}", [P, EC], I32) for i in range(2)]
    at_out = [m.sb(f"me_to{i}", [P, EC], I32) for i in range(2)]
    keys = [m.sb(f"me_keys{i}", [P, EC]) for i in range(2)]
    ends = m.sb("me_ends", [P, D, SLOTS])
    keep = m.sb("me_keep", [P, D, SLOTS])
    xn = [m.sb(f"me_xn{i}", [P, D, SLOTS]) for i in range(2)]
    turned = [m.sb(f"me_turned{i}", [P, HALF, P]) for i in range(2)]
    same = m.sb("me_same", [P, EC, P])
    cnt = m.sb("me_cnt", [P, EC])
    once = m.sb("me_once", [P, EC])
    less = m.sb("me_less", [P, EC])
    to_f = m.sb("me_to_f", [P, EC])
    logit = m.sb("me_logit", [P, EC])
    msg = m.sb("me_msg", [P, EC, AGG])
    mask = m.sb("me_mask", [P, EC])
    ps_t = m.ps("me_ps_t", 2)
    ps_q = m.ps("me_ps_q", 2)
    ps_r = m.ps("me_ps_r", 2)
    ps_v = [m.ps(f"me_ps_v{i}") for i in range(2)]
    landed = m.sems("me_landed", 2)
    picked = m.sems("me_picked", 2)
    added = m.sems("me_added", 2)
    ready, set_up, ends_in, keep_in, scanned = (m.sem("me_indices"), m.sem("me_set_up"), m.sem("me_ends_in"),
                                                m.sem("me_keep_in"), m.sem("me_scanned"))
    turn_done, turn_kept, q_done, q_kept, r_done, r_kept = (m.sem("me_turn_done"), m.sem("me_turn_kept"), m.sem("me_q_done"),
                                                            m.sem("me_q_kept"), m.sem("me_r_done"), m.sem("me_r_kept"))
    step, dotted, masked, msg_done, to_done, v_done, v_kept, free = (
        m.sem("me_step"), m.sem("me_dotted"), m.sem("me_masked"), m.sem("me_msg_done"), m.sem("me_to_done"),
        m.sem("me_v_done"), m.sem("me_v_kept"), m.sem("me_out_free"))
    STEPS = 5
    PER = EC // 2

    with nc.Block() as block:
        @block.gpsimd
        def _(pool):
            def pick(c, b):
                wait_apart(pool, k.pool_past, ready, c + 1)
                for j in range(EC):
                    pool.indirect_dma_start(prod[b][:, j, :], None, halves[:, :],
                                            bass.IndirectOffsetOnAxis(at_in[b][:, j:j + 1], 0)).then_inc(picked[b], 16)

            def add(c, b):
                wait_apart(pool, k.pool_past, v_kept, NV * c + NV)
                wait_apart(pool, k.pool_past, to_done, c + 1)
                for j in range(EC):
                    wait_apart(pool, k.pool_past, added[j % 2], 16 * (PER * c + j // 2))
                    pool.indirect_dma_start(sums[j % 2][:, :], bass.IndirectOffsetOnAxis(at_out[b][:, j:j + 1], 0),
                                            out[b][:, j, :], None, compute_op=ALU.add).then_inc(added[j % 2], 16)

            pick(0, 0)
            pick(1, 1)
            add(0, 0)
            with pool.Fori(1, ECHUNKS // 2) as t:
                pick(2 * t, 0)
                add(2 * t - 1, 1)
                pick(2 * t + 1, 1)
                add(2 * t, 0)
            add(ECHUNKS - 1, 1)
            for b in range(2):
                wait_apart(pool, k.pool_past, added[b], 16 * PER * ECHUNKS)

        @block.sync
        def _(sp):
            def chunk(c, b, turn):
                wait_apart(sp, k.sp_past, ends_in, c - 1)
                sp.dma_start(h_in[b][:, :, :], h_rev[:, bass.ds(c * EC, EC), :]).then_inc(landed[b], 16)

            edge_chunks(sp, chunk)

        @block.vector
        def _(v):
            def indices(c, b):
                v.tensor_copy(keys[b][:, :], e.key_rev[:, bass.ds(c * EC, EC)])
                v.tensor_copy(at_in[b][:, :], e.pick_rev[:, bass.ds(c * EC, EC)]).then_inc(ready, 1)

            for b in range(2):
                indices(b, b)
            v.memset(keep[:, :, 0:1], 0.0)
            v.memset(xn[1][:, :, :], 0.0)
            v.memset(msg[:, :, D + 1:AGG], 1.0).then_inc(set_up, 1)
            v.wait_ge(set_up, 1)

            def chunk(c, b, turn):
                base = c * STEPS

                def at(n):
                    v.wait_ge(step, base + n)

                for half in range(2):
                    v.wait_ge(r_done, 2 * c + half + 1)
                    wait_past(v, v_done, NV * c)
                    for i in range(HALF):
                        j = half * HALF + i
                        ins = v.scalar_tensor_tensor(out=same[:, j, :], in0=ps_r[:, i * P:(i + 1) * P],
                                                     scalar=keys[b][:, j:j + 1], in1=k.upto[:, :],
                                                     op0=ALU.is_equal, op1=ALU.mult, accum_out=cnt[:, j:j + 1])
                    ins.then_inc(r_kept, 1)
                wait_past(v, scanned, c)
                v.wait_ge(ends_in, c + 1)
                v.tensor_copy(ends[:, :, 0:1], xn[1 - b][:, :, EC:SLOTS]).then_inc(step, 1)
                v.wait_ge(keep_in, c + 1)
                at(1)
                v.tensor_tensor_scan(xn[b][:, :, :].rearrange("p f j -> p (f j)"), keep[:, :, :].rearrange("p f j -> p (f j)"),
                                     ends[:, :, :].rearrange("p f j -> p (f j)"), 0.0, op0=ALU.mult,
                                     op1=ALU.add).then_inc(scanned, 1)
                v.tensor_scalar(once[:, :], cnt[:, :], 1.0, None, op0=ALU.is_equal)
                v.tensor_scalar(less[:, :], keys[b][:, :], k.trash[:, :], None, op0=ALU.subtract).then_inc(step, 1)
                at(2)
                v.tensor_tensor(to_f[:, :], once[:, :], less[:, :], op=ALU.mult).then_inc(step, 1)
                at(3)
                if not (isinstance(c, int) and c < 2):
                    for table in range(2):
                        v.wait_ge(added[table], 16 * PER * (c - 1))
                v.tensor_scalar(at_out[b][:, :], to_f[:, :], k.trash[:, :], None, op0=ALU.add).then_inc(to_done, 1)
                v.wait_ge(picked[b], 16 * EC * (turn + 1))
                z = prod[b]
                for half in range(2):
                    js = slice(half * HALF, half * HALF + HALF)
                    v.wait_ge(q_done, 2 * c + half + 1)
                    v.tensor_tensor(z[:, js, :], z[:, js, :], ps_q[:, 0:HALF * D].rearrange("p (j f) -> p j f", j=HALF),
                                    op=ALU.add).then_inc(q_kept, 1)
                    v.wait_ge(q_kept, 2 * c + half + 1)
                    v.scalar_tensor_tensor(out=z[:, js, :], in0=z[:, js, :], scalar=0.0,
                                           in1=k.w2[:, :].unsqueeze(1).to_broadcast([P, HALF, D]), op0=ALU.max,
                                           op1=ALU.mult).then_inc(step, 1)
                    at(4 + half)
                v.tensor_reduce(logit[:, :], z[:, :, :], AX.X, ALU.add).then_inc(dotted, 1)
                v.wait_ge(dotted, c + 1)
                indices(c + 2, b)
                v.wait_ge(masked, c + 1)
                wait_past(v, v_done, NV * c)
                v.tensor_copy(msg[:, :, D:D + 1], mask[:, :].unsqueeze(2))
                v.tensor_tensor(msg[:, :, 0:D], xn[b][:, :, 1:SLOTS].rearrange("p f j -> p j f"),
                                mask[:, :].unsqueeze(2).to_broadcast([P, EC, D]), op=ALU.mult).then_inc(msg_done, 1)

            edge_chunks(v, chunk)

        @block.scalar
        def _(act):
            def chunk(c, b, turn):
                act.wait_ge(landed[b], 16 * (turn + 1))
                wait_past(act, scanned, c)
                act.activation(ends[:, :, 1:SLOTS].rearrange("p f j -> p j f"), h_in[b][:, :, :], ACT.Copy).then_inc(ends_in, 1)
                act.activation(keep[:, :, 1:SLOTS], e.go_on_rev[:, bass.ds(c * EC, EC)].unsqueeze(1).to_broadcast([P, D, EC]),
                               ACT.Copy).then_inc(keep_in, 1)
                for half in range(2):
                    act.wait_ge(turn_done, 2 * c + half + 1)
                    wait_past(act, q_done, 2 * c + half - 1)
                    act.activation(turned[half][:, :, :], ps_t[:, 0:HALF * P].rearrange("p (j f) -> p j f", j=HALF),
                                   ACT.Copy).then_inc(turn_kept, 1)
                act.wait_ge(dotted, c + 1)
                wait_past(act, msg_done, c)
                act.activation(mask[:, :], logit[:, :], ACT.Sigmoid, bias=k.b2[:, :]).then_inc(masked, 1)
                if not (isinstance(c, int) and c < 2):
                    for table in range(2):
                        act.wait_ge(added[table], 16 * PER * (c - 1))
                for g, (j, n) in enumerate(vgroups):
                    q = NV * c + g
                    act.wait_ge(v_done, q + 1)
                    act.activation(out[b][:, j:j + n, :], ps_v[(NV * b + g) % 2][:, 0:n * AGG].rearrange("p (j f) -> p j f", j=n),
                                   ACT.Copy).then_inc(v_kept, 1)

            edge_chunks(act, chunk)

        @block.tensor
        def _(pe):
            def chunk(c, b, turn):
                pe.wait_ge(ready, c + 1)
                for half in range(2):
                    wait_past(pe, r_kept, 2 * c + half)
                    for i in range(HALF):
                        j = half * HALF + i
                        ins = pe.transpose(ps_r[:, i * P:(i + 1) * P], keys[b][:, j:j + 1].to_broadcast([P, P]), k.ident[:, :])
                    ins.then_inc(r_done, 1)
                pe.wait_ge(scanned, c + 1)
                for half in range(2):
                    wait_past(pe, turn_kept, 2 * c + half)
                    for i in range(HALF):
                        ins = pe.transpose(ps_t[:, i * P:(i + 1) * P], xn[b][:, :, 1 + half * HALF + i], k.ident[:, :])
                    ins.then_inc(turn_done, 1)
                    pe.wait_ge(turn_kept, 2 * c + half + 1)
                    wait_past(pe, q_kept, 2 * c + half)
                    for i in range(HALF):
                        ins = pe.matmul(ps_q[:, i * D:(i + 1) * D], turned[half][:, i, :], k.w1_dst[:, :], start=True, stop=True)
                    ins.then_inc(q_done, 1)
                pe.wait_ge(msg_done, c + 1)
                for g, (j, n) in enumerate(vgroups):
                    q = NV * c + g
                    wait_past(pe, v_kept, q - 1)
                    for i in range(n):
                        ins = pe.matmul(ps_v[(NV * b + g) % 2][:, i * AGG:(i + 1) * AGG], same[:, j + i, :], msg[:, j + i, :], start=True, stop=True)
                    ins.then_inc(v_done, 1)

            edge_chunks(pe, chunk)



def nodes_out(nc, m, k, pairs, sums, out):
    x1 = [m.sb(f"no_x{i}", [P, NC, D]) for i in range(NB)]
    sum_a = [m.sb(f"no_a{i}", [P, NC, AGG]) for i in range(NB)]
    sum_b = [m.sb(f"no_b{i}", [P, NC, AGG]) for i in range(NB)]
    mixed = [m.sb(f"no_mixed{i}", [P, NC, D]) for i in range(NB)]
    turned = [m.sb(f"no_turned{i}", [P, NGROUP, P]) for i in range(2)]
    stats = [m.sb(f"no_stats{i}", [P, NC, 6]) for i in range(NB)]
    small = [m.sb(f"no_small{i}", [P, 12, NC]) for i in range(NB)]
    ps_t = [m.ps(f"no_ps_t{i}") for i in range(2)]
    ps_y = [m.ps(f"no_ps_y{i}") for i in range(2)]
    landed = m.sems("no_landed", NB)
    stored = m.sems("no_stored", NB)
    moments, varied, rooted, scaled, biased, norm_done = (m.sem("no_moments"), m.sem("no_varied"), m.sem("no_rooted"),
                                                          m.sem("no_scaled"), m.sem("no_biased"), m.sem("no_norm_done"))
    summed, step, mixed_done, turn_done, turn_kept, mul_done, res_done = (
        m.sem("no_summed"), m.sem("no_step"), m.sem("no_mixed_done"), m.sem("no_turn_done"), m.sem("no_turn_kept"),
        m.sem("no_mul_done"), m.sem("no_res_done"))
    STEPS = 3

    with nc.Block() as block:
        @block.sync
        def _(sp):
            def body(now, _1, _2, coming):
                if coming:
                    wait_apart(sp, k.sp_past, stored[coming.buf], 16 * coming.turn)
                    for to, table, width in ((x1, pairs, D), (sum_a, sums[0], AGG), (sum_b, sums[1], AGG)):
                        sp.dma_start(to[coming.buf][0:coming.parts, 0:coming.tiles, :],
                                     coming.rows(table, slice(0, width))).then_inc(landed[coming.buf], 16)
                if now:
                    wait_apart(sp, k.sp_past, res_done, now.c * NGROUPS + now.groups())
                    sp.dma_start(now.rows(out, slice(0, D)), x1[now.buf][0:now.parts, 0:now.tiles, :]).then_inc(stored[now.buf], 16)

            node_chunks(sp, body, lead=3)
            for h in range(NB):
                wait_apart(sp, k.sp_past, stored[h], 16 * uses(h))

        @block.gpsimd
        def _(pool):
            def body(_0, _1, soon):
                if soon:
                    p, n, a = soon.parts, soon.tiles, sum_a[soon.buf]
                    wait_apart(pool, k.pool_past, landed[soon.buf], 48 * (soon.turn + 1))
                    pool.tensor_tensor(a[0:p, 0:n, :], a[0:p, 0:n, :], sum_b[soon.buf][0:p, 0:n, :], op=ALU.add).then_inc(summed, 1)

            node_chunks(pool, body, lead=2)

        @block.vector
        def _(v):
            def stats_of(ch, g):
                q, b, j, n = ch.group(g)
                ins = norm_stats(v, lambda j: x1[ch.buf][0:ch.parts, j, :], stats[ch.buf], ch.parts, range(j, j + n))
                if g == ch.groups() - 1:
                    ins.then_inc(moments, 1)

            def mix(ch, g):
                p, s = ch.parts, small[ch.buf]
                q, b, j0, n = ch.group(g)
                for j in range(j0, j0 + n):
                    ins = v.scalar_tensor_tensor(out=mixed[ch.buf][0:p, j, :], in0=sum_a[ch.buf][0:p, j, 0:D],
                                                 scalar=s[0:p, 10, j:j + 1], in1=mixed[ch.buf][0:p, j, :], op0=ALU.mult,
                                                 op1=ALU.add)
                if g == ch.groups() - 1:
                    ins.then_inc(mixed_done, 1)

            def finish(ch, g):
                q, b, j, n = ch.group(g)
                r = x1[ch.buf][0:ch.parts, j:j + n, :]
                v.wait_ge(mul_done, q + 1)
                v.scalar_tensor_tensor(out=r, in0=ps_y[b][0:ch.parts, 0:n * D].rearrange("p (j f) -> p j f", j=n), scalar=0.0,
                                       in1=r, op0=ALU.max, op1=ALU.add).then_inc(res_done, 1)

            def scales(ch):
                p, n, s, a = ch.parts, ch.tiles, small[ch.buf], sum_a[ch.buf]
                base = ch.c * STEPS
                norm_moments(v, stats[ch.buf], s, moments, NORM_STEPS * ch.c, p, n)
                v.scalar_tensor_tensor(out=s[0:p, 4, 0:n], in0=s[0:p, 3, 0:n], scalar=0.25, in1=s[0:p, 2, 0:n],
                                       op0=ALU.mult, op1=ALU.add).then_inc(varied, 1)
                v.wait_ge(summed, ch.c + 1)
                v.tensor_scalar(s[0:p, 8, 0:n], a[0:p, 0:n, D], 1e-9, 2.0, op0=ALU.add, op1=ALU.mult)
                v.tensor_scalar(s[0:p, 11, 0:n], a[0:p, 0:n, D + 1], 1.0, -0.5, op0=ALU.min, op1=ALU.mult).then_inc(step, 1)
                v.wait_ge(step, base + 1)
                v.reciprocal(s[0:p, 10, 0:n], s[0:p, 8, 0:n])
                v.tensor_scalar(s[0:p, 9, 0:n], s[0:p, 11, 0:n], 1.0, None, op0=ALU.add).then_inc(step, 1)
                v.wait_ge(rooted, ch.c + 1)
                wait_past(v, norm_done, ch.c - (NB - 1))
                v.reciprocal(s[0:p, 3, 0:n], s[0:p, 5, 0:n]).then_inc(step, 1)
                v.wait_ge(step, base + 3)
                v.tensor_tensor(s[0:p, 6, 0:n], s[0:p, 3, 0:n], s[0:p, 9, 0:n], op=ALU.mult).then_inc(scaled, 1)
                v.wait_ge(scaled, ch.c + 1)
                v.scalar_tensor_tensor(out=s[0:p, 7, 0:n], in0=s[0:p, 0, 0:n], scalar=-0.5, in1=s[0:p, 6, 0:n],
                                       op0=ALU.mult, op1=ALU.mult).then_inc(biased, 1)

            def body(now, next_, soon, coming):
                if coming:
                    v.wait_ge(landed[coming.buf], 48 * (coming.turn + 1))
                if next_:
                    v.wait_ge(norm_done, next_.c + 1)
                for g in groups_of(now, next_, coming):
                    if coming and g < coming.groups():
                        stats_of(coming, g)
                    if now and g < now.groups():
                        finish(now, g)
                    if next_ and g < next_.groups():
                        mix(next_, g)
                if coming:
                    scales(coming)

            node_chunks(v, body, lead=3)

        @block.scalar
        def _(act):
            def turn(ch, g):
                p = ch.parts
                q, b, j, n = ch.group(g)
                act.wait_ge(turn_done, q + 1)
                wait_past(act, mul_done, q - 1)
                act.activation(turned[b][:, 0:n, 0:p], ps_t[b][:, 0:n * P].rearrange("p (j f) -> p j f", j=n)[:, :, 0:p],
                               ACT.Copy).then_inc(turn_kept, 1)

            def norm(ch, g):
                p, s = ch.parts, small[ch.buf]
                q, b, j0, n = ch.group(g)
                for j in range(j0, j0 + n):
                    ins = act.activation(mixed[ch.buf][0:p, j, :], x1[ch.buf][0:p, j, :], ACT.Relu,
                                         bias=s[0:p, 7, j:j + 1], scale=s[0:p, 6, j:j + 1])
                if g == ch.groups() - 1:
                    ins.then_inc(norm_done, 1)

            def body(now, _1, soon, coming):
                if soon:
                    act.wait_ge(biased, soon.c + 1)
                    wait_past(act, turn_done, (soon.c - (NB - 1)) * NGROUPS)
                for g in groups_of(now, soon):
                    if now and g < now.groups():
                        turn(now, g)
                    if soon and g < soon.groups():
                        norm(soon, g)
                if coming:
                    p, n, s = coming.parts, coming.tiles, small[coming.buf]
                    act.wait_ge(varied, coming.c + 1)
                    act.activation(s[0:p, 5, 0:n], s[0:p, 4, 0:n], ACT.Sqrt, bias=k.eps[0:p, :]).then_inc(rooted, 1)

            node_chunks(act, body, lead=3)

        @block.tensor
        def _(pe):
            def multiply(ch, g):
                p = ch.parts
                q, b, j, n = ch.group(g)
                pe.wait_ge(turn_kept, q + 1)
                wait_past(pe, res_done, q - 1)
                for i in range(n):
                    y = ps_y[b][0:p, i * D:(i + 1) * D]
                    pe.matmul(y, turned[b][:, i, 0:p], k.wl[:, :], start=True, stop=False)
                    ins = pe.matmul(y, k.ones[0:1, 0:p], k.bl[0:1, :], start=False, stop=True)
                ins.then_inc(mul_done, 1)

            def body(now):
                if not now:
                    return
                p = now.parts
                pe.wait_ge(mixed_done, now.c + 1)
                for g in range(now.groups()):
                    q, b, j, n = now.group(g)
                    wait_past(pe, turn_kept, q - 1)
                    for i in range(n):
                        ins = pe.transpose(ps_t[b][:, i * P:i * P + p], mixed[now.buf][0:p, j + i, :], k.ident[0:p, 0:p])
                    ins.then_inc(turn_done, 1)
                    if g:
                        multiply(now, g - 1)
                multiply(now, now.groups() - 1)

            node_chunks(pe, body, lead=0)


def program(nc, x, src, dst, coeffs, lin_weight, lin_bias, att_src, att_dst, w1, b1, w2, b2, wl, bl, out):
    def scratch(name, shape, dt=F32):
        return nc.dram_tensor(name, shape, dt, kind="Internal").ap()

    by_src = scratch("by_src", [N, XT])
    by_dst = scratch("by_dst", [N, XD])
    pairs = scratch("node_pairs", [N, PAIR])
    h_rev = scratch("h_rev", [P, T, D])
    sums = [scratch(f"sums{i}", [P * T, AGG]) for i in range(2)]
    by_low, by_key = (scratch(name, [P * T, 2], I32) for name in ("edges_by_low", "edges_by_dst"))

    with ExitStack() as outer:
        shared = Mem(nc, outer)
        k = Const(shared)
        e = Edges(shared)
        flag = shared.sb("unsorted", [1, 1], I32)
        joint = {"head": shared.sb("head_state", [P, D + 2 * HEADS]), "tail": shared.sb("tail_state", [P, D + 2 * HEADS]),
                 "head_len": shared.sb("head_len", [P, 1])}

        def run(part, *args):
            with ExitStack() as ctx:
                part(nc, Mem(nc, ctx), k, *args)

        run(constants, coeffs, lin_weight, lin_bias, att_src, att_dst, w1, b1, w2, b2, wl, bl)
        run(edges_in, e, src, dst, flag)
        run(edges_sorted, e, flag, by_low, by_key)
        run(edge_marks, e, joint)
        run(nodes_in, x, by_src, by_dst, pairs)
        run(attention, e, by_src, by_dst, pairs, h_rev, sums, joint)
        run(joints, e, by_dst, pairs, h_rev, joint)
        run(messages, e, pairs.rearrange("n (two f) -> (n two) f", two=2), h_rev, sums)
        run(nodes_out, pairs, sums, out)


_INS = ['x', 'src', 'dst', 'L0_gnn_coeffs_t', 'L0_gnn_lin_weight', 'L0_gnn_lin_bias', 'L0_gnn_att_src', 'L0_gnn_att_dst',
        'L1_gnn_W1', 'L1_gnn_b1', 'L1_gnn_W2', 'L1_gnn_b2', 'L1_gnn_Wl', 'L1_gnn_bl']


def kernel(**inputs):
    import numpy as _np
    import concourse.bacc as _bacc
    from concourse import mybir as _mybir
    from concourse.bass_utils import run_bass_kernel_spmd as _run

    nc = _bacc.Bacc("TRN2", target_bir_lowering=False, num_devices=1)
    arrays, args = {}, []
    for name in _INS:
        a = _np.ascontiguousarray(inputs[name])
        arrays[f"in_{name}_dram"] = a
        args.append(nc.dram_tensor(f"in_{name}_dram", a.shape, _mybir.dt.from_np(a.dtype), kind="ExternalInput").ap())
    out = nc.dram_tensor("out_0_dram", (N, D), _mybir.dt.float32, kind="ExternalOutput").ap()
    program(nc, *args, out)
    r = _run(nc, [arrays], core_ids=[0])
    return r.results[0]["out_0_dram"]
```

```python
import concourse.bass as bass
from concourse import mybir
from contextlib import ExitStack

F32 = mybir.dt.float32
I32 = mybir.dt.int32
ALU = mybir.AluOpType
ACT = mybir.ActivationFunctionType
AX = mybir.AxisListType

P = 128
N = 50000
E = 50000
D = 128
HEADS = 4
CH = D // HEADS
SLICES = 3
EPS = 1e-5
SLOPE = 0.2
BIG = 1e38

EC = 14
T = 2 * EC * -(-E // (P * 2 * EC))
ECHUNKS = T // EC
SLOTS = EC + 1
PAD_DST = P * T - 1
SKIP = 1 << 17
LAST_FULL = (P - 1) * T
REST = E - LAST_FULL

NC = 10
NB = 5
NB_OUT = 7
NCHUNKS = N // (P * NC)
TAIL = N - NCHUNKS * P * NC
NGROUP = 3
NGROUPS = -(-NC // NGROUP)
assert ECHUNKS % 2 == 0 and NGROUPS == 4
assert 0 < T - NCHUNKS * NC <= NGROUP
assert ((NCHUNKS - 2) // NB * NB + 2 + NB) * NC <= T + 2 * EC

XT = D + HEADS
XD = D + HEADS
PAIR = 2 * D
AGG = D + 2
RADIX = max(P, T)


def wait_past(eng, sem, value):
    if isinstance(value, int) and value <= 0:
        return
    eng.wait_ge(sem, value)


def wait_apart(eng, past, sem, value):
    wait_past(eng, sem, value)
    if not isinstance(value, int):
        eng.sem_inc(past, 1)


class Chunk:

    def __init__(self, c, buf, turn, parts=P, tiles=NC):
        self.c, self.buf, self.turn, self.parts, self.tiles = c, buf, turn, parts, tiles

    def rows(self, table, cols):
        if self.parts == P:
            part = table[bass.ds(self.c * (P * NC), P * NC), cols]
        else:
            part = table[NCHUNKS * P * NC:N, cols]
        return part.rearrange("(p j) f -> p j f", p=self.parts)

    def group(self, g):
        return self.c * NGROUPS + g, g % 2, g * NGROUP, min(NGROUP, self.tiles - g * NGROUP)

    def groups(self):
        return -(-self.tiles // NGROUP)


def uses(buf, buffers):
    return len(range(buf, NCHUNKS + 1, buffers))


def node_chunks(eng, body, lead, buffers):
    def at(c):
        if 0 <= c < NCHUNKS:
            return Chunk(c, c % buffers, c // buffers)
        return Chunk(c, c % buffers, c // buffers, parts=TAIL, tiles=1) if c == NCHUNKS else None

    turns = (NCHUNKS - lead) // buffers
    for c in range(-lead, buffers):
        body(*(at(c + i) for i in range(lead + 1)))
    with eng.Fori(1, turns) as k:
        for h in range(buffers):
            body(*(Chunk(buffers * k + (h + i), (h + i) % buffers, k + (h + i) // buffers) for i in range(lead + 1)))
    for c in range(buffers * turns, NCHUNKS + 1):
        body(*(at(c + i) for i in range(lead + 1)))


def edge_chunks(eng, body):
    body(0, 0, 0)
    body(1, 1, 0)
    with eng.Fori(1, ECHUNKS // 2) as k:
        body(2 * k, 0, k)
        body(2 * k + 1, 1, k)


class Mem:

    def __init__(self, nc, ctx):
        self.nc, self.ctx = nc, ctx

    def sb(self, name, shape, dt=F32):
        return self.ctx.enter_context(self.nc.sbuf_tensor(name, shape, dt))

    def ps(self, name, banks=1):
        return self.ctx.enter_context(self.nc.psum_tensor(name, [P, 512 * banks], F32))

    def sem(self, name):
        return self.ctx.enter_context(self.nc.semaphore(name))

    def sems(self, name, n):
        return [self.sem(f"{name}{i}") for i in range(n)]


class Const:

    def __init__(self, m):
        self.ident = m.sb("ident", [P, P])
        self.ones = m.sb("ones", [P, P])
        self.before = m.sb("before", [P, P])
        self.upto = m.sb("upto", [P, P])
        self.proj = m.sb("proj", [P, D + 2 * HEADS])
        self.proj_bias = m.sb("proj_bias", [P, D + 2 * HEADS])
        self.w1_src = m.sb("w1_src", [P, D])
        self.w1_dst = m.sb("w1_dst", [P, D])
        self.b1 = m.sb("b1", [P, D])
        self.w2 = m.sb("w2", [P, D])
        self.b2 = m.sb("b2", [P, 1])
        self.wl = m.sb("wl", [P, D])
        self.bl = m.sb("bl", [P, D])
        self.eps = m.sb("eps", [P, 1])
        self.pool_past = m.sem("pool_past")
        self.sp_past = m.sem("sp_past")
        self.trash = m.sb("trash", [P, 1])


class Edges:

    def __init__(self, m):
        self.src = m.sb("e_src", [P, T + 2 * EC], I32)
        self.dst = m.sb("e_dst", [P, T], I32)
        self.dst_pick = m.sb("e_dst_pick", [P, T + 2 * EC], I32)
        self.put = m.sb("e_put", [P, T], I32)
        self.dst_f = m.sb("e_dst_f", [P, T])
        self.reset = m.sb("e_reset", [P, T])
        self.last = m.sb("e_last", [P, T])
        self.head_end = m.sb("e_head_end", [P, T])
        self.go_on_rev = m.sb("e_go_on_rev", [P, T])
        self.key_rev = m.sb("e_key_rev", [P, T + 2 * EC])
        self.pick_rev = m.sb("e_pick_rev", [P, T + 2 * EC], I32)



def constants(nc, m, k, coeffs, lin_weight, lin_bias, att_src, att_dst, w1, b1, w2, b2, wl, bl):
    w_all = m.sb("w_all", [P, SLICES, D])
    col_all = m.sb("col_all", [P, 3, SLICES])
    mix = m.sb("mix", [P, SLICES])
    w_mix = m.sb("w_mix", [P, D])
    cols = m.sb("cols", [P, 3])
    eye_att = m.sb("eye_att", [P, D + 2 * HEADS])
    bias_wide = m.sb("bias_wide", [P, P])
    ps_w = m.ps("ps_w")
    ps_b = m.ps("ps_b")
    loaded, filled, drawn, mixed, spread, folded, kept = (
        m.sem("const_loaded"), m.sem("const_filled"), m.sem("const_drawn"), m.sem("const_mixed"),
        m.sem("const_spread"), m.sem("const_folded"), m.sem("const_kept"))

    with nc.Block() as block:
        @block.sync
        def _(sp):
            loads = [
                (w_all[:, :, :], lin_weight.rearrange("b o i -> o b i")),
                (col_all[:, 0, :], lin_bias.rearrange("b o -> o b")),
                (col_all[:, 1, :], att_src.rearrange("b q h c -> (q h c) b")),
                (col_all[:, 2, :], att_dst.rearrange("b q h c -> (q h c) b")),
                (mix[:, :], coeffs.unsqueeze(0).to_broadcast([P, SLICES])),
                (k.w1_src[:, :], w1[0:D, :]),
                (k.w1_dst[:, :], w1[D:2 * D, :]),
                (k.b1[:, :], b1.unsqueeze(0).to_broadcast([P, D])),
                (k.w2[:, :], w2.rearrange("d one -> one d").to_broadcast([P, D])),
                (k.b2[:, :], b2.unsqueeze(0).to_broadcast([P, 1])),
                (k.wl[:, :], wl[:, :]),
                (k.bl[:, :], bl.unsqueeze(0).to_broadcast([P, D])),
            ]
            with nc.allow_non_contiguous_dma(reason="small weights, once"):
                for to, of in loads:
                    sp.dma_start(to, of).then_inc(loaded, 16)
            wait_apart(sp, k.sp_past, loaded, 16 * len(loads))
            sp.sem_inc(kept, 1)

        @block.gpsimd
        def _(pool):
            wait_apart(pool, k.pool_past, filled, 1)
            nc.gpsimd.affine_select(out=k.ident[:, :], in_=k.ones[:, :], pattern=[[-1, P]], compare_op=ALU.is_equal,
                                    fill=0.0, base=0, channel_multiplier=1).then_inc(drawn, 1)
            nc.gpsimd.affine_select(out=k.before[:, :], in_=k.ones[:, :], pattern=[[1, P]], compare_op=ALU.is_gt,
                                    fill=0.0, base=0, channel_multiplier=-1).then_inc(drawn, 1)
            nc.gpsimd.affine_select(out=k.upto[:, :], in_=k.ones[:, :], pattern=[[-1, P]], compare_op=ALU.is_ge,
                                    fill=0.0, base=0, channel_multiplier=1).then_inc(drawn, 1)
            nc.gpsimd.iota(k.trash[:, :], pattern=[[0, 1]], base=N, channel_multiplier=1,
                           allow_small_or_imprecise_dtypes=True).then_inc(drawn, 1)
            wait_apart(pool, k.pool_past, drawn, 4)

        @block.vector
        def _(v):
            v.memset(k.ones[:, :], 1.0).then_inc(filled, 1)
            v.memset(k.eps[:, :], EPS)
            v.memset(eye_att[:, :], 0.0).then_inc(spread, 1)
            v.wait_ge(kept, 1)
            v.tensor_scalar(w_mix[:, :], w_all[:, 0, :], mix[:, 0:1], None, op0=ALU.mult).then_inc(mixed, 1)
            v.tensor_scalar(cols[:, :], col_all[:, :, 0], mix[:, 0:1], None, op0=ALU.mult).then_inc(mixed, 1)
            for b in range(1, SLICES):
                v.wait_ge(mixed, 2 * b)
                v.scalar_tensor_tensor(out=w_mix[:, :], in0=w_all[:, b, :], scalar=mix[:, b:b + 1], in1=w_mix[:, :],
                                       op0=ALU.mult, op1=ALU.add).then_inc(mixed, 1)
                v.scalar_tensor_tensor(out=cols[:, :], in0=col_all[:, :, b], scalar=mix[:, b:b + 1], in1=cols[:, :],
                                       op0=ALU.mult, op1=ALU.add).then_inc(mixed, 1)
            v.wait_ge(mixed, 2 * SLICES)
            v.wait_ge(spread, 1)
            v.wait_ge(drawn, 1)
            for h in range(HEADS):
                rows = slice(CH * h, CH * h + CH)
                v.tensor_copy(eye_att[rows, D + h:D + h + 1], cols[rows, 1:2])
                v.tensor_copy(eye_att[rows, D + HEADS + h:D + HEADS + h + 1], cols[rows, 2:3])
            v.tensor_copy(eye_att[:, 0:D], k.ident[:, :])
            v.tensor_scalar(bias_wide[:, :], k.ones[:, :], cols[:, 0:1], None, op0=ALU.mult).then_inc(spread, 1)
            v.wait_ge(folded, 2)
            v.tensor_copy(k.proj[:, :], ps_w[:, 0:D + 2 * HEADS])
            v.tensor_copy(k.proj_bias[:, :], ps_b[:, 0:D + 2 * HEADS]).then_inc(kept, 1)
            v.wait_ge(kept, 2)

        @block.tensor
        def _(pe):
            pe.wait_ge(spread, 2)
            pe.matmul(ps_w[:, 0:D + 2 * HEADS], w_mix[:, :], eye_att[:, :], start=True, stop=True).then_inc(folded, 1)
            pe.matmul(ps_b[:, 0:D + 2 * HEADS], bias_wide[:, :], eye_att[:, :], start=True, stop=True).then_inc(folded, 1)



def edges_in(nc, m, k, e, src, dst, flag):
    prev = m.sb("prev", [P, T], I32)
    prev_f = m.sb("prev_f", [P, T])
    falls = m.sb("falls", [P, T])
    fall = m.sb("fall", [P, 1])
    ps_f = m.ps("ps_fall")
    blank, loaded, step, counted = m.sem("edges_blank"), m.sem("edges_loaded"), m.sem("falls_step"), m.sem("falls_counted")

    with nc.Block() as block:
        @block.sync
        def _(sp):
            wait_apart(sp, k.sp_past, blank, 1)
            loads = [
                (e.src[0:P - 1, 0:T], src[0:LAST_FULL].rearrange("(p t) -> p t", t=T)),
                (e.src[P - 1:P, 0:REST], src[LAST_FULL:E].unsqueeze(0)),
                (e.dst[0:P - 1, :], dst[0:LAST_FULL].rearrange("(p t) -> p t", t=T)),
                (e.dst[P - 1:P, 0:REST], dst[LAST_FULL:E].unsqueeze(0)),
                (prev[0:1, 1:T], dst[0:T - 1].unsqueeze(0)),
                (prev[1:P - 1, :], dst[T - 1:LAST_FULL - 1].rearrange("(p t) -> p t", t=T)),
                (prev[P - 1:P, 0:REST + 1], dst[LAST_FULL - 1:E].unsqueeze(0)),
            ]
            for to, of in loads:
                sp.dma_start(to, of).then_inc(loaded, 16)
            wait_apart(sp, k.sp_past, loaded, 16 * len(loads))

        @block.vector
        def _(v):
            v.memset(e.src[:, :], 0)
            v.memset(e.dst[:, :], PAD_DST)
            v.memset(prev[:, :], 0).then_inc(blank, 1)
            v.wait_ge(loaded, 16 * 7)
            v.tensor_copy(e.dst_f[:, :], e.dst[:, :])
            v.tensor_copy(prev_f[:, :], prev[:, :]).then_inc(step, 1)
            v.wait_ge(step, 1)
            v.tensor_tensor(falls[:, :], prev_f[:, :], e.dst_f[:, :], op=ALU.is_gt).then_inc(step, 1)
            v.wait_ge(step, 2)
            v.tensor_reduce(fall[:, :], falls[:, :], AX.X, ALU.max).then_inc(step, 1)
            v.wait_ge(counted, 1)
            v.tensor_copy(flag[:, :], ps_f[0:1, 0:1]).then_inc(step, 1)
            v.wait_ge(step, 4)

        @block.tensor
        def _(pe):
            pe.wait_ge(step, 3)
            pe.matmul(ps_f[0:1, 0:1], fall[:, :], k.ones[:, 0:1], start=True, stop=True).then_inc(counted, 1)


def edges_sorted(nc, m, k, e, flag, by_low, by_dst):
    pairs = m.sb("pairs", [P, T, 2], I32)
    bucket_i = m.sb("bucket_i", [P, T], I32)
    bucket = m.sb("bucket", [P, T])
    number_i = m.sb("number_i", [P, RADIX], I32)
    number = m.sb("number", [P, RADIX])
    count = m.sb("count", [P, RADIX])
    ends = m.sb("ends", [P, RADIX])
    place = m.sb("place", [P, RADIX])
    scrap = m.sb("scrap", [P, RADIX])
    at = m.sb("at", [P, 1])
    at_i = m.sb("at_i", [P, 1], I32)
    pair = m.sb("pair", [P, 2], I32)
    ps_c = m.ps("ps_count")
    ps_e = m.ps("ps_before")
    numbered, ready, counted, summed, sent, back = (m.sem("sort_numbered"), m.sem("sort_ready"), m.sem("sort_counted"),
                                                    m.sem("sort_summed"), m.sem("sort_sent"), m.sem("sort_back"))
    step, taken, placed = m.sem("sort_step"), m.sem("sort_taken"), m.sem("sort_placed")
    passes = [(0, P, by_low), (1, T, by_dst)]

    with nc.Block() as block:
        @block.gpsimd
        def _(pool):
            nc.gpsimd.iota(number_i[:, :], pattern=[[1, RADIX]], base=0, channel_multiplier=0).then_inc(numbered, 1)
            with pool.If(pool.value_load(flag[0:1, 0:1], min_val=0, max_val=P) != 0):
                for n, radix, table in passes:
                    with pool.Fori(0, T) as t:
                        wait_apart(pool, k.pool_past, ready, n * T + t + 1)
                        pool.indirect_dma_start(table[:, :], bass.IndirectOffsetOnAxis(at_i[:, 0:1], 0), pair[:, :],
                                                None).then_inc(sent, 16)
                        wait_apart(pool, k.pool_past, sent, 16 * (n * T + t + 1))
                        pool.sem_inc(taken, 1)

        @block.sync
        def _(sp):
            with sp.If(sp.value_load(flag[0:1, 0:1], min_val=0, max_val=P) != 0):
                for n, radix, table in passes:
                    wait_apart(sp, k.sp_past, taken, (n + 1) * T)
                    sp.dma_start(pairs[:, :, :], table.rearrange("(p t) two -> p t two", t=T)).then_inc(back, 16)
                    wait_apart(sp, k.sp_past, back, 16 * (n + 1))

        @block.tensor
        def _(pe):
            with pe.If(pe.value_load(flag[0:1, 0:1], min_val=0, max_val=P) != 0):
                for n, radix, table in passes:
                    pe.wait_ge(counted, n + 1)
                    pe.matmul(ps_c[:, 0:radix], k.ones[:, :], count[:, 0:radix], start=True, stop=True)
                    pe.matmul(ps_e[:, 0:radix], k.before[:, :], count[:, 0:radix], start=True,
                              stop=True).then_inc(summed, 1)

        @block.vector
        def _(v):
            with v.If(v.value_load(flag[0:1, 0:1], min_val=0, max_val=P) != 0):
                done = [0]

                def link(ins):
                    done[0] += 1
                    ins.then_inc(step, 1)
                    v.wait_ge(step, done[0])

                v.tensor_copy(pairs[:, :, 0], e.src[:, 0:T])
                link(v.tensor_copy(pairs[:, :, 1], e.dst[:, :]))
                v.wait_ge(numbered, 1)
                link(v.tensor_copy(number[:, :], number_i[:, :]))
                for n, radix, table in passes:
                    if n:
                        v.wait_ge(back, 16 * n)
                        link(v.tensor_single_scalar(bucket_i[:, :], pairs[:, :, 1], 7, op=ALU.logical_shift_right))
                    else:
                        link(v.tensor_single_scalar(bucket_i[:, :], pairs[:, :, 1], P - 1, op=ALU.bitwise_and))
                    link(v.tensor_copy(bucket[:, :], bucket_i[:, :]))
                    link(v.memset(count[:, 0:radix], 0.0))
                    base = done[0]
                    with v.Fori(0, T) as t:
                        v.scalar_tensor_tensor(out=count[:, 0:radix], in0=number[:, 0:radix],
                                               scalar=bucket[:, bass.ds(t, 1)], in1=count[:, 0:radix],
                                               op0=ALU.is_equal, op1=ALU.add).then_inc(step, 1)
                        v.wait_ge(step, t + (base + 1))
                    done[0] += T
                    v.sem_inc(counted, 1)
                    v.wait_ge(summed, n + 1)
                    link(v.tensor_copy(scrap[:, 0:radix], ps_c[:, 0:radix]))
                    link(v.tensor_tensor_scan(ends[:, 0:radix], k_ones(k, radix), scrap[:, 0:radix], 0.0,
                                              op0=ALU.mult, op1=ALU.add))
                    link(v.tensor_tensor(ends[:, 0:radix], ends[:, 0:radix], scrap[:, 0:radix], op=ALU.subtract))
                    link(v.tensor_tensor(place[:, 0:radix], ends[:, 0:radix], ps_e[:, 0:radix], op=ALU.add))
                    base = done[0]
                    with v.Fori(0, T) as t:
                        v.scalar_tensor_tensor(out=scrap[:, 0:radix], in0=number[:, 0:radix],
                                               scalar=bucket[:, bass.ds(t, 1)], in1=place[:, 0:radix],
                                               op0=ALU.is_equal, op1=ALU.mult, accum_out=at[:, :]).then_inc(step, 1)
                        v.scalar_tensor_tensor(out=place[:, 0:radix], in0=number[:, 0:radix],
                                               scalar=bucket[:, bass.ds(t, 1)], in1=place[:, 0:radix],
                                               op0=ALU.is_equal, op1=ALU.add).then_inc(step, 1)
                        v.wait_ge(step, 2 * t + (base + 2))
                        v.tensor_copy(at_i[:, :], at[:, :])
                        v.tensor_copy(pair[:, :], pairs[:, bass.ds(t, 1), :].rearrange("p one two -> p (one two)")).then_inc(ready, 1)
                        v.wait_ge(taken, n * T + t + 1)
                    done[0] += 2 * T
                v.wait_ge(back, 16 * len(passes))
                v.tensor_copy(e.src[:, 0:T], pairs[:, :, 0])
                v.tensor_copy(e.dst[:, :], pairs[:, :, 1]).then_inc(placed, 1)
                v.wait_ge(placed, 1)


def k_ones(k, n):
    return k.ones[:, 0:1].to_broadcast([P, n])


def edge_marks(nc, m, k, e, joint):
    src_f = m.sb("src_f", [P, T])
    first = m.sb("first", [P, T])
    in_head = m.sb("in_head", [P, T])
    in_tail = m.sb("in_tail", [P, T])
    work = m.sb("work", [P, T])
    step = m.sem("marks_step")

    with nc.Block() as block:
        @block.vector
        def _(v):
            done = [0]

            def link(ins):
                done[0] += 1
                ins.then_inc(step, 1)
                v.wait_ge(step, done[0])

            v.memset(first[:, 0:1], 1.0)
            v.memset(e.last[:, T - 1:T], 1.0)
            v.memset(e.dst_pick[:, T:], 0)
            v.memset(e.pick_rev[:, T:], 0)
            v.memset(e.key_rev[:, T:], 0.0)
            v.tensor_copy(src_f[:, :], e.src[:, 0:T])
            link(v.tensor_copy(e.dst_f[:, :], e.dst[:, :]))
            v.tensor_tensor(first[:, 1:T], e.dst_f[:, 1:T], e.dst_f[:, 0:T - 1], op=ALU.not_equal)
            v.tensor_tensor(e.last[:, 0:T - 1], e.dst_f[:, 1:T], e.dst_f[:, 0:T - 1], op=ALU.not_equal)
            v.tensor_scalar(in_head[:, :], e.dst_f[:, :], e.dst_f[:, 0:1], None, op0=ALU.is_equal)
            v.tensor_scalar(in_tail[:, :], e.dst_f[:, :], e.dst_f[:, T - 1:T], None, op0=ALU.is_equal)
            link(v.tensor_scalar(e.dst_pick[:, 0:T], e.dst_f[:, :], float(N - 1), None, op0=ALU.min))
            v.tensor_scalar(e.reset[:, :], first[:, :], -BIG, None, op0=ALU.mult)
            v.tensor_scalar(e.go_on_rev[:, ::-1], e.last[:, :], -1.0, 1.0, op0=ALU.mult, op1=ALU.add)
            v.tensor_reduce(joint["head_len"][:, :], in_head[:, :], AX.X, ALU.add)
            v.tensor_scalar(work[:, :], in_tail[:, :], -1.0, 1.0, op0=ALU.mult, op1=ALU.add).then_inc(step, 1)
            done[0] += 1
            v.wait_ge(step, done[0])
            link(v.tensor_tensor(work[:, :], work[:, :], e.last[:, :], op=ALU.mult))
            link(v.tensor_tensor(e.head_end[:, :], work[:, :], in_head[:, :], op=ALU.mult))
            link(v.tensor_tensor(work[:, :], work[:, :], e.head_end[:, :], op=ALU.subtract))
            link(v.scalar_tensor_tensor(out=work[:, :], in0=e.dst_f[:, :], scalar=-float(SKIP), in1=work[:, :],
                                        op0=ALU.add, op1=ALU.mult))
            v.tensor_scalar(e.put[:, :], work[:, :], float(SKIP), None, op0=ALU.add)
            link(v.tensor_scalar(first[:, :], e.dst_f[:, :], float(N), float(N + P - 1), op0=ALU.is_ge, op1=ALU.mult))
            v.tensor_tensor(e.key_rev[:, 0:T][:, ::-1], first[:, :], src_f[:, :], op=ALU.max)
            link(v.tensor_scalar(e.pick_rev[:, 0:T][:, ::-1], src_f[:, :], 2.0, 1.0, op0=ALU.mult, op1=ALU.add))



def norm_stats(v, x, stats, parts, tiles):
    for j in tiles:
        ins = v.bn_stats(stats[0:parts, j, :], x(j))
    return ins


def norm_moments(v, stats, small, step, at, parts, tiles):
    st = stats[0:parts, 0:tiles, :]
    v.wait_ge(step, at + 1)
    v.tensor_tensor(small[0:parts, 0, 0:tiles], st[:, :, 1], st[:, :, 4], op=ALU.add)
    v.tensor_tensor(small[0:parts, 1, 0:tiles], st[:, :, 1], st[:, :, 4], op=ALU.subtract)
    v.tensor_tensor(small[0:parts, 2, 0:tiles], st[:, :, 2], st[:, :, 5], op=ALU.add).then_inc(step, 1)
    v.wait_ge(step, at + 2)
    v.tensor_tensor(small[0:parts, 3, 0:tiles], small[0:parts, 1, 0:tiles], small[0:parts, 1, 0:tiles], op=ALU.mult)
    v.tensor_scalar(small[0:parts, 2, 0:tiles], small[0:parts, 2, 0:tiles], 1.0 / D, None, op0=ALU.mult).then_inc(step, 1)
    v.wait_ge(step, at + 3)


NORM_STEPS = 3



def nodes_in(nc, m, k, e, x, by_src, by_dst, pairs):
    src_rows = [m.sb(f"src_rows{i}", [P, NC, XT]) for i in range(NB)]
    pair_rows = [m.sb(f"pair_rows{i}", [P, NC, PAIR]) for i in range(NB)]
    dst_rows = [m.sb(f"dst_rows{i}", [P, NC, XD]) for i in range(NB)]
    centred = [m.sb(f"centred{i}", [P, NC, D]) for i in range(NB)]
    dst_at = [m.sb(f"in_dst_at{i}", [P, NC], I32) for i in range(NB)]
    turned = [m.sb(f"turned{i}", [P, NGROUP, P]) for i in range(2)]
    e_turned = [m.sb(f"e_turned{i}", [P, NGROUP, P]) for i in range(2)]
    e_scores = m.sb("e_scores", [P, NC, HEADS])
    stats = [m.sb(f"stats{i}", [P, 2 * NC, 6]) for i in range(NB)]
    small = [m.sb(f"small{i}", [P, 9, 2 * NC]) for i in range(NB)]
    ps_t = [m.ps(f"ps_t{i}") for i in range(2)]
    ps_a = [m.ps(f"ps_a{i}") for i in range(2)]
    ps_b = [m.ps(f"ps_b{i}") for i in range(2)]
    ps_e = m.ps("ps_e")
    ps_s = m.ps("ps_s")
    x_in = m.sems("in_x_landed", NB)
    e_in = m.sems("in_edges_landed", NB)
    stored = m.sems("in_stored", NB)
    indexed, moments, varied, rooted, scaled, biased = (m.sem("in_indexed"), m.sem("in_moments"), m.sem("in_varied"),
                                                        m.sem("in_rooted"), m.sem("in_scaled"), m.sem("in_biased"))
    norm_done, turn_done, turn_kept, mul_done, mul_kept = (
        m.sem("in_norm_done"), m.sem("in_turn_done"), m.sem("in_turn_kept"), m.sem("in_mul_done"), m.sem("in_mul_kept"))
    e_turn_done, e_turn_kept, e_mul_done, e_read, e_kept = (
        m.sem("in_e_turn_done"), m.sem("in_e_turn_kept"), m.sem("in_e_mul_done"), m.sem("in_e_read"), m.sem("in_e_kept"))

    def columns(ch):
        return NC if ch.parts == P else T - NCHUNKS * NC

    def edge_group(ch, g):
        return g * NGROUP, min(NGROUP, columns(ch) - g * NGROUP)

    def sections(ch):
        if ch.parts == P:
            return [(P, slice(0, 2 * NC))]
        return [(ch.parts, slice(0, ch.tiles)), (P, slice(NC, NC + columns(ch)))]

    with nc.Block() as block:
        @block.sync
        def _(sp):
            def body(now, _1, _2, _3, coming):
                if coming:
                    wait_apart(sp, k.sp_past, stored[coming.buf], 48 * coming.turn)
                    sp.dma_start(pair_rows[coming.buf][0:coming.parts, 0:coming.tiles, 0:D],
                                 coming.rows(x, slice(0, D))).then_inc(x_in[coming.buf], 16)
                if now:
                    part = (slice(0, now.parts), slice(0, now.tiles))
                    wait_apart(sp, k.sp_past, mul_kept, now.c * NGROUPS + now.groups())
                    for table, rows, width in ((by_src, src_rows, XT), (pairs, pair_rows, PAIR)):
                        sp.dma_start(now.rows(table, slice(0, width)), rows[now.buf][part]).then_inc(stored[now.buf], 16)
                    wait_apart(sp, k.sp_past, e_kept, now.c + 1)
                    sp.dma_start(by_dst[:, bass.ds(now.c * NC, columns(now)), :],
                                 dst_rows[now.buf][:, 0:columns(now), :]).then_inc(stored[now.buf], 16)

            node_chunks(sp, body, lead=4, buffers=NB)
            for h in range(NB):
                wait_apart(sp, k.sp_past, stored[h], 48 * uses(h, NB))

        @block.gpsimd
        def _(pool):
            def body(_0, _1, _2, _3, coming):
                if coming:
                    wait_apart(pool, k.pool_past, indexed, coming.c + 1)
                    wait_apart(pool, k.pool_past, stored[coming.buf], 48 * coming.turn)
                    for j in range(columns(coming)):
                        pool.indirect_dma_start(dst_rows[coming.buf][:, j, 0:D], None, x[:, :],
                                                bass.IndirectOffsetOnAxis(dst_at[coming.buf][:, j:j + 1], 0)
                                                ).then_inc(e_in[coming.buf], 16)

            node_chunks(pool, body, lead=4, buffers=NB)

        @block.vector
        def _(v):
            def indices(c, buf):
                v.tensor_copy(dst_at[buf][:, :], e.dst_pick[:, bass.ds(c * NC, NC)]).then_inc(indexed, 1)

            def statistics(ch):
                b, cols, s = ch.buf, columns(ch), small[ch.buf]
                v.wait_ge(x_in[b], 16 * (ch.turn + 1))
                norm_stats(v, lambda j: pair_rows[b][0:ch.parts, j, 0:D], stats[b], ch.parts, range(ch.tiles))
                v.wait_ge(e_in[b], 16 * NC * ch.turn + 16 * cols)
                for j in range(cols):
                    ins = v.bn_stats(stats[b][:, NC + j, :], dst_rows[b][:, j, 0:D])
                ins.then_inc(moments, 1)
                if not (isinstance(ch.c, int) and ch.c + NB > NCHUNKS):
                    indices(ch.c + NB, b)
                wait_past(v, norm_done, (ch.c - (NB - 1)) * NGROUPS)
                v.wait_ge(moments, 3 * ch.c + 1)
                for p, t in sections(ch):
                    st = stats[b][0:p, t, :]
                    v.tensor_tensor(s[0:p, 0, t], st[:, :, 1], st[:, :, 4], op=ALU.add)
                    v.tensor_tensor(s[0:p, 1, t], st[:, :, 1], st[:, :, 4], op=ALU.subtract)
                    ins = v.tensor_tensor(s[0:p, 2, t], st[:, :, 2], st[:, :, 5], op=ALU.add)
                ins.then_inc(moments, 1)
                v.wait_ge(moments, 3 * ch.c + 2)
                for p, t in sections(ch):
                    v.tensor_tensor(s[0:p, 3, t], s[0:p, 1, t], s[0:p, 1, t], op=ALU.mult)
                    v.tensor_scalar(s[0:p, 8, t], s[0:p, 0, t], -0.5, None, op0=ALU.mult)
                    ins = v.tensor_scalar(s[0:p, 2, t], s[0:p, 2, t], 1.0 / D, None, op0=ALU.mult)
                ins.then_inc(moments, 1)
                v.wait_ge(moments, 3 * ch.c + 3)
                for p, t in sections(ch):
                    ins = v.scalar_tensor_tensor(out=s[0:p, 4, t], in0=s[0:p, 3, t], scalar=0.25, in1=s[0:p, 2, t],
                                                 op0=ALU.mult, op1=ALU.add)
                ins.then_inc(varied, 1)

            def scales(ch):
                s = small[ch.buf]
                v.wait_ge(rooted, ch.c + 1)
                for p, t in sections(ch):
                    ins = v.reciprocal(s[0:p, 6, t], s[0:p, 5, t])
                ins.then_inc(scaled, 1)
                v.wait_ge(scaled, ch.c + 1)
                for p, t in sections(ch):
                    ins = v.tensor_tensor(s[0:p, 7, t], s[0:p, 8, t], s[0:p, 6, t], op=ALU.mult)
                ins.then_inc(biased, 1)

            def keep(ch, g):
                p = ch.parts
                q, b, j, n = ch.group(g)
                v.wait_ge(mul_done, q + 1)
                v.tensor_tensor(src_rows[ch.buf][0:p, j:j + n, :], ps_a[b][0:p, 0:n * XT].rearrange("p (j f) -> p j f", j=n),
                                k.proj_bias[0:p, 0:XT].unsqueeze(1).to_broadcast([p, n, XT]), op=ALU.add)
                v.tensor_tensor(pair_rows[ch.buf][0:p, j:j + n, D:PAIR],
                                ps_b[b][0:p, 0:n * D].rearrange("p (j f) -> p j f", j=n),
                                k.b1[0:p, :].unsqueeze(1).to_broadcast([p, n, D]), op=ALU.add).then_inc(mul_kept, 1)

            def keep_scores(ch):
                cols = columns(ch)
                v.wait_ge(e_mul_done, ch.c * NGROUPS + ch.groups())
                wait_past(v, e_kept, ch.c)
                v.tensor_tensor(e_scores[:, 0:cols, :], ps_s[:, 0:cols * HEADS].rearrange("p (j f) -> p j f", j=cols),
                                small[ch.buf][:, 6, NC:NC + cols].unsqueeze(2).to_broadcast([P, cols, HEADS]),
                                op=ALU.mult).then_inc(e_read, 1)
                v.wait_ge(e_read, ch.c + 1)
                v.tensor_tensor(dst_rows[ch.buf][:, 0:cols, D:XD], e_scores[:, 0:cols, :],
                                k.proj_bias[:, XT:XT + HEADS].unsqueeze(1).to_broadcast([P, cols, HEADS]),
                                op=ALU.add).then_inc(e_kept, 1)

            def body(now, _1, soon):
                if soon:
                    statistics(soon)
                for g in range(NGROUPS):
                    if now and g < now.groups():
                        keep(now, g)
                    if soon and g == 1:
                        scales(soon)
                if now:
                    keep_scores(now)

            for b in range(NB):
                indices(b, b)
            node_chunks(v, body, lead=2, buffers=NB)

        @block.scalar
        def _(act):
            def turn(ch, g):
                p = ch.parts
                q, b, j, n = ch.group(g)
                act.wait_ge(turn_done, q + 1)
                wait_past(act, mul_done, q - 1)
                act.activation(turned[b][:, 0:n, 0:p], ps_t[b][:, 0:n * D].rearrange("p (j f) -> p j f", j=n)[:, :, 0:p],
                               ACT.Copy).then_inc(turn_kept, 1)
                j, n = edge_group(ch, g)
                act.wait_ge(e_turn_done, q + 1)
                wait_past(act, e_mul_done, q - 1)
                act.activation(e_turned[b][:, 0:n, :], ps_e[:, 0:n * D].rearrange("p (j f) -> p j f", j=n),
                               ACT.Copy).then_inc(e_turn_kept, 1)

            def norm(ch, g):
                p, s = ch.parts, small[ch.buf]
                q, b, j0, n = ch.group(g)
                for j in range(j0, j0 + n):
                    act.activation(src_rows[ch.buf][0:p, j, 0:D], pair_rows[ch.buf][0:p, j, 0:D], ACT.Relu,
                                   bias=s[0:p, 7, j:j + 1], scale=s[0:p, 6, j:j + 1])
                j0, n = edge_group(ch, g)
                for j in range(j0, j0 + n):
                    ins = act.activation(centred[ch.buf][:, j, :], dst_rows[ch.buf][:, j, 0:D], ACT.Relu,
                                         bias=s[:, 8, NC + j:NC + j + 1])
                ins.then_inc(norm_done, 1)

            def body(now, next_, soon):
                if next_:
                    act.wait_ge(biased, next_.c + 1)
                    wait_past(act, e_turn_done, (next_.c - (NB - 1)) * NGROUPS)
                for g in range(NGROUPS):
                    if now and g < now.groups():
                        turn(now, g)
                    if next_ and g < next_.groups():
                        norm(next_, g)
                    if soon and g == 1:
                        act.wait_ge(varied, soon.c + 1)
                        for p, t in sections(soon):
                            ins = act.activation(small[soon.buf][0:p, 5, t], small[soon.buf][0:p, 4, t], ACT.Sqrt,
                                                 bias=k.eps[0:p, :])
                        ins.then_inc(rooted, 1)

            node_chunks(act, body, lead=2, buffers=NB)

        @block.tensor
        def _(pe):
            def turn_over(ch, g):
                p = ch.parts
                q, b, j, n = ch.group(g)
                pe.wait_ge(norm_done, q + 1)
                wait_past(pe, turn_kept, q - 1)
                for i in range(n):
                    ins = pe.transpose(ps_t[b][:, i * D:i * D + p], src_rows[ch.buf][0:p, j + i, 0:D], k.ident[0:p, 0:p])
                ins.then_inc(turn_done, 1)
                wait_past(pe, e_turn_kept, q)
                j, n = edge_group(ch, g)
                for i in range(n):
                    ins = pe.transpose(ps_e[:, i * D:(i + 1) * D], centred[ch.buf][:, j + i, :], k.ident[:, :])
                ins.then_inc(e_turn_done, 1)

            def multiply(ch, g):
                p = ch.parts
                q, b, j, n = ch.group(g)
                pe.wait_ge(turn_kept, q + 1)
                wait_past(pe, mul_kept, q - 1)
                for i in range(n):
                    pe.matmul(ps_a[b][0:p, i * XT:(i + 1) * XT], turned[b][:, i, 0:p], k.proj[:, 0:XT], start=True, stop=True)
                    ins = pe.matmul(ps_b[b][0:p, i * D:(i + 1) * D], turned[b][:, i, 0:p], k.w1_src[:, :], start=True, stop=True)
                ins.then_inc(mul_done, 1)
                pe.wait_ge(e_turn_kept, q + 1)
                if g == 0:
                    wait_past(pe, e_read, ch.c)
                j, n = edge_group(ch, g)
                for i in range(n):
                    ins = pe.matmul(ps_s[:, (j + i) * HEADS:(j + i + 1) * HEADS], e_turned[b][:, i, :],
                                    k.proj[:, XT:XT + HEADS], start=True, stop=True)
                ins.then_inc(e_mul_done, 1)

            def body(now, next_):
                if not now:
                    turn_over(next_, 0)
                    return
                for g in range(now.groups()):
                    if g + 1 < now.groups():
                        turn_over(now, g + 1)
                    elif next_:
                        turn_over(next_, 0)
                    multiply(now, g)

            node_chunks(pe, body, lead=1, buffers=NB)



def attention(nc, m, k, e, by_src, by_dst, pairs, h_rev, sums, joint):
    HALF = EC // 2
    src_rows = [m.sb(f"at_src{i}", [P, EC, XT]) for i in range(2)]
    dst_rows = [m.sb(f"at_dst{i}", [P, EC, XD]) for i in range(2)]
    out_rows = [m.sb(f"at_out{i}", [P, EC, PAIR]) for i in range(2)]
    h_rows = [m.sb(f"at_h{i}", [P, EC, D]) for i in range(2)]
    src_at = [m.sb(f"src_at{i}", [P, EC], I32) for i in range(2)]
    put_at = [m.sb(f"put_at{i}", [P, EC], I32) for i in range(2)]
    score = m.sb("score", [P, HEADS, EC])
    score_in = m.sb("score_in", [P, HEADS, SLOTS])
    reset_in = m.sb("reset_in", [P, HEADS, SLOTS])
    peak = m.sb("peak", [P, HEADS, SLOTS])
    gap = m.sb("gap", [P, 2, HEADS, EC])
    fade = m.sb("fade", [P, HEADS, SLOTS])
    weight = m.sb("weight", [P, HEADS, SLOTS])
    total = m.sb("total", [P, HEADS, SLOTS])
    over = m.sb("over", [P, HEADS, EC])
    fades = m.sb("fades", [P, D, SLOTS])
    part = m.sb("part", [P, D, SLOTS])
    acc = m.sb("acc", [P, D, SLOTS])
    mixed = m.sb("mixed_rows", [P, EC, D])
    caught = m.sb("caught", [P, D, EC])
    caught_sum = m.sb("caught_sum", [P, D])
    few = m.sb("few", [P, 2, HEADS, EC])
    few_sum = m.sb("few_sum", [P, 2, HEADS])
    stats = m.sb("at_stats", [P, EC, 6])
    small = m.sb("at_small", [P, 8, EC])
    turned = [m.sb(f"at_turned{i}", [P, HALF, P]) for i in range(2)]
    zeros = m.sb("zeros", [P, EC * AGG])
    ps_t = [m.ps(f"at_ps_t{i}", 2) for i in range(2)]
    ps_p = [m.ps(f"at_ps_p{i}", 2) for i in range(2)]
    picked = m.sems("at_picked", 2)
    streamed = m.sems("at_streamed", 2)
    put = m.sems("at_put", 2)
    h_out = m.sems("at_h_out", 2)
    zeroed, ready, set_up = m.sem("at_zeroed"), m.sem("at_indices"), m.sem("at_set_up")
    step, gaps, fade_done, weight_done, spread = (m.sem("at_step"), m.sem("at_gaps"), m.sem("at_fade"),
                                                  m.sem("at_weight"), m.sem("at_spread"))
    moments, varied, rooted, scaled = m.sem("at_moments"), m.sem("at_varied"), m.sem("at_rooted"), m.sem("at_scaled")
    norm_done, turn_done, turn_kept, mul_done, rows_done, scanned = (
        m.sem("at_norm_done"), m.sem("at_turn_done"), m.sem("at_turn_kept"), m.sem("at_mul_done"),
        m.sem("at_rows_done"), m.sem("at_scanned"))
    PICKS = 16 * EC
    PUTS = 16 * EC
    STEPS = 13

    with nc.Block() as block:
        @block.gpsimd
        def _(pool):
            def pick(c, b, turn):
                wait_apart(pool, k.pool_past, ready, c + 1)
                for j in range(EC):
                    pool.indirect_dma_start(src_rows[b][:, j, :], None, by_src[:, :],
                                            bass.IndirectOffsetOnAxis(src_at[b][:, j:j + 1], 0)).then_inc(picked[b], 16)

            def put_rows(c, b):
                for j in range(EC):
                    if j % HALF == 0:
                        wait_apart(pool, k.pool_past, rows_done, 2 * c + j // HALF + 1)
                    pool.indirect_dma_start(pairs[:, :], bass.IndirectOffsetOnAxis(put_at[b][:, j:j + 1], 0),
                                            out_rows[b][:, j, :], None, bounds_check=N - 1,
                                            oob_is_err=False).then_inc(put[b], 16)

            pick(0, 0, 0)
            with pool.Fori(0, ECHUNKS // 2 - 1) as t:
                pick(2 * t + 1, 1, t)
                put_rows(2 * t, 0)
                pick(2 * t + 2, 0, t + 1)
                put_rows(2 * t + 1, 1)
            pick(ECHUNKS - 1, 1, ECHUNKS // 2 - 1)
            put_rows(ECHUNKS - 2, 0)
            put_rows(ECHUNKS - 1, 1)
            for b in range(2):
                wait_apart(pool, k.pool_past, put[b], PUTS * (ECHUNKS // 2))

        @block.sync
        def _(sp):
            wait_apart(sp, k.sp_past, set_up, 1)

            def chunk(c, b, turn):
                wait_apart(sp, k.sp_past, ready, c + 1)
                sp.dma_start(dst_rows[b][:, :, :], by_dst[:, bass.ds(c * EC, EC), :]).then_inc(streamed[b], 16)
                if not (isinstance(c, int) and c == 0):
                    store_h(c - 1, 1 - b)
                wait_apart(sp, k.sp_past, picked[b], PICKS * (turn + 1))
                for table in sums:
                    sp.dma_start(table[bass.ds(c * (P * EC), P * EC), :].rearrange("(p j) f -> p (j f)", p=P),
                                 zeros[:, :]).then_inc(zeroed, 16)

            def store_h(c, b):
                wait_apart(sp, k.sp_past, norm_done, 2 * (c + 1))
                sp.dma_start(h_rev[:, bass.ds((ECHUNKS - 1 - c) * EC, EC), :], h_rows[b][:, :, :]).then_inc(h_out[b], 16)

            edge_chunks(sp, chunk)
            store_h(ECHUNKS - 1, 1)
            wait_apart(sp, k.sp_past, zeroed, 16 * 2 * ECHUNKS)
            for b in range(2):
                wait_apart(sp, k.sp_past, h_out[b], 16 * (ECHUNKS // 2))

        @block.vector
        def _(v):
            def indices(c, b):
                v.tensor_copy(src_at[b][:, :], e.src[:, bass.ds(c * EC, EC)]).then_inc(ready, 1)

            for b in range(2):
                indices(b, b)
            v.memset(reset_in[:, :, 0:1], -BIG)
            v.memset(fade[:, :, :], 0.0)
            v.memset(peak[:, :, :], 0.0)
            v.memset(total[:, :, :], 0.0)
            v.memset(acc[:, :, :], 0.0)
            v.memset(joint["head"][:, :], 0.0)
            v.memset(zeros[:, :], 0.0).then_inc(set_up, 1)
            v.wait_ge(set_up, 1)

            def chunk(c, b, turn):
                cols = bass.ds(c * EC, EC)
                base = c * STEPS
                xs, xd, out, s = src_rows[b], dst_rows[b], out_rows[b], small

                def at(n):
                    v.wait_ge(step, base + n)

                if not (isinstance(c, int) and c == 0):
                    v.wait_ge(scanned, 3 * c)
                v.tensor_copy(score_in[:, :, 0:1], peak[:, :, EC:SLOTS])
                v.tensor_copy(weight[:, :, 0:1], total[:, :, EC:SLOTS])
                v.tensor_copy(part[:, :, 0:1], acc[:, :, EC:SLOTS])
                v.tensor_copy(reset_in[:, :, 1:SLOTS], e.reset[:, cols].unsqueeze(1).to_broadcast([P, HEADS, EC])).then_inc(step, 1)
                v.wait_ge(picked[b], PICKS * (turn + 1))
                v.wait_ge(streamed[b], 16 * (turn + 1))
                v.tensor_tensor(score[:, :, :], xs[:, :, D:XT].rearrange("p j h -> p h j"),
                                xd[:, :, D:XD].rearrange("p j h -> p h j"), op=ALU.add).then_inc(step, 1)
                at(2)
                v.scalar_tensor_tensor(out=score_in[:, :, 1:SLOTS], in0=score[:, :, :], scalar=SLOPE, in1=score[:, :, :],
                                       op0=ALU.mult, op1=ALU.max).then_inc(step, 1)
                at(3)
                v.tensor_tensor_scan(peak[:, :, :].rearrange("p h j -> p (h j)"), reset_in[:, :, :].rearrange("p h j -> p (h j)"),
                                     score_in[:, :, :].rearrange("p h j -> p (h j)"), 0.0, op0=ALU.add,
                                     op1=ALU.max).then_inc(scanned, 1)
                v.wait_ge(scanned, 3 * c + 1)
                v.tensor_tensor(score[:, :, :], peak[:, :, 0:EC], reset_in[:, :, 1:SLOTS], op=ALU.add).then_inc(step, 1)
                v.tensor_tensor(gap[:, 1, :, :], score_in[:, :, 1:SLOTS], peak[:, :, 1:SLOTS], op=ALU.subtract)
                at(4)
                v.tensor_tensor(gap[:, 0, :, :], score[:, :, :], peak[:, :, 1:SLOTS], op=ALU.subtract).then_inc(gaps, 1)
                v.wait_ge(weight_done, c + 1)
                v.tensor_tensor_scan(total[:, :, :].rearrange("p h j -> p (h j)"), fade[:, :, :].rearrange("p h j -> p (h j)"),
                                     weight[:, :, :].rearrange("p h j -> p (h j)"), 0.0, op0=ALU.mult,
                                     op1=ALU.add).then_inc(scanned, 1)
                v.tensor_tensor(part[:, :, 1:SLOTS].rearrange("p (h f) j -> p h f j", h=HEADS),
                                xs[:, :, 0:D].rearrange("p j (h f) -> p h f j", h=HEADS),
                                weight[:, :, 1:SLOTS].unsqueeze(2).to_broadcast([P, HEADS, CH, EC]),
                                op=ALU.mult).then_inc(step, 1)
                v.wait_ge(scanned, 3 * c + 2)
                v.tensor_scalar(over[:, :, :], total[:, :, 1:SLOTS], 1e-16, None, op0=ALU.add).then_inc(step, 1)
                at(6)
                v.reciprocal(score[:, :, :], over[:, :, :])
                v.wait_ge(spread, c + 1)
                v.tensor_tensor_scan(acc[:, :, :].rearrange("p f j -> p (f j)"), fades[:, :, :].rearrange("p f j -> p (f j)"),
                                     part[:, :, :].rearrange("p f j -> p (f j)"), 0.0, op0=ALU.mult,
                                     op1=ALU.add).then_inc(scanned, 1)
                v.wait_ge(scanned, 3 * c + 3)
                v.tensor_tensor(mixed[:, :, :].rearrange("p j (h f) -> p h f j", h=HEADS),
                                acc[:, :, 1:SLOTS].rearrange("p (h f) j -> p h f j", h=HEADS),
                                score[:, :, :].unsqueeze(2).to_broadcast([P, HEADS, CH, EC]),
                                op=ALU.mult).then_inc(step, 1)
                at(7)
                if not (isinstance(turn, int) and turn == 0):
                    v.wait_ge(put[b], PUTS * turn)
                v.tensor_tensor(out[:, :, 0:D], mixed[:, :, :], xd[:, :, 0:D], op=ALU.add).then_inc(step, 1)
                indices(c + 2, b)
                v.tensor_copy(put_at[b][:, :], e.put[:, cols])
                at(8)
                norm_stats(v, lambda j: out[:, j, 0:D], stats, P, range(EC)).then_inc(moments, 1)
                norm_moments(v, stats, s, moments, NORM_STEPS * c, P, EC)
                v.scalar_tensor_tensor(out=s[:, 4, :], in0=s[:, 3, :], scalar=0.25, in1=s[:, 2, :],
                                       op0=ALU.mult, op1=ALU.add).then_inc(varied, 1)
                v.wait_ge(rooted, c + 1)
                wait_past(v, norm_done, 2 * c)
                v.reciprocal(s[:, 3, :], s[:, 5, :]).then_inc(step, 1)
                at(9)
                v.tensor_tensor(s[:, 6, :], s[:, 3, :], e.last[:, cols], op=ALU.mult).then_inc(step, 1)
                at(10)
                v.scalar_tensor_tensor(out=s[:, 7, :], in0=s[:, 0, :], scalar=-0.5, in1=s[:, 6, :],
                                       op0=ALU.mult, op1=ALU.mult).then_inc(scaled, 1)
                mark = e.head_end[:, cols]
                v.tensor_tensor(caught[:, :, :], acc[:, :, 1:SLOTS], mark.unsqueeze(1).to_broadcast([P, D, EC]), op=ALU.mult)
                v.tensor_tensor(few[:, 0, :, :], peak[:, :, 1:SLOTS], mark.unsqueeze(1).to_broadcast([P, HEADS, EC]), op=ALU.mult)
                v.tensor_tensor(few[:, 1, :, :], total[:, :, 1:SLOTS], mark.unsqueeze(1).to_broadcast([P, HEADS, EC]),
                                op=ALU.mult).then_inc(step, 1)
                at(11)
                v.tensor_reduce(caught_sum[:, :], caught[:, :, :], AX.X, ALU.add)
                v.tensor_reduce(few_sum[:, :, :], few[:, :, :, :], AX.X, ALU.add).then_inc(step, 1)
                at(12)
                head = joint["head"]
                v.tensor_tensor(head[:, 0:D], head[:, 0:D], caught_sum[:, :], op=ALU.add)
                v.tensor_tensor(head[:, D:D + 2 * HEADS], head[:, D:D + 2 * HEADS],
                                few_sum[:, :, :].rearrange("p two h -> p (two h)"), op=ALU.add).then_inc(step, 1)
                for half in range(2):
                    js = slice(half * HALF, half * HALF + HALF)
                    v.wait_ge(mul_done, 2 * c + half + 1)
                    v.tensor_tensor(out[:, js, D:PAIR], ps_p[half][:, 0:HALF * D].rearrange("p (j f) -> p j f", j=HALF),
                                    k.b1[:, :].unsqueeze(1).to_broadcast([P, HALF, D]), op=ALU.add).then_inc(rows_done, 1)

            edge_chunks(v, chunk)
            v.tensor_copy(joint["tail"][:, 0:D], acc[:, :, EC])
            v.tensor_copy(joint["tail"][:, D:D + HEADS], peak[:, :, EC])
            v.tensor_copy(joint["tail"][:, D + HEADS:D + 2 * HEADS], total[:, :, EC]).then_inc(set_up, 1)
            v.wait_ge(set_up, 2)

        @block.scalar
        def _(act):
            def chunk(c, b, turn):
                act.wait_ge(gaps, c + 1)
                act.activation(fade[:, :, 1:SLOTS], gap[:, 0, :, :], ACT.Exp).then_inc(fade_done, 1)
                act.activation(weight[:, :, 1:SLOTS], gap[:, 1, :, :], ACT.Exp).then_inc(weight_done, 1)
                act.wait_ge(fade_done, c + 1)
                act.activation(fades[:, :, :].rearrange("p (h f) j -> p h f j", h=HEADS),
                               fade[:, :, :].unsqueeze(2).to_broadcast([P, HEADS, CH, SLOTS]), ACT.Copy).then_inc(spread, 1)
                act.wait_ge(varied, c + 1)
                act.activation(small[:, 5, :], small[:, 4, :], ACT.Sqrt, bias=k.eps[:, :]).then_inc(rooted, 1)
                act.wait_ge(scaled, c + 1)
                if not (isinstance(turn, int) and turn == 0):
                    act.wait_ge(h_out[b], 16 * turn)
                wait_past(act, turn_done, 2 * c - 2)
                for half in range(2):
                    for j in range(half * HALF, (half + 1) * HALF):
                        ins = act.activation(h_rows[b][:, EC - 1 - j, :], out_rows[b][:, j, 0:D], ACT.Relu,
                                             bias=small[:, 7, j:j + 1], scale=small[:, 6, j:j + 1])
                    ins.then_inc(norm_done, 1)
                for half in range(2):
                    act.wait_ge(turn_done, 2 * c + half + 1)
                    wait_past(act, mul_done, 2 * c + half - 1)
                    act.activation(turned[half][:, :, :], ps_t[half][:, 0:HALF * P].rearrange("p (j f) -> p j f", j=HALF),
                                   ACT.Copy).then_inc(turn_kept, 1)

            edge_chunks(act, chunk)

        @block.tensor
        def _(pe):
            def chunk(c, b, turn):
                for half in range(2):
                    pe.wait_ge(norm_done, 2 * c + half + 1)
                    wait_past(pe, turn_kept, 2 * c + half - 1)
                    for i in range(HALF):
                        ins = pe.transpose(ps_t[half][:, i * P:(i + 1) * P], h_rows[b][:, EC - 1 - (half * HALF + i), :], k.ident[:, :])
                    ins.then_inc(turn_done, 1)
                for half in range(2):
                    pe.wait_ge(turn_kept, 2 * c + half + 1)
                    wait_past(pe, rows_done, 2 * c + half - 1)
                    for i in range(HALF):
                        ins = pe.matmul(ps_p[half][:, i * D:(i + 1) * D], turned[half][:, i, :], k.w1_src[:, :], start=True, stop=True)
                    ins.then_inc(mul_done, 1)

            edge_chunks(pe, chunk)



def joints(nc, m, k, e, x, pairs, h_rev, joint):
    W = D + HEADS
    part = [joint["tail"], joint["head"]]
    key = m.sb("j_key", [P, 2])
    key_at = [m.sb(f"j_at{i}", [P, 1], I32) for i in range(2)]
    same = [m.sb(f"j_same{i}", [P, 2, P]) for i in range(2)]
    pen = m.sb("j_pen", [P, 2, P])
    top = [m.sb(f"j_top{i}", [P, HEADS]) for i in range(2)]
    cand = m.sb("j_cand", [P, HEADS, 2 * P])
    fac = m.sb("j_fac", [P, 2, HEADS])
    scaled = m.sb("j_scaled", [P, 2, W])
    xrow = [m.sb(f"j_x{i}", [P, D]) for i in range(2)]
    den = m.sb("j_den", [P, 2, HEADS])
    rows = [m.sb(f"j_rows{i}", [P, PAIR]) for i in range(2)]
    h = [m.sb(f"j_h{i}", [P, D]) for i in range(2)]
    hT = [m.sb(f"j_ht{i}", [P, P]) for i in range(2)]
    stats = m.sb("j_stats", [P, 2, 6])
    small = m.sb("j_small", [P, 8, 2])
    scrap = m.sb("j_scrap", [P, P])
    cnt = m.sb("j_cnt", [P, 2])
    flat = m.sb("j_flat", [P, 4])
    put = [m.sb(f"j_put{i}", [P, 1], I32) for i in range(2)]
    h_put = m.sb("j_h_put", [P, 1], I32)
    ps_k = m.ps("j_ps_k")
    ps_m = m.ps("j_ps_m", 2)
    ps_s = m.ps("j_ps_s", 1)
    ps_h = m.ps("j_ps_h")
    step, turned, peaks, weighed, gathered, out, stage, muls, acts = (
        m.sem("j_step"), m.sem("j_turned"), m.sem("j_peaks"), m.sem("j_weighed"), m.sem("j_gathered"), m.sem("j_out"),
        m.sem("j_stage"), m.sem("j_muls"), m.sem("j_acts"))
    tails_out = m.sem("j_tails_out")
    keyed, indexed, masked, summed, normed_, h_kept, ready = (
        m.sem("j_keyed"), m.sem("j_indexed"), m.sem("j_masked"), m.sem("j_summed"), m.sem("j_normed"), m.sem("j_h_kept"),
        m.sem("j_ready"))
    edge0 = m.sb("j_edge0", [P, 1])

    with nc.Block() as block:
        @block.vector
        def _(v):
            done = [0]

            def link(ins):
                done[0] += 1
                ins.then_inc(step, 1)
                v.wait_ge(step, done[0])

            first, last = e.dst_f[:, 0:1], e.dst_f[:, T - 1:T]
            v.tensor_copy(key[:, 0:1], last)
            v.tensor_copy(key_at[0][:, :], e.dst_pick[:, T - 1:T])
            v.tensor_copy(key_at[1][:, :], e.dst_pick[:, 0:1]).then_inc(indexed, 1)
            link(v.tensor_tensor(flat[:, 0:1], first, last, op=ALU.is_equal))
            v.tensor_tensor(flat[:, 1:2], flat[:, 0:1], k.trash[:, :], op=ALU.mult)
            link(v.tensor_scalar(flat[:, 2:3], flat[:, 0:1], -1.0, 1.0, op0=ALU.mult, op1=ALU.add))
            link(v.tensor_tensor(flat[:, 3:4], flat[:, 2:3], first, op=ALU.mult))
            link(v.scalar_tensor_tensor(out=key[:, 1:2], in0=flat[:, 1:2], scalar=-1.0, in1=flat[:, 3:4],
                                        op0=ALU.mult, op1=ALU.add))
            v.sem_inc(keyed, 1)
            v.wait_ge(turned, 1)
            keys = ps_k[:, 0:2 * P].rearrange("p (a f) -> p a f", a=2)
            for i in range(2):
                link(v.tensor_scalar(same[i][:, :, :], keys, key[:, i:i + 1], None, op0=ALU.is_equal))
            v.sem_inc(masked, 1)
            for i in range(2):
                link(v.tensor_scalar(pen[:, :, :], same[i][:, :, :], -1.0, BIG, op0=ALU.add, op1=ALU.mult))
                v.wait_ge(peaks, 1)
                link(v.tensor_tensor(cand[:, :, :], ps_m[:, :].rearrange("p (h a) -> p h a", h=HEADS),
                                     pen[:, :, :].rearrange("p a f -> p (a f)").unsqueeze(1).to_broadcast([P, HEADS, 2 * P]), op=ALU.add))
                link(v.tensor_reduce(top[i][:, :], cand[:, :, :], AX.X, ALU.max))
                link(v.tensor_tensor(fac[:, i, :], part[i][:, D:D + HEADS], top[i][:, :], op=ALU.subtract))
            v.sem_inc(stage, 1)
            v.wait_ge(weighed, 1)
            for i in range(2):
                v.tensor_tensor(scaled[:, i, 0:D].rearrange("p (h f) -> p h f", h=HEADS),
                                part[i][:, 0:D].rearrange("p (h f) -> p h f", h=HEADS),
                                fac[:, i, :].unsqueeze(2).to_broadcast([P, HEADS, CH]), op=ALU.mult)
                link(v.tensor_tensor(scaled[:, i, D:W], part[i][:, D + HEADS:D + 2 * HEADS], fac[:, i, :], op=ALU.mult))
            v.sem_inc(stage, 1)
            v.tensor_tensor(scrap[:, :], same[0][:, 0, :], k.upto[:, :], op=ALU.mult)
            link(v.tensor_reduce(cnt[:, 1:2], same[1][:, 0, :], AX.X, ALU.max))
            link(v.tensor_reduce(cnt[:, 0:1], scrap[:, :], AX.X, ALU.add))
            link(v.tensor_scalar(flat[:, 0:1], cnt[:, 0:1], 1.0, None, op0=ALU.is_equal))
            link(v.tensor_scalar(flat[:, 3:4], cnt[:, 1:2], -1.0, 1.0, op0=ALU.mult, op1=ALU.add))
            link(v.tensor_tensor(flat[:, 1:2], flat[:, 3:4], flat[:, 2:3], op=ALU.mult))
            for i in range(2):
                link(v.scalar_tensor_tensor(out=den[:, i, 0:1], in0=key[:, i:i + 1], scalar=-float(SKIP), in1=flat[:, i:i + 1],
                                            op0=ALU.add, op1=ALU.mult))
                link(v.tensor_scalar(put[i][:, :], den[:, i, 0:1], float(SKIP), None, op0=ALU.add))
            link(v.tensor_scalar(edge0[:, :], k.trash[:, :], float(1 - N), float(T), op0=ALU.add, op1=ALU.mult))
            link(v.tensor_tensor(edge0[:, :], edge0[:, :], joint["head_len"][:, :], op=ALU.subtract))
            link(v.scalar_tensor_tensor(out=edge0[:, :], in0=edge0[:, :], scalar=-float(SKIP), in1=flat[:, 2:3],
                                        op0=ALU.add, op1=ALU.mult))
            link(v.tensor_scalar(h_put[:, :], edge0[:, :], float(SKIP), None, op0=ALU.add))
            v.wait_ge(summed, 1)
            v.wait_ge(gathered, 32)
            for i in range(2):
                got = ps_s[:, i * W:(i + 1) * W]
                link(v.tensor_scalar(den[:, i, :], got[:, D:W], 1e-16, None, op0=ALU.add))
                link(v.reciprocal(fac[:, i, :], den[:, i, :]))
                link(v.tensor_tensor(rows[i][:, 0:D].rearrange("p (h f) -> p h f", h=HEADS),
                                     got[:, 0:D].rearrange("p (h f) -> p h f", h=HEADS),
                                     fac[:, i, :].unsqueeze(2).to_broadcast([P, HEADS, CH]), op=ALU.mult))
                link(v.tensor_tensor(rows[i][:, 0:D], rows[i][:, 0:D], xrow[i][:, 0:D], op=ALU.add))
            norm_stats(v, lambda j: rows[j][:, 0:D], stats, P, range(2)).then_inc(normed_, 1)
            norm_moments(v, stats, small, normed_, 0, P, 2)
            link(v.scalar_tensor_tensor(out=small[:, 4, :], in0=small[:, 3, :], scalar=0.25, in1=small[:, 2, :],
                                        op0=ALU.mult, op1=ALU.add))
            v.sem_inc(stage, 1)
            v.wait_ge(acts, 1)
            link(v.reciprocal(small[:, 6, :], small[:, 5, :]))
            link(v.scalar_tensor_tensor(out=small[:, 7, :], in0=small[:, 0, :], scalar=-0.5, in1=small[:, 6, :],
                                        op0=ALU.mult, op1=ALU.mult))
            v.sem_inc(stage, 1)
            v.wait_ge(muls, 2)
            for i in range(2):
                link(v.tensor_copy(hT[i][:, :], ps_h[:, i * P:(i + 1) * P]))
            v.sem_inc(stage, 1)
            v.wait_ge(muls, 4)
            for i in range(2):
                link(v.tensor_tensor(rows[i][:, D:PAIR], ps_h[:, 256 + i * D:256 + (i + 1) * D], k.b1[:, :], op=ALU.add))
            v.sem_inc(ready, 1)

        @block.scalar
        def _(act):
            act.wait_ge(stage, 1)
            act.activation(fac[:, :, :], fac[:, :, :], ACT.Exp).then_inc(weighed, 1)
            act.wait_ge(stage, 3)
            act.activation(small[:, 5, :], small[:, 4, :], ACT.Sqrt, bias=k.eps[:, :]).then_inc(acts, 1)
            act.wait_ge(stage, 4)
            for i in range(2):
                act.activation(h[i][:, :], rows[i][:, 0:D], ACT.Relu, bias=small[:, 7, i:i + 1],
                               scale=small[:, 6, i:i + 1]).then_inc(h_kept, 1)

        @block.tensor
        def _(pe):
            pe.wait_ge(keyed, 1)
            for i in range(2):
                ins = pe.transpose(ps_k[:, i * P:(i + 1) * P], key[:, i:i + 1].to_broadcast([P, P]), k.ident[:, :])
            ins.then_inc(turned, 1)
            for hd in range(HEADS):
                for i in range(2):
                    ins = pe.transpose(ps_m[:, (2 * hd + i) * P:(2 * hd + i + 1) * P],
                                       part[i][:, D + hd:D + hd + 1].to_broadcast([P, P]), k.ident[:, :])
            ins.then_inc(peaks, 1)
            pe.wait_ge(masked, 1)
            pe.wait_ge(stage, 2)
            for i in range(2):
                for j in range(2):
                    ins = pe.matmul(ps_s[:, i * W:(i + 1) * W], same[j][:, i, :], scaled[:, j, :], start=(j == 0), stop=(j == 1))
            ins.then_inc(summed, 1)
            for i in range(2):
                pe.wait_ge(h_kept, 2)
                pe.transpose(ps_h[:, i * P:(i + 1) * P], h[i][:, :], k.ident[:, :]).then_inc(muls, 1)
            pe.wait_ge(stage, 5)
            for i in range(2):
                pe.matmul(ps_h[:, 256 + i * D:256 + (i + 1) * D], hT[i][:, :], k.w1_src[:, :], start=True, stop=True).then_inc(muls, 1)

        @block.gpsimd
        def _(pool):
            wait_apart(pool, k.pool_past, indexed, 1)
            for i in range(2):
                pool.indirect_dma_start(xrow[i][:, :], None, x[:, :],
                                        bass.IndirectOffsetOnAxis(key_at[i][:, 0:1], 0)).then_inc(gathered, 16)
            wait_apart(pool, k.pool_past, ready, 1)
            for i in range(2):
                pool.indirect_dma_start(pairs[:, :], bass.IndirectOffsetOnAxis(put[i][:, 0:1], 0), rows[i][:, :], None,
                                        bounds_check=N - 1, oob_is_err=False).then_inc(out, 16)
            pool.indirect_dma_start(h_rev.rearrange("p t f -> (p t) f"), bass.IndirectOffsetOnAxis(h_put[:, 0:1], 0),
                                    h[1][:, :], None, bounds_check=P * T - 1, oob_is_err=False).then_inc(out, 16)
            wait_apart(pool, k.pool_past, out, 48)

        @block.sync
        def _(sp):
            wait_apart(sp, k.sp_past, h_kept, 2)
            sp.dma_start(h_rev[:, 0:1, :].rearrange("p one f -> p (one f)"), h[0][:, :]).then_inc(tails_out, 16)
            wait_apart(sp, k.sp_past, tails_out, 16)



def messages(nc, m, k, e, halves, h_rev, sums):
    TG = 4
    tgroups = [(j, min(TG, EC - j)) for j in range(0, EC, TG)]
    NT = len(tgroups)
    VG = 3
    vgroups = [(j, min(VG, EC - j)) for j in range(0, EC, VG)]
    NV = len(vgroups)
    h_in = [m.sb(f"me_h{i}", [P, EC, D]) for i in range(2)]
    prod = [m.sb(f"me_prod{i}", [P, EC, D]) for i in range(2)]
    out = [m.sb(f"me_out{i}", [P, EC, AGG]) for i in range(2)]
    at_in = [m.sb(f"me_at{i}", [P, EC], I32) for i in range(2)]
    at_out = [m.sb(f"me_to{i}", [P, EC], I32) for i in range(2)]
    keys = [m.sb(f"me_keys{i}", [P, EC]) for i in range(2)]
    ends = m.sb("me_ends", [P, D, SLOTS])
    keep = m.sb("me_keep", [P, D, SLOTS])
    xn = [m.sb(f"me_xn{i}", [P, D, SLOTS]) for i in range(2)]
    turned = [m.sb(f"me_turned{i}", [P, TG, P]) for i in range(2)]
    same = [m.sb(f"me_same{i}", [P, EC, P]) for i in range(2)]
    cnt = [m.sb(f"me_cnt{i}", [P, EC]) for i in range(2)]
    once = m.sb("me_once", [P, EC])
    less = m.sb("me_less", [P, EC])
    to_f = m.sb("me_to_f", [P, EC])
    logit = m.sb("me_logit", [P, EC])
    msg = m.sb("me_msg", [P, EC, AGG])
    mask = m.sb("me_mask", [P, EC])
    ps_t = [m.ps(f"me_ps_t{i}") for i in range(2)]
    ps_q = [m.ps(f"me_ps_q{i}") for i in range(2)]
    ps_r = [m.ps(f"me_ps_r{i}") for i in range(2)]
    ps_v = [m.ps(f"me_ps_v{i}") for i in range(2)]
    landed = m.sems("me_landed", 2)
    picked = m.sems("me_picked", 2)
    added = m.sems("me_added", 2)
    ready, set_up, ends_in, keep_in, scanned = (m.sem("me_indices"), m.sem("me_set_up"), m.sem("me_ends_in"),
                                                m.sem("me_keep_in"), m.sem("me_scanned"))
    turn_done, turn_kept, q_done, q_kept, r_done, r_kept = (m.sem("me_turn_done"), m.sem("me_turn_kept"), m.sem("me_q_done"),
                                                            m.sem("me_q_kept"), m.sem("me_r_done"), m.sem("me_r_kept"))
    step, dotted, masked, msg_done, to_done, v_done, v_kept, free = (
        m.sem("me_step"), m.sem("me_dotted"), m.sem("me_masked"), m.sem("me_msg_done"), m.sem("me_to_done"),
        m.sem("me_v_done"), m.sem("me_v_kept"), m.sem("me_out_free"))
    STEPS = 3 + NT
    PER = EC // 2

    assert NT % 2 == 0

    def chunks_but_last(eng, body):
        body(0, 0, 0)
        body(1, 1, 0)
        with eng.Fori(1, ECHUNKS // 2 - 1) as k:
            body(2 * k, 0, k)
            body(2 * k + 1, 1, k)
        body(ECHUNKS - 2, 0, ECHUNKS // 2 - 1)
        body(ECHUNKS - 1, 1, ECHUNKS // 2 - 1, after=False)

    with nc.Block() as block:
        @block.gpsimd
        def _(pool):
            def pick(b, j):
                pool.indirect_dma_start(prod[b][:, j, :], None, halves[:, :],
                                        bass.IndirectOffsetOnAxis(at_in[b][:, j:j + 1], 0)).then_inc(picked[b], 16)

            def add(c, b, j):
                wait_apart(pool, k.pool_past, added[j % 2], 16 * (PER * c + j // 2))
                pool.indirect_dma_start(sums[j % 2][:, :], bass.IndirectOffsetOnAxis(at_out[b][:, j:j + 1], 0),
                                        out[b][:, j, :], None, compute_op=ALU.add).then_inc(added[j % 2], 16)

            def chunk(c, b, ahead=True):
                if ahead:
                    wait_apart(pool, k.pool_past, ready, c + 3)
                    pick(b, 0)
                wait_apart(pool, k.pool_past, v_kept, NV * c + NV)
                wait_apart(pool, k.pool_past, to_done, c + 1)
                for j in range(EC):
                    add(c, b, j)
                    if ahead and j + 1 < EC:
                        pick(b, j + 1)

            for b in range(2):
                wait_apart(pool, k.pool_past, ready, b + 1)
                for j in range(EC):
                    pick(b, j)
            chunk(0, 0)
            chunk(1, 1)
            with pool.Fori(1, ECHUNKS // 2 - 1) as t:
                chunk(2 * t, 0)
                chunk(2 * t + 1, 1)
            chunk(ECHUNKS - 2, 0, ahead=False)
            chunk(ECHUNKS - 1, 1, ahead=False)
            for b in range(2):
                wait_apart(pool, k.pool_past, added[b], 16 * PER * ECHUNKS)

        @block.sync
        def _(sp):
            def chunk(c, b, turn):
                wait_apart(sp, k.sp_past, ends_in, c - 1)
                sp.dma_start(h_in[b][:, :, :], h_rev[:, bass.ds(c * EC, EC), :]).then_inc(landed[b], 16)

            edge_chunks(sp, chunk)

        @block.vector
        def _(v):
            def indices(c, b):
                v.tensor_copy(keys[b][:, :], e.key_rev[:, bass.ds(c * EC, EC)])
                v.tensor_copy(at_in[b][:, :], e.pick_rev[:, bass.ds(c * EC, EC)]).then_inc(ready, 1)

            def match(c, b):
                for g, (j0, n) in enumerate(tgroups):
                    v.wait_ge(r_done, NT * c + g + 1)
                    if g == 0:
                        wait_past(v, v_done, NV * (c - 1))
                    for i in range(n):
                        j = j0 + i
                        ins = v.scalar_tensor_tensor(out=same[b][:, j, :], in0=ps_r[g % 2][:, i * P:(i + 1) * P],
                                                     scalar=keys[b][:, j:j + 1], in1=k.upto[:, :],
                                                     op0=ALU.is_equal, op1=ALU.mult, accum_out=cnt[b][:, j:j + 1])
                    ins.then_inc(r_kept, 1)

            for b in range(2):
                indices(b, b)
            v.memset(keep[:, :, 0:1], 0.0)
            v.memset(xn[1][:, :, :], 0.0)
            v.memset(msg[:, :, D + 1:AGG], 1.0).then_inc(set_up, 1)
            v.wait_ge(set_up, 1)
            match(0, 0)

            def chunk(c, b, turn, after=True):
                base = c * STEPS

                def at(n):
                    v.wait_ge(step, base + n)

                wait_past(v, scanned, c)
                v.wait_ge(ends_in, c + 1)
                v.tensor_copy(ends[:, :, 0:1], xn[1 - b][:, :, EC:SLOTS]).then_inc(step, 1)
                v.wait_ge(keep_in, c + 1)
                at(1)
                v.tensor_tensor_scan(xn[b][:, :, :].rearrange("p f j -> p (f j)"), keep[:, :, :].rearrange("p f j -> p (f j)"),
                                     ends[:, :, :].rearrange("p f j -> p (f j)"), 0.0, op0=ALU.mult,
                                     op1=ALU.add).then_inc(scanned, 1)
                v.wait_ge(r_kept, NT * (c + 1))
                v.tensor_scalar(once[:, :], cnt[b][:, :], 1.0, None, op0=ALU.is_equal)
                v.tensor_scalar(less[:, :], keys[b][:, :], k.trash[:, :], None, op0=ALU.subtract).then_inc(step, 1)
                at(2)
                v.tensor_tensor(to_f[:, :], once[:, :], less[:, :], op=ALU.mult).then_inc(step, 1)
                if after:
                    match(c + 1, 1 - b)
                at(3)
                if not (isinstance(c, int) and c < 2):
                    for table in range(2):
                        v.wait_ge(added[table], 16 * PER * (c - 1))
                v.tensor_scalar(at_out[b][:, :], to_f[:, :], k.trash[:, :], None, op0=ALU.add).then_inc(to_done, 1)
                v.wait_ge(picked[b], 16 * EC * (turn + 1))
                z = prod[b]
                for g, (j, n) in enumerate(tgroups):
                    js = slice(j, j + n)
                    v.wait_ge(q_done, NT * c + g + 1)
                    v.tensor_tensor(z[:, js, :], z[:, js, :], ps_q[g % 2][:, 0:n * D].rearrange("p (j f) -> p j f", j=n),
                                    op=ALU.add).then_inc(q_kept, 1)
                    v.wait_ge(q_kept, NT * c + g + 1)
                    v.scalar_tensor_tensor(out=z[:, js, :], in0=z[:, js, :], scalar=0.0,
                                           in1=k.w2[:, :].unsqueeze(1).to_broadcast([P, n, D]), op0=ALU.max,
                                           op1=ALU.mult).then_inc(step, 1)
                at(3 + NT)
                v.tensor_reduce(logit[:, :], z[:, :, :], AX.X, ALU.add).then_inc(dotted, 1)
                v.wait_ge(dotted, c + 1)
                indices(c + 2, b)
                v.wait_ge(masked, c + 1)
                wait_past(v, v_done, NV * c)
                v.tensor_copy(msg[:, :, D:D + 1], mask[:, :].unsqueeze(2))
                v.tensor_tensor(msg[:, :, 0:D], xn[b][:, :, 1:SLOTS].rearrange("p f j -> p j f"),
                                mask[:, :].unsqueeze(2).to_broadcast([P, EC, D]), op=ALU.mult).then_inc(msg_done, 1)

            chunks_but_last(v, chunk)

        @block.scalar
        def _(act):
            def spread(c, b, turn):
                act.wait_ge(landed[b], 16 * (turn + 1))
                wait_past(act, scanned, c)
                act.activation(ends[:, :, 1:SLOTS].rearrange("p f j -> p j f"), h_in[b][:, :, :], ACT.Copy).then_inc(ends_in, 1)
                act.activation(keep[:, :, 1:SLOTS], e.go_on_rev[:, bass.ds(c * EC, EC)].unsqueeze(1).to_broadcast([P, D, EC]),
                               ACT.Copy).then_inc(keep_in, 1)

            spread(0, 0, 0)

            def chunk(c, b, turn, after=True):
                for g, (j, n) in enumerate(tgroups):
                    act.wait_ge(turn_done, NT * c + g + 1)
                    wait_past(act, q_done, NT * c + g - 1)
                    act.activation(turned[g % 2][:, 0:n, :], ps_t[g % 2][:, 0:n * P].rearrange("p (j f) -> p j f", j=n),
                                   ACT.Copy).then_inc(turn_kept, 1)
                if after:
                    spread(c + 1, 1 - b, turn + b)
                act.wait_ge(dotted, c + 1)
                wait_past(act, msg_done, c)
                act.activation(mask[:, :], logit[:, :], ACT.Sigmoid, bias=k.b2[:, :]).then_inc(masked, 1)
                if not (isinstance(c, int) and c < 2):
                    for table in range(2):
                        act.wait_ge(added[table], 16 * PER * (c - 1))
                for g, (j, n) in enumerate(vgroups):
                    q = NV * c + g
                    act.wait_ge(v_done, q + 1)
                    act.activation(out[b][:, j:j + n, :], ps_v[(NV * b + g) % 2][:, 0:n * AGG].rearrange("p (j f) -> p j f", j=n),
                                   ACT.Copy).then_inc(v_kept, 1)

            chunks_but_last(act, chunk)

        @block.tensor
        def _(pe):
            def rows_of_keys(c, b):
                pe.wait_ge(ready, c + 1)
                for g, (j, n) in enumerate(tgroups):
                    wait_past(pe, r_kept, NT * c + g - 1)
                    for i in range(n):
                        ins = pe.transpose(ps_r[g % 2][:, i * P:(i + 1) * P], keys[b][:, j + i:j + i + 1].to_broadcast([P, P]),
                                           k.ident[:, :])
                    ins.then_inc(r_done, 1)

            rows_of_keys(0, 0)

            def chunk(c, b, turn, after=True):
                def turn_over(g):
                    j, n = tgroups[g]
                    wait_past(pe, turn_kept, NT * c + g - 1)
                    for i in range(n):
                        ins = pe.transpose(ps_t[g % 2][:, i * P:(i + 1) * P], xn[b][:, :, 1 + j + i], k.ident[:, :])
                    ins.then_inc(turn_done, 1)

                pe.wait_ge(scanned, c + 1)
                turn_over(0)
                for g, (j, n) in enumerate(tgroups):
                    if g + 1 < NT:
                        turn_over(g + 1)
                    pe.wait_ge(turn_kept, NT * c + g + 1)
                    wait_past(pe, q_kept, NT * c + g - 1)
                    for i in range(n):
                        ins = pe.matmul(ps_q[g % 2][:, i * D:(i + 1) * D], turned[g % 2][:, i, :], k.w1_dst[:, :], start=True, stop=True)
                    ins.then_inc(q_done, 1)
                    if g == 1 and after:
                        rows_of_keys(c + 1, 1 - b)
                pe.wait_ge(msg_done, c + 1)
                for g, (j, n) in enumerate(vgroups):
                    q = NV * c + g
                    wait_past(pe, v_kept, q - 1)
                    for i in range(n):
                        ins = pe.matmul(ps_v[(NV * b + g) % 2][:, i * AGG:(i + 1) * AGG], same[b][:, j + i, :], msg[:, j + i, :], start=True, stop=True)
                    ins.then_inc(v_done, 1)

            chunks_but_last(pe, chunk)



def nodes_out(nc, m, k, pairs, sums, out):
    x1 = [m.sb(f"no_x{i}", [P, NC, D]) for i in range(NB_OUT)]
    sum_a = [m.sb(f"no_a{i}", [P, NC, AGG]) for i in range(NB_OUT)]
    sum_b = [m.sb(f"no_b{i}", [P, NC, AGG]) for i in range(NB_OUT)]
    mixed = [m.sb(f"no_mixed{i}", [P, NC, D]) for i in range(NB_OUT)]
    turned = [m.sb(f"no_turned{i}", [P, NGROUP, P]) for i in range(2)]
    stats = [m.sb(f"no_stats{i}", [P, NC, 6]) for i in range(NB_OUT)]
    small = [m.sb(f"no_small{i}", [P, 12, NC]) for i in range(NB_OUT)]
    ps_t = [m.ps(f"no_ps_t{i}") for i in range(2)]
    ps_y = [m.ps(f"no_ps_y{i}") for i in range(2)]
    landed = m.sems("no_landed", NB_OUT)
    stored = m.sems("no_stored", NB_OUT)
    moments, varied, rooted, scaled, biased, norm_done = (m.sem("no_moments"), m.sem("no_varied"), m.sem("no_rooted"),
                                                          m.sem("no_scaled"), m.sem("no_biased"), m.sem("no_norm_done"))
    summed, step, mixed_done, turn_done, turn_kept, mul_done, y_done, clipped, res_done = (
        m.sem("no_summed"), m.sem("no_step"), m.sem("no_mixed_done"), m.sem("no_turn_done"), m.sem("no_turn_kept"),
        m.sem("no_mul_done"), m.sem("no_y_done"), m.sem("no_clipped"), m.sem("no_res_done"))
    STEPS = 3

    with nc.Block() as block:
        @block.sync
        def _(sp):
            def body(now, *ahead):
                coming = ahead[-1]
                if coming:
                    wait_apart(sp, k.sp_past, stored[coming.buf], 16 * coming.turn)
                    for to, table, width in ((x1, pairs, D), (sum_a, sums[0], AGG), (sum_b, sums[1], AGG)):
                        sp.dma_start(to[coming.buf][0:coming.parts, 0:coming.tiles, :],
                                     coming.rows(table, slice(0, width))).then_inc(landed[coming.buf], 16)
                if now:
                    wait_apart(sp, k.sp_past, res_done, now.c + 1)
                    sp.dma_start(now.rows(out, slice(0, D)), x1[now.buf][0:now.parts, 0:now.tiles, :]).then_inc(stored[now.buf], 16)

            node_chunks(sp, body, lead=NB_OUT - 2, buffers=NB_OUT)
            for h in range(NB_OUT):
                wait_apart(sp, k.sp_past, stored[h], 16 * uses(h, NB_OUT))

        @block.gpsimd
        def _(pool):
            def body(now, _1, _2, _3, coming):
                if coming:
                    p, n, a = coming.parts, coming.tiles, sum_a[coming.buf]
                    wait_apart(pool, k.pool_past, landed[coming.buf], 48 * (coming.turn + 1))
                    pool.tensor_tensor(a[0:p, 0:n, :], a[0:p, 0:n, :], sum_b[coming.buf][0:p, 0:n, :], op=ALU.add).then_inc(summed, 1)
                if now:
                    p, n, r = now.parts, now.tiles, x1[now.buf]
                    wait_apart(pool, k.pool_past, clipped, now.c + 1)
                    pool.tensor_tensor(r[0:p, 0:n, :], sum_a[now.buf][0:p, 0:n, 0:D], r[0:p, 0:n, :],
                                       op=ALU.add).then_inc(res_done, 1)

            node_chunks(pool, body, lead=4, buffers=NB_OUT)

        @block.vector
        def _(v):
            def stats_of(ch, g):
                q, b, j, n = ch.group(g)
                ins = norm_stats(v, lambda j: x1[ch.buf][0:ch.parts, j, :], stats[ch.buf], ch.parts, range(j, j + n))
                if g == ch.groups() - 1:
                    ins.then_inc(moments, 1)

            def mix(ch, g):
                p, s = ch.parts, small[ch.buf]
                q, b, j0, n = ch.group(g)
                for j in range(j0, j0 + n):
                    ins = v.scalar_tensor_tensor(out=mixed[ch.buf][0:p, j, :], in0=sum_a[ch.buf][0:p, j, 0:D],
                                                 scalar=s[0:p, 10, j:j + 1], in1=mixed[ch.buf][0:p, j, :], op0=ALU.mult,
                                                 op1=ALU.add)
                ins.then_inc(mixed_done, 1)

            def finish(ch, g):
                q, b, j, n = ch.group(g)
                v.wait_ge(mul_done, q + 1)
                v.tensor_tensor(sum_a[ch.buf][0:ch.parts, j:j + n, 0:D],
                                ps_y[b][0:ch.parts, 0:n * D].rearrange("p (j f) -> p j f", j=n),
                                k.bl[0:ch.parts, :].unsqueeze(1).to_broadcast([ch.parts, n, D]), op=ALU.add).then_inc(y_done, 1)

            def scales(ch, part):
                p, n, s, a = ch.parts, ch.tiles, small[ch.buf], sum_a[ch.buf]
                st = stats[ch.buf][0:p, 0:n, :]
                if part == 0:
                    v.wait_ge(moments, 3 * ch.c + 1)
                    v.tensor_tensor(s[0:p, 0, 0:n], st[:, :, 1], st[:, :, 4], op=ALU.add)
                    v.tensor_tensor(s[0:p, 1, 0:n], st[:, :, 1], st[:, :, 4], op=ALU.subtract)
                    v.tensor_tensor(s[0:p, 2, 0:n], st[:, :, 2], st[:, :, 5], op=ALU.add).then_inc(moments, 1)
                elif part == 1:
                    v.wait_ge(moments, 3 * ch.c + 2)
                    v.tensor_tensor(s[0:p, 3, 0:n], s[0:p, 1, 0:n], s[0:p, 1, 0:n], op=ALU.mult)
                    v.tensor_scalar(s[0:p, 2, 0:n], s[0:p, 2, 0:n], 1.0 / D, None, op0=ALU.mult).then_inc(moments, 1)
                    v.wait_ge(summed, ch.c + 1)
                    v.tensor_scalar(s[0:p, 8, 0:n], a[0:p, 0:n, D], 1e-9, 2.0, op0=ALU.add, op1=ALU.mult)
                    v.tensor_scalar(s[0:p, 11, 0:n], a[0:p, 0:n, D + 1], 1.0, -0.5, op0=ALU.min, op1=ALU.mult).then_inc(step, 1)
                elif part == 2:
                    v.wait_ge(moments, 3 * ch.c + 3)
                    v.scalar_tensor_tensor(out=s[0:p, 4, 0:n], in0=s[0:p, 3, 0:n], scalar=0.25, in1=s[0:p, 2, 0:n],
                                           op0=ALU.mult, op1=ALU.add).then_inc(varied, 1)
                    v.wait_ge(step, STEPS * ch.c + 1)
                    v.reciprocal(s[0:p, 10, 0:n], s[0:p, 8, 0:n])
                    v.tensor_scalar(s[0:p, 9, 0:n], s[0:p, 11, 0:n], 1.0, None, op0=ALU.add).then_inc(step, 1)
                elif part == 3:
                    v.wait_ge(rooted, ch.c + 1)
                    wait_past(v, norm_done, ch.c - (NB_OUT - 1))
                    v.reciprocal(s[0:p, 3, 0:n], s[0:p, 5, 0:n]).then_inc(step, 1)
                else:
                    v.wait_ge(step, STEPS * ch.c + 3)
                    v.tensor_tensor(s[0:p, 6, 0:n], s[0:p, 3, 0:n], s[0:p, 9, 0:n], op=ALU.mult).then_inc(scaled, 1)
                    v.wait_ge(scaled, ch.c + 1)
                    v.scalar_tensor_tensor(out=s[0:p, 7, 0:n], in0=s[0:p, 0, 0:n], scalar=-0.5, in1=s[0:p, 6, 0:n],
                                           op0=ALU.mult, op1=ALU.mult).then_inc(biased, 1)

            def body(now, next_, soon, coming):
                if coming:
                    v.wait_ge(landed[coming.buf], 48 * (coming.turn + 1))
                    for g in range(coming.groups()):
                        stats_of(coming, g)
                if next_:
                    v.wait_ge(norm_done, next_.c + 1)
                for g in range(NGROUPS):
                    if next_ and g < next_.groups():
                        mix(next_, g)
                    if coming:
                        scales(coming, g)
                    if now and g < now.groups():
                        finish(now, g)
                if coming:
                    scales(coming, NGROUPS)

            node_chunks(v, body, lead=3, buffers=NB_OUT)

        @block.scalar
        def _(act):
            def turn(ch, g):
                p = ch.parts
                q, b, j, n = ch.group(g)
                act.wait_ge(turn_done, q + 1)
                wait_past(act, mul_done, q - 1)
                act.activation(turned[b][:, 0:n, 0:p], ps_t[b][:, 0:n * P].rearrange("p (j f) -> p j f", j=n)[:, :, 0:p],
                               ACT.Copy).then_inc(turn_kept, 1)

            def root(ch):
                p, n, s = ch.parts, ch.tiles, small[ch.buf]
                act.wait_ge(varied, ch.c + 1)
                act.activation(s[0:p, 5, 0:n], s[0:p, 4, 0:n], ACT.Sqrt, bias=k.eps[0:p, :]).then_inc(rooted, 1)

            def clip(ch):
                y = sum_a[ch.buf][0:ch.parts, 0:ch.tiles, 0:D]
                act.wait_ge(y_done, ch.c * NGROUPS + ch.groups())
                act.activation(y, y, ACT.Relu).then_inc(clipped, 1)

            def norm(ch, g):
                p, s = ch.parts, small[ch.buf]
                q, b, j0, n = ch.group(g)
                for j in range(j0, j0 + n):
                    ins = act.activation(mixed[ch.buf][0:p, j, :], x1[ch.buf][0:p, j, :], ACT.Relu,
                                         bias=s[0:p, 7, j:j + 1], scale=s[0:p, 6, j:j + 1])
                if g == ch.groups() - 1:
                    ins.then_inc(norm_done, 1)

            def body(prev, now, _2, soon, coming):
                if soon:
                    act.wait_ge(biased, soon.c + 1)
                    wait_past(act, turn_done, (soon.c - (NB_OUT - 1)) * NGROUPS)
                for g in range(NGROUPS):
                    if now and g < now.groups():
                        turn(now, g)
                    if soon and g < soon.groups():
                        norm(soon, g)
                    if prev and g == 1:
                        clip(prev)
                    if coming and g == 2:
                        root(coming)

            node_chunks(act, body, lead=4, buffers=NB_OUT)

        @block.tensor
        def _(pe):
            def multiply(ch, g):
                p = ch.parts
                q, b, j, n = ch.group(g)
                pe.wait_ge(turn_kept, q + 1)
                wait_past(pe, y_done, q - 1)
                for i in range(n):
                    y = ps_y[b][0:p, i * D:(i + 1) * D]
                    ins = pe.matmul(y, turned[b][:, i, 0:p], k.wl[:, :], start=True, stop=True)
                ins.then_inc(mul_done, 1)

            def turn_over(ch, g):
                p = ch.parts
                q, b, j, n = ch.group(g)
                pe.wait_ge(mixed_done, q + 1)
                wait_past(pe, turn_kept, q - 1)
                for i in range(n):
                    ins = pe.transpose(ps_t[b][:, i * P:i * P + p], mixed[ch.buf][0:p, j + i, :], k.ident[0:p, 0:p])
                ins.then_inc(turn_done, 1)

            def body(now, next_):
                if not now:
                    turn_over(next_, 0)
                    return
                for g in range(now.groups()):
                    if g + 1 < now.groups():
                        turn_over(now, g + 1)
                    elif next_:
                        turn_over(next_, 0)
                    multiply(now, g)

            node_chunks(pe, body, lead=1, buffers=NB_OUT)


def program(nc, x, src, dst, coeffs, lin_weight, lin_bias, att_src, att_dst, w1, b1, w2, b2, wl, bl, out):
    def scratch(name, shape, dt=F32):
        return nc.dram_tensor(name, shape, dt, kind="Internal").ap()

    by_src = scratch("by_src", [N, XT])
    by_dst = scratch("by_dst", [P, T, XD])
    pairs = scratch("node_pairs", [N, PAIR])
    h_rev = scratch("h_rev", [P, T, D])
    sums = [scratch(f"sums{i}", [P * T, AGG]) for i in range(2)]
    by_low, by_key = (scratch(name, [P * T, 2], I32) for name in ("edges_by_low", "edges_by_dst"))

    with ExitStack() as outer:
        shared = Mem(nc, outer)
        k = Const(shared)
        e = Edges(shared)
        flag = shared.sb("unsorted", [1, 1], I32)
        joint = {"head": shared.sb("head_state", [P, D + 2 * HEADS]), "tail": shared.sb("tail_state", [P, D + 2 * HEADS]),
                 "head_len": shared.sb("head_len", [P, 1])}

        def run(part, *args):
            with ExitStack() as ctx:
                part(nc, Mem(nc, ctx), k, *args)

        run(constants, coeffs, lin_weight, lin_bias, att_src, att_dst, w1, b1, w2, b2, wl, bl)
        run(edges_in, e, src, dst, flag)
        run(edges_sorted, e, flag, by_low, by_key)
        run(edge_marks, e, joint)
        run(nodes_in, e, x, by_src, by_dst, pairs)
        run(attention, e, by_src, by_dst, pairs, h_rev, sums, joint)
        run(joints, e, x, pairs, h_rev, joint)
        run(messages, e, pairs.rearrange("n (two f) -> (n two) f", two=2), h_rev, sums)
        run(nodes_out, pairs, sums, out)


_INS = ['x', 'src', 'dst', 'L0_gnn_coeffs_t', 'L0_gnn_lin_weight', 'L0_gnn_lin_bias', 'L0_gnn_att_src', 'L0_gnn_att_dst',
        'L1_gnn_W1', 'L1_gnn_b1', 'L1_gnn_W2', 'L1_gnn_b2', 'L1_gnn_Wl', 'L1_gnn_bl']


def kernel(**inputs):
    import numpy as _np
    import concourse.bacc as _bacc
    from concourse import mybir as _mybir
    from concourse.bass_utils import run_bass_kernel_spmd as _run

    nc = _bacc.Bacc("TRN2", target_bir_lowering=False, num_devices=1)
    arrays, args = {}, []
    for name in _INS:
        a = _np.ascontiguousarray(inputs[name])
        arrays[f"in_{name}_dram"] = a
        args.append(nc.dram_tensor(f"in_{name}_dram", a.shape, _mybir.dt.from_np(a.dtype), kind="ExternalInput").ap())
    out = nc.dram_tensor("out_0_dram", (N, D), _mybir.dt.float32, kind="ExternalOutput").ap()
    program(nc, *args, out)
    r = _run(nc, [arrays], core_ids=[0])
    return r.results[0]["out_0_dram"]
```
